# Optimizing a Trainium2 kernel written in Bass

```python
import numpy as np
import jax
import jax.numpy as jnp

def _softmax(x, axis=-1):
    return jax.nn.softmax(x, axis=axis)

def _gelu(x):
    return jax.nn.gelu(x, approximate=True)

def _silu(x):
    return jax.nn.silu(x)

def _sigmoid(x):
    return jax.nn.sigmoid(x)

def _layernorm(x, axis=-1, eps=1e-05):
    m = jnp.mean(x, axis=axis, keepdims=True)
    v = jnp.var(x, axis=axis, keepdims=True)
    return (x - m) / jnp.sqrt(v + eps)

def _scatter_add(tgt, idx, src, axis=0):
    return tgt.at[idx].add(src)

def _segment_sum(src, seg, n):
    return jax.ops.segment_sum(src, seg, n)
kernel_name = 'mk_cond_resid_d4_seqx_r8_958dd9'

def setup_inputs(seed: int=0):
    np.random.seed(seed)
    _w = jnp.asarray

    def _rec_inputs():
        import jax
        import jax.numpy as jnp
        _rk = jax.random.key(seed)
        x = -7.109e-05 + 0.9999 * jax.random.normal(jax.random.fold_in(_rk, 1), (128, 32, 256), jnp.float32)
        _lenS = 32 - jax.random.randint(jax.random.fold_in(_rk, 7), (128,), 0, max(1, 32 // 4) + 1, jnp.int32)
        _lenS2 = 32 - jax.random.randint(jax.random.fold_in(_rk, 8), (128,), 0, max(1, 32 // 4) + 1, jnp.int32)
        itok_B_1_198 = jax.random.randint(jax.random.fold_in(_rk, 11), (128,), 1, 199, jnp.int32)
        itok_Bx257_0_4111 = jax.random.randint(jax.random.fold_in(_rk, 12), (128, 257), 0, 514, jnp.int32)
        itok_B_37_3939 = jax.random.randint(jax.random.fold_in(_rk, 13), (128,), 37, 3940, jnp.int32)
        itok_B_0_6 = jax.random.randint(jax.random.fold_in(_rk, 14), (128,), 0, 7, jnp.int32)
        itok_B_0_7 = jax.random.randint(jax.random.fold_in(_rk, 15), (128,), 0, 8, jnp.int32)
        fside_8xS_0 = -0.00162727 + 0.0609077 * jax.random.normal(jax.random.fold_in(_rk, 16), (8, 32), jnp.float32)
        return (x, itok_B_1_198, itok_Bx257_0_4111, itok_B_37_3939, itok_B_0_6, itok_B_0_7, fside_8xS_0)
    x, itok_B_1_198, itok_Bx257_0_4111, itok_B_37_3939, itok_B_0_6, itok_B_0_7, fside_8xS_0 = _rec_inputs()

    def _L0_cond_setup():
        import jax, jax.numpy as jnp
        import numpy as np
        B, C, T = (128, 32, 256)
        S, D = (200, 32)
        key = jax.random.key(seed)
        k1, k2, k3 = jax.random.split(key, 3)
        x = jax.random.normal(k1, (B, C, T), dtype=jnp.float32)
        conditions = jax.random.randint(k2, (B,), 0, S, dtype=jnp.int64)
        weights = jax.random.normal(k3, (S, C, D), dtype=jnp.float32) / jnp.sqrt(jnp.float32(C))
        return {'x': x, 'conditions': conditions, 'weights': weights}
    _L0_cond_all = _L0_cond_setup()
    _L0_cond_in = {k: v for k, v in _L0_cond_all.items() if k in ('weights',)}
    del _L0_cond_all

    def _L1_cond_setup():
        import jax, jax.numpy as jnp
        import numpy as np
        H, G, HD = (8, 4, 32)
        GSZ = H // G
        BLOCK = 16
        WINDOW = 128
        SCALE = 256.0 ** (-0.5)
        EPS = 1e-06
        THETA = 10000.0
        B, T, D = (16, 4, 256)
        NBLK = 257

        def _rms(x, scale):
            var = jnp.mean(x * x, axis=-1, keepdims=True)
            return x * jax.lax.rsqrt(var + EPS) * (1.0 + scale)

        def _rope(x, pos):
            half = HD // 2
            inv = 1.0 / THETA ** (jnp.arange(half, dtype=jnp.float32) / half)
            ang = pos[:, :, None].astype(jnp.float32) * inv
            cos = jnp.cos(ang)[:, None, :, :]
            sin = jnp.sin(ang)[:, None, :, :]
            x1, x2 = (x[..., :half], x[..., half:])
            return jnp.concatenate([x1 * cos - x2 * sin, x2 * cos + x1 * sin], axis=-1)
        key = jax.random.key(seed)
        ks = jax.random.split(key, 10)
        inv_d = 1.0 / np.sqrt(D)
        return {'x': jax.random.normal(ks[0], (B, T, D), jnp.float32), 'Wq': jax.random.normal(ks[1], (H * HD, D), jnp.float32) * inv_d, 'Wk': jax.random.normal(ks[2], (G * HD, D), jnp.float32) * inv_d, 'Wv': jax.random.normal(ks[3], (G * HD, D), jnp.float32) * inv_d, 'Wo': jax.random.normal(ks[4], (D, H * HD), jnp.float32) * inv_d, 'q_norm_scale': jax.random.normal(ks[5], (HD,), jnp.float32) * 0.02, 'k_norm_scale': jax.random.normal(ks[6], (HD,), jnp.float32) * 0.02, 'k_blocks': jax.random.normal(ks[7], (B * NBLK, G, BLOCK, HD), jnp.float32), 'v_blocks': jax.random.normal(ks[8], (B * NBLK, G, BLOCK, HD), jnp.float32), 'block_tables': jnp.arange(B * NBLK, dtype=jnp.int32).reshape(B, NBLK), 'kv_lens': jax.random.randint(ks[9], (B,), 0, 512, dtype=jnp.int32)}
    _L1_cond_all = _L1_cond_setup()
    _L1_cond_in = {k: v for k, v in _L1_cond_all.items() if k in ('Wq', 'Wk', 'Wv', 'Wo', 'q_norm_scale', 'k_norm_scale', 'k_blocks', 'v_blocks')}
    del _L1_cond_all

    def _L2_cond_setup():
        import jax, jax.numpy as jnp
        import numpy as np
        B, T, D_IN, D_OUT = (16, 256, 256, 256)
        N_ADAPTERS, RANK = (8, 16)
        key = jax.random.key(seed)
        k_x, k_w, k_a, k_b, k_s, k_idx = jax.random.split(key, 6)
        x = jax.random.normal(k_x, (B, T, D_IN), dtype=jnp.float32)
        W = jax.random.normal(k_w, (D_OUT, D_IN), dtype=jnp.float32) * (1.0 / np.sqrt(D_IN))
        A = jax.random.normal(k_a, (N_ADAPTERS, RANK, D_IN), dtype=jnp.float32) * 0.02
        Bm = jax.random.normal(k_b, (N_ADAPTERS, D_OUT, RANK), dtype=jnp.float32) * 0.02
        scalings = jnp.ones((N_ADAPTERS,), dtype=jnp.float32)
        adapter_idx = jax.random.randint(k_idx, (B,), 0, N_ADAPTERS, dtype=jnp.int32)
        return {'x': x, 'W': W, 'A': A, 'Bm': Bm, 'scalings': scalings, 'adapter_idx': adapter_idx}
    _L2_cond_all = _L2_cond_setup()
    _L2_cond_in = {k: v for k, v in _L2_cond_all.items() if k in ('W', 'A', 'Bm', 'scalings')}
    del _L2_cond_all

    def _L3_cond_setup():
        import jax, jax.numpy as jnp
        import numpy as np
        B, C, T = (64, 32, 256)
        D, N = (32, 8)
        key = jax.random.key(seed)
        k_x, k_s, k_w, k_b = jax.random.split(key, 4)
        scale = 1.0 / np.sqrt(C)
        x = jax.random.normal(k_x, (B, C, T), dtype=jnp.float32)
        subjects = jax.random.randint(k_s, (B,), 0, N, dtype=jnp.int64)
        weights = jax.random.normal(k_w, (N, C, D), dtype=jnp.float32) * scale
        bias = jax.random.normal(k_b, (N, D), dtype=jnp.float32) * scale
        return {'x': x, 'subjects': subjects, 'weights': weights, 'bias': bias}
    _L3_cond_all = _L3_cond_setup()
    _L3_cond_in = {k: v for k, v in _L3_cond_all.items() if k in ('weights',)}
    del _L3_cond_all
    return {'x': x, 'itok_B_1_198': itok_B_1_198, 'itok_Bx257_0_4111': itok_Bx257_0_4111, 'itok_B_37_3939': itok_B_37_3939, 'itok_B_0_6': itok_B_0_6, 'itok_B_0_7': itok_B_0_7, 'fside_8xS_0': fside_8xS_0, 'L0_cond_weights': _L0_cond_in['weights'], 'L1_cond_Wq': _L1_cond_in['Wq'], 'L1_cond_Wk': _L1_cond_in['Wk'], 'L1_cond_Wv': _L1_cond_in['Wv'], 'L1_cond_Wo': _L1_cond_in['Wo'], 'L1_cond_q_norm_scale': _L1_cond_in['q_norm_scale'], 'L1_cond_k_norm_scale': _L1_cond_in['k_norm_scale'], 'L1_cond_k_blocks': _L1_cond_in['k_blocks'], 'L1_cond_v_blocks': _L1_cond_in['v_blocks'], 'L2_cond_W': _L2_cond_in['W'], 'L2_cond_A': _L2_cond_in['A'], 'L2_cond_Bm': _L2_cond_in['Bm'], 'L2_cond_scalings': _L2_cond_in['scalings'], 'L3_cond_weights': _L3_cond_in['weights']}

def reference(x, itok_B_1_198, itok_Bx257_0_4111, itok_B_37_3939, itok_B_0_6, itok_B_0_7, fside_8xS_0, L0_cond_weights, L1_cond_Wq, L1_cond_Wk, L1_cond_Wv, L1_cond_Wo, L1_cond_q_norm_scale, L1_cond_k_norm_scale, L1_cond_k_blocks, L1_cond_v_blocks, L2_cond_W, L2_cond_A, L2_cond_Bm, L2_cond_scalings, L3_cond_weights):
    import jax
    import jax.numpy as jnp

    def _L0_cond_ref(x, conditions, weights):
        import jax, jax.numpy as jnp
        import numpy as np
        B, C, T = (128, 32, 256)
        S, D = (200, 32)
        w = weights[conditions]
        return jnp.einsum('bct,bcd->bdt', x, w)

    def _L1_cond_ref(x, Wq, Wk, Wv, Wo, q_norm_scale, k_norm_scale, k_blocks, v_blocks, block_tables, kv_lens):
        import jax, jax.numpy as jnp
        import numpy as np
        H, G, HD = (8, 4, 32)
        GSZ = H // G
        BLOCK = 16
        WINDOW = 128
        SCALE = 256.0 ** (-0.5)
        EPS = 1e-06
        THETA = 10000.0
        B, T, D = (16, 4, 256)
        NBLK = 257

        def _rms(x, scale):
            var = jnp.mean(x * x, axis=-1, keepdims=True)
            return x * jax.lax.rsqrt(var + EPS) * (1.0 + scale)

        def _rope(x, pos):
            half = HD // 2
            inv = 1.0 / THETA ** (jnp.arange(half, dtype=jnp.float32) / half)
            ang = pos[:, :, None].astype(jnp.float32) * inv
            cos = jnp.cos(ang)[:, None, :, :]
            sin = jnp.sin(ang)[:, None, :, :]
            x1, x2 = (x[..., :half], x[..., half:])
            return jnp.concatenate([x1 * cos - x2 * sin, x2 * cos + x1 * sin], axis=-1)
        Bx, Tx, _ = x.shape
        q = jnp.einsum('btd,od->bto', x, Wq).reshape(Bx, Tx, H, HD).transpose(0, 2, 1, 3)
        k = jnp.einsum('btd,od->bto', x, Wk).reshape(Bx, Tx, G, HD).transpose(0, 2, 1, 3)
        v = jnp.einsum('btd,od->bto', x, Wv).reshape(Bx, Tx, G, HD).transpose(0, 2, 1, 3)
        q = _rms(q, q_norm_scale)
        k = _rms(k, k_norm_scale)
        pos = kv_lens[:, None] + jnp.arange(Tx, dtype=jnp.int32)
        q = _rope(q, pos)
        k = _rope(k, pos)
        slot = pos // BLOCK
        off = pos % BLOCK
        blk = jnp.take_along_axis(block_tables, slot, axis=1)
        k_blocks = k_blocks.at[blk, :, off, :].set(k.transpose(0, 2, 1, 3))
        v_blocks = v_blocks.at[blk, :, off, :].set(v.transpose(0, 2, 1, 3))
        k_all = k_blocks[block_tables].transpose(0, 2, 1, 3, 4).reshape(Bx, G, -1, HD)
        v_all = v_blocks[block_tables].transpose(0, 2, 1, 3, 4).reshape(Bx, G, -1, HD)
        S = k_all.shape[2]
        qg = q.reshape(Bx, G, GSZ, Tx, HD)
        scores = jnp.einsum('bghtd,bgsd->bghts', qg, k_all) * SCALE
        kpos = jnp.arange(S, dtype=jnp.int32)
        allowed = (kpos[None, None, :] <= pos[:, :, None]) & (kpos[None, None, :] > pos[:, :, None] - WINDOW)
        scores = jnp.where(allowed[:, None, None, :, :], scores, -jnp.inf)
        p = jax.nn.softmax(scores, axis=-1)
        o = jnp.einsum('bghts,bgsd->bghtd', p, v_all).reshape(Bx, H, Tx, HD)
        o = o.transpose(0, 2, 1, 3).reshape(Bx, Tx, H * HD)
        return jnp.einsum('bto,do->btd', o, Wo)

    def _L2_cond_ref(x, W, A, Bm, scalings, adapter_idx):
        import jax, jax.numpy as jnp
        import numpy as np
        B, T, D_IN, D_OUT = (16, 256, 256, 256)
        N_ADAPTERS, RANK = (8, 16)
        H = jnp.einsum('btd,od->bto', x, W)
        A_b = A[adapter_idx]
        B_b = Bm[adapter_idx]
        s_b = scalings[adapter_idx]
        xa = jnp.einsum('btd,brd->btr', x, A_b)
        delta = jnp.einsum('btr,bor->bto', xa, B_b)
        delta = jax.lax.stop_gradient(delta * s_b[:, None, None])
        return H + delta

    def _L3_cond_ref(x, subjects, weights, bias):
        import jax, jax.numpy as jnp
        import numpy as np
        B, C, T = (64, 32, 256)
        D, N = (32, 8)
        w = weights[subjects]
        b = bias[subjects]
        out = jnp.einsum('bct,bcd->bdt', x, w)
        out = out + b[:, :, None]
        return out
    x = x + _L0_cond_ref(x, itok_B_1_198, L0_cond_weights)
    x = x + _L1_cond_ref(x, L1_cond_Wq, L1_cond_Wk, L1_cond_Wv, L1_cond_Wo, L1_cond_q_norm_scale, L1_cond_k_norm_scale, L1_cond_k_blocks, L1_cond_v_blocks, itok_Bx257_0_4111, itok_B_37_3939)
    x = x + _L2_cond_ref(x, L2_cond_W, L2_cond_A, L2_cond_Bm, L2_cond_scalings, itok_B_0_6)
    x = x + _L3_cond_ref(x, itok_B_0_7, L3_cond_weights, fside_8xS_0)
    return x

_drawn_inputs = setup_inputs


def setup_inputs(seed=0):
    import zlib

    import numpy as np

    out = dict(_drawn_inputs(seed))
    spreads = {'L2_cond_scalings': (1.0, 0.6)}
    factors = {'L1_cond_q_norm_scale': 8.0,
     'L1_cond_k_norm_scale': 64.0,
     'L1_cond_k_blocks': 3.457,
     'L2_cond_A': 2.995,
     'L2_cond_Bm': 2.994,
     'fside_8xS_0': 2.713,
     'L1_cond_Wk': 3.054}
    for name, (base, spread) in spreads.items():
        noise = np.random.default_rng([zlib.crc32(name.encode()), seed]).standard_normal(out[name].shape)
        drawn = base * np.exp(spread * noise) if base else spread * noise
        out[name] = jnp.asarray(drawn.astype(out[name].dtype))
    for name, factor in factors.items():
        out[name] = (out[name] * factor).astype(out[name].dtype)
    return out
```

```python
import numpy as np
import concourse.bass as bass
from concourse import mybir
from contextlib import ExitStack

F32 = mybir.dt.float32
I32 = mybir.dt.int32
ALU = mybir.AluOpType
ACT = mybir.ActivationFunctionType
AX = mybir.AxisListType

P = 128
B, T, D = 128, 32, 256
ROWS = B * T
BPT = P // T
TILES = ROWS // P
G, GSZ, HD = 4, 2, 32
H = G * GSZ
QK = (H + G) * HD
KV = G * HD
BLK = 16
NBLK = 257
CACHE = 4112
WINDOW = 128
SCALE = 256.0 ** -0.5
EPS = 1e-6
THETA = 10000.0
ROW_G = BLK * HD
ROW_B = G * ROW_G
WS = 3
NW = B * WS
RS = 11
RSP = 12
KEYS = RS * BLK
KC = KEYS // 2
PH = 4
PB = B // PH
PROWS = PB * T
OFFS = WINDOW + BLK - 2
BIG = 1 << 20
NEG = -1.0e30
RANK = 16
NAD = P // RANK
TP = NBLK + 15
LAG = 3
TWO_PI_HI = 6.28125
TWO_PI_LO = float(2 * np.pi - 6.28125)
MAGIC = 12582912.0
PI = float(np.float32(3.1415925))
INV_FREQ = (np.float32(1.0) / np.float32(THETA) ** (np.arange(HD // 2, dtype=np.float32) / np.float32(HD // 2))).astype(np.float32)


def build(nc, a, dbg=None):
    ctx = ExitStack()
    with ctx:
        def sb(name, shape, dt=F32):
            return ctx.enter_context(nc.sbuf_tensor(name, shape, dt))

        def sem(name):
            return ctx.enter_context(nc.semaphore(name))

        def dram(name, shape, dt=F32):
            return nc.dram_tensor(name, shape, dt, kind="Internal").ap()

        x_rows = a["x"].rearrange("b t d -> (b t) d")
        out_rows = a["out"].rearrange("b t d -> (b t) d")
        k_by_block = a["L1_cond_k_blocks"].rearrange("n g o d -> n (g o d)")
        v_by_head = a["L1_cond_v_blocks"].rearrange("n g o d -> (n g) (o d)")
        v_by_block = a["L1_cond_v_blocks"].rearrange("n g o d -> n (g o d)")
        w0_by_b = dram("w0_by_b", [B, T * T])
        w3_by_b = dram("w3_by_b", [B, T * T])
        b3_by_b = dram("b3_by_b", [B, T])
        writer_keys = dram("writer_keys", [NW])
        new_rows = dram("new_rows", [ROWS, 2 * KV])
        x1_T = dram("x1_T", [2, P, ROWS])
        q_T = dram("q_T", [GSZ, P, ROWS])
        merged_k = dram("merged_k", [NW, ROW_B])
        merged_v = dram("merged_v", [NW, ROW_B])
        merged_v_by_head = merged_v.rearrange("n (g e) -> (n g) e", g=G)
        k_slots = dram("k_slots", [2, B * RSP], I32)
        v_slots = dram("v_slots", [2, B * G * RSP], I32)

        ident = sb("ident", [P, P])
        wqkv = sb("wqkv", [P, 2, 512])
        woT = sb("woT", [P, GSZ, D])
        wT = sb("wT", [P, 2, D])
        aT = sb("aT", [P, 2, P])
        bT = sb("bT", [P, D])
        same_b = sb("same_b", [P, BPT])
        head_scale = sb("head_scale", [P, G])
        adapt = sb("adapt", [P, B])
        w0_all = sb("w0_all", [P, TILES, T])
        w3_all = sb("w3_all", [P, TILES, T])
        b3_all = sb("b3_all", [P, TILES])
        b3_nat = sb("b3_nat", [TILES, P])
        cos2 = sb("cos2", [P, TILES, HD])
        sin2 = sb("sin2", [P, TILES, HD])
        gain = sb("gain", [P, H + G, HD])
        mask_wide = sb("mask_wide", [P, KEYS + OFFS])
        mask_at = sb("mask_at", [1, B], I32)
        eps_t = sb("eps_t", [P, 1])
        slot_idx = sb("slot_idx", [P, PH, 2 * 3 + 2 * RSP], I32)
        slot_now = sb("slot_now", [P, 2 * 3 + 2 * RSP], I32)
        kv_col = sb("kv_col", [P, 8], I32)
        cols = sb("cols", [P, 16])
        own_idx = sb("own_idx", [P, WS * BLK], I32)
        own_any = sb("own_any", [P, WS * BLK], I32)
        w_idx = sb("w_idx", [P, WS], I32)
        idx_cols = sb("idx_cols", [P, 4], I32)

        arena = sb("arena", [P, 25600])
        row_new = arena[:, 0:12288].rearrange("p (s e) -> p s e", s=WS * BLK)
        blk_k = arena[:, 12288:18432].rearrange("p (j e) -> p j e", j=WS)
        blk_v = arena[:, 18432:24576].rearrange("p (j e) -> p j e", j=WS)
        cover = arena[:, 0:6144].rearrange("p (o w) -> p o w", o=BLK)
        match = arena[:, 6144:10752].rearrange("p (r w) -> p r w", r=RSP)
        owner_o = arena[:, 10752:11136]
        match2 = arena[:, 0:4608].rearrange("p (r w) -> p r w", r=RSP)
        k_raw = arena[:, 0:6144].rearrange("p (u g o d) -> p u g o d", u=3, g=G, o=BLK)
        v_raw = arena[:, 6144:11776]
        kT = arena[:, 11776:17408].rearrange("p (b k) -> p b k", b=PB)
        k_perm = arena[:, 17408:17408 + 6144].rearrange("p (u o e) -> p u o e", u=3, o=BLK)
        vK = arena[:, 17408:25600].rearrange("p (c d n) -> p c d n", c=2, d=HD)
        stage = arena[:, 12288:17408]
        wq_n = stage[:, 0:512].rearrange("p (c n) -> p c n", c=2)
        wk_n = stage[:, 512:768]
        wv_n = stage[:, 768:1024]
        wo_n = stage[:, 1024:1536].rearrange("p (c n) -> p c n", c=2)
        w_n = stage[:, 1536:2048].rearrange("p (c n) -> p c n", c=2)
        a_n = stage[:, 2048:2304]
        wo_p = stage[:, 2560:3072].rearrange("p (c h n) -> p c h n", c=2, h=GSZ)
        bm_n = stage[:, 2304:2560].rearrange("p (c n r) -> p c n r", c=2, n=NAD)
        small = sb("small", [P, 3264])
        table = small[:, 0:TP]
        hot_r = small[:, 272:272 + NBLK]
        hot_w = small[:, 544:544 + NBLK]
        iota_row = small[:, 816:816 + NBLK]
        wkey_bc = small[:, 1088:1088 + NW]
        value_bc = small[:, 1472:1472 + NW]
        order_bc = small[:, 1856:1856 + NW]
        m_bc = small[:, 2240:2240 + B]
        tmp_bc = small[:, 2368:2368 + B]
        read_blk = small[:, 2496:2496 + RSP]
        read_w = small[:, 2512:2512 + RSP]
        wblk = small[:, 2528:2528 + WS]
        wkey = small[:, 2532:2532 + WS]
        own_max = small[:, 2544:2592]
        own_none = small[:, 2592:2640]
        off_io = small[:, 2640:2688]
        own_f = small[:, 2688:2736]
        r_hit = small[:, 2736:2748]
        r_a = small[:, 2752:2764]
        r_b = small[:, 2768:2780]
        r_ag = small[:, 2784:2832]
        r_bg = small[:, 2832:2880]
        scrap = small[:, 2880:2880 + NW]
        table_i = sb("table_i", [P, NBLK], I32)
        kv_bc_i = sb("kv_bc_i", [P, 2, B], I32)
        r_int = sb("r_int", [P, 2 * RSP + 2 * G * RSP], I32)
        n_idx_bc = sb("n_idx_bc", [P, B], I32)

        ring = sb("ring", [P, 8032])
        def cut(at, n):
            return ring[:, at:at + n]
        xt = [cut(0, 256), cut(256, 256)]
        w0_bd = [cut(512, 128), cut(640, 128)]
        x1t = [cut(768 + 256 * s, 256).rearrange("p (c r) -> p c r", c=2) for s in range(2)]
        sq = [cut(1280 + 384 * s, QK) for s in range(2)]
        nrm = [cut(2048 + 384 * s, QK) for s in range(2)]
        gained = [cut(2816 + 384 * s, QK) for s in range(2)]
        rot_c = [cut(3584 + 384 * s, QK) for s in range(2)]
        rot_s = [cut(4352 + 384 * s, QK) for s in range(2)]
        qkv_o = [cut(5120 + 512 * s, 512) for s in range(2)]
        qt = [cut(6144 + 256 * s, 256).rearrange("p (h r) -> p h r", h=GSZ) for s in range(2)]
        ssum = [cut(6656 + 16 * s, 12) for s in range(2)]
        rstd = [cut(6688 + 16 * s, 12) for s in range(2)]
        rtmp = [cut(6720 + 16 * s, 12) for s in range(2)]
        angle = cut(0, 512).rearrange("p (i f) -> p i f", i=TILES)
        turn_a = cut(512, 512).rearrange("p (i f) -> p i f", i=TILES)
        turn_b = cut(1024, 512).rearrange("p (i f) -> p i f", i=TILES)
        turn_c = cut(1536, 512).rearrange("p (i f) -> p i f", i=TILES)
        pos_f = cut(2048, 32)
        inv_f = cut(2080, 16)
        gathered = arena[:, 22528:24576].rearrange("p (a e) -> p a e", a=2)
        gathered_b = arena[:, 24576:24608]
        SR, PR = 2, 4
        shifted = [cut(352 * s, 352).rearrange("p (j k) -> p j k", j=2) for s in range(3)]
        probs = [cut(1056 + 352 * s, 352).rearrange("p (j k) -> p j k", j=2) for s in range(PR)]
        normed = [cut(2464 + 352 * s, 352).rearrange("p (j k) -> p j k", j=2) for s in range(PR)]
        pT = [cut(3872 + 512 * s, 512) for s in range(2)]
        masks = [cut(4896 + KEYS * s, KEYS) for s in range(8)]
        x3 = [cut(6304 + 256 * s, 256) for s in range(2)]
        o_t = [cut(6816 + 256 * s, 256) for s in range(2)]
        w3_bd = [cut(7328 + 128 * s, 128) for s in range(4)]
        neg_max = cut(7840, 64)
        p_sum = cut(7904, 64)
        p_inv = cut(7968, 64)
        q_bd = [sb(f"q_bd{s}", [P, BPT, G, GSZ * T]) for s in range(2)]
        qT_ph = sb("qT_ph", [P, GSZ, PROWS])
        xT_ph = sb("xT_ph", [P, 2, PROWS])
        oT_ph = small[:, 0:GSZ * PROWS].rearrange("p (h r) -> p h r", h=GSZ)
        low = small[:, GSZ * PROWS:GSZ * PROWS + 512]

        bank = [ctx.enter_context(nc.psum_tensor(f"bank{i}", [P, 512], F32)) for i in range(8)]

        names = """weights_in xt_in0 xt_in1 const_in table_in kv_in wgath wgath_out wgath_back pool_const pool_step
            wtr_done wtr_moved dve_pre act_pre dve_tab keys_out keys_back x_l0 l0_done x1_ready x1_out0 x1_out1 qkv_done sq_done
            bd0_ready dve_a ms_done sqrt_done v_copied rows_ready rows_out0 rows_out1 qtr_done qt_ready qt_out0 qt_out1
            own_known new_zero blk_in rows_in merged_done merged_out slots_out slots_back
            ph_in orig_in merged_in slots_now ktr_done ktr_moved vtr_done vtr_moved raw_free qbd_ready mask_ready
            s_done shifted_done exp_done inv_done norm_done pt_done pt_moved av_done o_moved y_done y_moved
            lo_done lo_moved x3_done x3_moved bd3_ready l3_done l3_moved out_done0 out_done1 mwide b3_ready pre2 angles_ready wo_sorted k_sorted held""".split()
        S = {n: sem(n) for n in names}

        block = ctx.enter_context(nc.Block())

        def hold(eng):
            eng.sem_inc(S["held"], 1)

        @block.sync
        def _(sp):
            for dst, src in ((table_i[:, :], a["itok_Bx257_0_4111"]),
                             (kv_col[:, 0:1], a["itok_B_37_3939"].rearrange("(b o) -> b o", o=1))):
                sp.dma_start(dst, src).then_inc(S["table_in"], 16)
            lens = a["itok_B_37_3939"].rearrange("(o b) -> o b", o=1)
            sp.dma_start(kv_bc_i[:, 0, :], lens.broadcast_to([P, B])).then_inc(S["kv_in"], 16)
            for dst, src in ((wq_n, a["L1_cond_Wq"].rearrange("(c p) d -> p c d", p=P)),
                             (wk_n, a["L1_cond_Wk"]), (wv_n, a["L1_cond_Wv"]),
                             (wo_n, a["L1_cond_Wo"].rearrange("(c p) d -> p c d", p=P)),
                             (w_n, a["L2_cond_W"].rearrange("(c p) d -> p c d", p=P)),
                             (a_n, a["L2_cond_A"].rearrange("n r d -> (n r) d")),
                             (bm_n[:, 0], a["L2_cond_Bm"].rearrange("n (c p) r -> c p n r", p=P)[0]),
                             (bm_n[:, 1], a["L2_cond_Bm"].rearrange("n (c p) r -> c p n r", p=P)[1])):
                sp.dma_start(dst, src).then_inc(S["weights_in"], 16)
            ones = lambda n: a[n].rearrange("(o d) -> o d", o=1)
            for n in range(NAD):
                sp.dma_start(cols[RANK * n:RANK * n + RANK, 0:1], ones("L2_cond_scalings")[:, n:n + 1].broadcast_to([RANK, 1])
                             ).then_inc(S["const_in"], 16)
            sp.dma_start(gain[:, 0, :], ones("L1_cond_q_norm_scale").broadcast_to([P, HD])).then_inc(S["const_in"], 16)
            sp.dma_start(gain[:, H, :], ones("L1_cond_k_norm_scale").broadcast_to([P, HD])).then_inc(S["const_in"], 16)
            sp.dma_start(n_idx_bc[:, :], ones("itok_B_0_6").broadcast_to([P, B])).then_inc(S["const_in"], 16)
            sp.wait_ge(S["wgath"], 48)
            sp.dma_start(w0_by_b, gathered[:, 0, :]).then_inc(S["wgath_out"], 16)
            sp.dma_start(w3_by_b, gathered[:, 1, :]).then_inc(S["wgath_out"], 16)
            sp.dma_start(b3_by_b, gathered_b).then_inc(S["wgath_out"], 16)
            sp.wait_ge(S["wgath_out"], 48)
            for dst, src in ((w0_all, w0_by_b), (w3_all, w3_by_b)):
                for j in range(BPT):
                    sp.dma_start(dst[T * j:T * j + T, :, :],
                                 src.rearrange("(i j) (t d) -> j t i d", j=BPT, d=T)[j]).then_inc(S["wgath_back"], 16)
            sp.dma_start(b3_nat[:, :], b3_by_b.rearrange("(i j) d -> i (j d)", j=BPT)).then_inc(S["wgath_back"], 16)
            sp.wait_ge(S["dve_tab"], 1)
            sp.dma_start(writer_keys.rearrange("(b j) -> b j", j=WS), wkey).then_inc(S["keys_out"], 16)
            sp.wait_ge(S["keys_out"], 16)
            sp.dma_start(wkey_bc, writer_keys.rearrange("(o w) -> o w", o=1).broadcast_to([P, NW])).then_inc(S["keys_back"], 16)
            sp.wait_ge(S["act_pre"], 4)
            def tile_pair(it, later):
                for s in range(2):
                    if later:
                        sp.wait_ge(S["l0_done"], 2 * it)
                    sp.dma_start(xt[s], x_rows[bass.ds((it * 2 + s) * P, P), :]).then_inc(S[f"xt_in{s}"], 16)
                for s in range(2):
                    at = bass.ds(sp.snap((it * 2 + s) * P) if later else s * P, P)
                    sp.wait_ge(S["x1_ready"], 2 * it + s + 1)
                    hold(sp)
                    sp.dma_start(x1_T.rearrange("c p r -> p c r")[:, :, at], x1t[s]).then_inc(S[f"x1_out{s}"], 16)
                    sp.wait_ge(S["rows_ready"], 2 * it + s + 1)
                    sp.wait_ge(S["v_copied"], 2 * it + s + 1)
                    sp.dma_start(new_rows[at, :], qkv_o[s][:, D:2 * D]).then_inc(S[f"rows_out{s}"], 16)
                    sp.wait_ge(S["qt_ready"], 2 * it + s + 1)
                    sp.dma_start(q_T.rearrange("h p r -> p h r")[:, :, at], qt[s]).then_inc(S[f"qt_out{s}"], 16)

            tile_pair(0, False)
            with sp.Fori(1, TILES // 2) as it:
                tile_pair(it, True)
            sp.wait_ge(S["dve_tab"], 2)
            for n in range(2):
                sp.dma_start(k_slots[n].rearrange("(b e) -> b e", e=RSP), r_int[:, RSP * n:RSP * n + RSP]).then_inc(S["slots_out"], 16)
                sp.dma_start(v_slots[n].rearrange("(b e) -> b e", e=G * RSP),
                             r_int[:, 24 + 48 * n:24 + 48 * n + 48]).then_inc(S["slots_out"], 16)
            sp.wait_ge(S["slots_out"], 64)
            for n in range(2):
                sp.dma_start(slot_idx[:, :, 3 * n:3 * n + 3],
                             k_slots[n].rearrange("(h p u) -> p h u", p=P, u=3)).then_inc(S["slots_back"], 16)
                sp.dma_start(slot_idx[:, :, 6 + RSP * n:6 + RSP * n + RSP],
                             v_slots[n].rearrange("(h p r) -> p h r", p=P, r=RSP)).then_inc(S["slots_back"], 16)
            sp.wait_ge(S["merged_done"], 1)
            sp.dma_start(merged_k.rearrange("(b j) e -> b j e", j=WS), blk_k).then_inc(S["merged_out"], 16)
            sp.wait_ge(S["merged_done"], 2)
            sp.dma_start(merged_v.rearrange("(b j) e -> b j e", j=WS), blk_v).then_inc(S["merged_out"], 16)
            for s in range(2):
                sp.wait_ge(S[f"x1_out{s}"], 16 * (TILES // 2))
                sp.wait_ge(S[f"qt_out{s}"], 16 * (TILES // 2))
            def phase(ph, later):
                at = bass.ds(ph * PROWS, PROWS)
                if later:
                    sp.wait_ge(S["qbd_ready"], 8 * ph)
                sp.dma_start(qT_ph[:, :, :], q_T.rearrange("h p r -> p h r")[:, :, at]).then_inc(S["ph_in"], 16)
                if later:
                    sp.wait_ge(S["x3_done"], 8 * ph)
                sp.dma_start(xT_ph[:, :, :], x1_T.rearrange("c p r -> p c r")[:, :, at]).then_inc(S["ph_in"], 16)
                for i in range(8):
                    sp.wait_ge(S["l3_moved"], 8 * ph + i + 1)
                    sp.dma_start(out_rows[bass.ds(ph * PROWS + i * P, P), :], o_t[i % 2]).then_inc(S[f"out_done{i % 2}"], 16)

            phase(0, False)
            with sp.Fori(1, PH) as ph:
                phase(ph, True)
            for s in range(2):
                sp.wait_ge(S[f"out_done{s}"], 16 * PH * 4)

        @block.gpsimd
        def _(pool):
            g = nc.gpsimd
            steps = [0]

            def link(ins):
                ins.then_inc(S["pool_step"], 1)
                steps[0] += 1
                pool.wait_ge(S["pool_step"], steps[0])

            for n, name in enumerate(("itok_B_1_198", "itok_B_0_7")):
                pool.dma_start(idx_cols[:, n:n + 1], a[name].rearrange("(b o) -> b o", o=1)).then_inc(S["pre2"], 16)
            pool.wait_ge(S["pre2"], 32)
            g.indirect_dma_start(gathered[:, 0, :], None, a["L0_cond_weights"].rearrange("s c d -> s (c d)"),
                                 bass.IndirectOffsetOnAxis(ap=idx_cols[:, 0:1], axis=0),
                                 bounds_check=199, oob_is_err=False).then_inc(S["wgath"], 16)
            g.indirect_dma_start(gathered[:, 1, :], None, a["L3_cond_weights"].rearrange("s c d -> s (c d)"),
                                 bass.IndirectOffsetOnAxis(ap=idx_cols[:, 1:2], axis=0),
                                 bounds_check=7, oob_is_err=False).then_inc(S["wgath"], 16)
            g.indirect_dma_start(gathered_b, None, a["fside_8xS_0"],
                                 bass.IndirectOffsetOnAxis(ap=idx_cols[:, 1:2], axis=0),
                                 bounds_check=7, oob_is_err=False).then_inc(S["wgath"], 16)
            link(g.memset(ident[:, :], 0.0))
            link(g.affine_select(out=ident[:, :], in_=ident[:, :], compare_op=ALU.not_equal, fill=1.0, base=0,
                                 pattern=[[-1, P]], channel_multiplier=1))
            g.iota(iota_row, pattern=[[1, NBLK]], base=0, channel_multiplier=0,
                   allow_small_or_imprecise_dtypes=True).then_inc(S["pool_const"], 1)
            g.iota(off_io, pattern=[[0, WS], [1, BLK]], base=0, channel_multiplier=0,
                   allow_small_or_imprecise_dtypes=True).then_inc(S["pool_const"], 1)
            g.iota(order_bc, pattern=[[1, NW]], base=1, channel_multiplier=0,
                   allow_small_or_imprecise_dtypes=True).then_inc(S["pool_const"], 1)
            g.iota(value_bc.rearrange("p (b j) -> p b j", j=WS), pattern=[[T, B], [BLK, WS]], base=64, channel_multiplier=0,
                   allow_small_or_imprecise_dtypes=True).then_inc(S["pool_const"], 1)
            g.iota(kv_col[:, 1:2], pattern=[[0, 1]], base=0, channel_multiplier=1).then_inc(S["pool_const"], 1)
            g.memset(eps_t[:, :], EPS).then_inc(S["pool_const"], 1)
            for f in range(HD // 2):
                g.memset(inv_f[:, f:f + 1], float(INV_FREQ[f])).then_inc(S["pool_const"], 1)
            for m, v in ((same_b, 1.0), (head_scale, SCALE)):
                link(g.memset(m[:, :], v))
                link(g.affine_select(out=m[:, :], in_=m[:, :], compare_op=ALU.is_ge, fill=0.0, base=0,
                                     pattern=[[-T, BPT]], channel_multiplier=1))
                link(g.affine_select(out=m[:, :], in_=m[:, :], compare_op=ALU.is_ge, fill=0.0, base=T - 1,
                                     pattern=[[T, BPT]], channel_multiplier=-1))
            pool.wait_ge(S["wgath"], 48)
            for q in range(BPT):
                m = mask_wide[T * q:T * q + T, :]
                link(g.memset(m, 0.0))
                link(g.affine_select(out=m, in_=m, compare_op=ALU.is_ge, fill=NEG, base=OFFS,
                                     pattern=[[-1, KEYS + OFFS]], channel_multiplier=1))
                link(g.affine_select(out=m, in_=m, compare_op=ALU.is_ge, fill=NEG, base=WINDOW - 1 - OFFS,
                                     pattern=[[1, KEYS + OFFS]], channel_multiplier=-1))
            g.memset(small[:, NBLK:TP], 0.0).then_inc(S["pool_const"], 1)
            pool.wait_ge(S["pool_step"], steps[0])
            g.memset(cols[:, 15:16], 0.0).then_inc(S["pool_const"], 1)
            pool.wait_ge(S["wgath_back"], 16 * 9)
            pool.wait_ge(S["act_pre"], 4)
            def tile_pair(it, later):
                for s in range(2):
                    if later:
                        pool.wait_ge(S["l0_done"], 2 * it)
                    g.tensor_tensor(w0_bd[s].rearrange("p (j d) -> p j d", j=BPT),
                                    w0_all[:, bass.ds(it * 2 + s, 1), :].broadcast_to([P, BPT, T]),
                                    same_b[:, :, None].broadcast_to([P, BPT, T]), op=ALU.mult).then_inc(S["bd0_ready"], 1)
                    pool.wait_ge(S["bd0_ready"], 4 * it + 2 * s + 1)
                    g.tensor_tensor(w0_bd[s], w0_bd[s], ident[:, :], op=ALU.add).then_inc(S["bd0_ready"], 1)

            tile_pair(0, False)
            with pool.Fori(1, TILES // 2) as it:
                tile_pair(it, True)
            pool.wait_ge(S["own_known"], 1)
            for j in range(WS):
                for dst, src in ((blk_k, k_by_block), (blk_v, v_by_block)):
                    g.indirect_dma_start(dst[:, j, :], None, src, bass.IndirectOffsetOnAxis(ap=w_idx[:, j:j + 1], axis=0),
                                         bounds_check=CACHE - 1, oob_is_err=False).then_inc(S["blk_in"], 16)
            for s in range(2):
                pool.wait_ge(S[f"rows_out{s}"], 16 * (TILES // 2))
            pool.wait_ge(S["new_zero"], 1)
            for n in range(WS * BLK):
                g.indirect_dma_start(row_new[:, n, :], None, new_rows, bass.IndirectOffsetOnAxis(ap=own_idx[:, n:n + 1], axis=0),
                                     bounds_check=ROWS - 1, oob_is_err=False).then_inc(S["rows_in"], 16)
            pool.wait_ge(S["slots_back"], 64)
            pool.wait_ge(S["merged_out"], 32)
            def phase(ph, later):
                g.tensor_copy(slot_now[:, :], slot_idx[:, bass.ds(ph, 1), :].rearrange("p h e -> p (h e)")).then_inc(S["slots_now"], 1)
                pool.wait_ge(S["slots_now"], ph + 1)
                if later:
                    pool.wait_ge(S["ktr_done"], 12 * ph)
                if later:
                    pool.wait_ge(S["vtr_done"], 16 * ph)
                hold(pool)
                for n, done in enumerate(("orig_in", "merged_in")):
                    for u in range(3):
                        g.indirect_dma_start(k_raw[:, u].rearrange("p g o d -> p (g o d)"), None, (k_by_block, merged_k)[n],
                                             bass.IndirectOffsetOnAxis(ap=slot_now[:, 3 * n + u:3 * n + u + 1], axis=0),
                                             bounds_check=(CACHE, NW)[n] - 1, oob_is_err=False).then_inc(S[done], 16)
                    for r in range(RS):
                        c = 6 + RSP * n + r
                        g.indirect_dma_start(v_raw[:, ROW_G * r:ROW_G * (r + 1)], None, (v_by_head, merged_v_by_head)[n],
                                             bass.IndirectOffsetOnAxis(ap=slot_now[:, c:c + 1], axis=0),
                                             bounds_check=(CACHE, NW)[n] * G - 1, oob_is_err=False).then_inc(S[done], 16)
                    pool.wait_ge(S[done], 16 * (3 + RS) * (ph + 1))
                    hold(pool)
                for b in range(PB + 1):
                    if b < PB:
                        if b >= 8:
                            pool.wait_ge(S["shifted_done"], 2 * (ph * PB + b - 7))
                        else:
                            if later:
                                pool.wait_ge(S["shifted_done"], 2 * (ph * PB))
                        at = pool.value_load(mask_at[0:1, bass.ds(ph * PB + b, 1)], min_val=0, max_val=OFFS)
                        g.tensor_tensor(masks[b % 8], mask_wide[:, bass.ds(at, KEYS)],
                                        cols[:, 15:16].broadcast_to([P, KEYS]), op=ALU.add).then_inc(S["mask_ready"], 1)
                    if b >= 1:
                        m = b - 1
                        pool.wait_ge(S["inv_done"], ph * PB + m + 1)
                        if m >= PR:
                            pool.wait_ge(S["pt_done"], ph * PB + m - PR + 1)
                        else:
                            if later:
                                pool.wait_ge(S["pt_done"], ph * PB)
                        hold(pool)
                        for j in range(2):
                            g.tensor_scalar(normed[m % PR][:, j, :], probs[m % PR][:, j, :], p_inv[:, 2 * m + j:2 * m + j + 1], 1.0,
                                            ALU.mult, ALU.mult).then_inc(S["norm_done"], 1)
                    if b % 4 == 0 and b >= 4:
                        i = b // 4 - 1
                        if i >= 4:
                            pool.wait_ge(S["l3_done"], 8 * ph + i - 3)
                        else:
                            if later:
                                pool.wait_ge(S["l3_done"], 8 * ph)
                        g.tensor_tensor(w3_bd[i % 4].rearrange("p (j d) -> p j d", j=BPT),
                                        w3_all[:, bass.ds(ph * 8 + i, 1), :].broadcast_to([P, BPT, T]),
                                        same_b[:, :, None].broadcast_to([P, BPT, T]), op=ALU.mult).then_inc(S["bd3_ready"], 1)
                        pool.wait_ge(S["bd3_ready"], 16 * ph + 2 * i + 1)
                        g.tensor_tensor(w3_bd[i % 4], w3_bd[i % 4], ident[:, :], op=ALU.add).then_inc(S["bd3_ready"], 1)

            phase(0, False)
            with pool.Fori(1, PH) as ph:
                phase(ph, True)

        wtr = []
        for c in range(2):
            for oc in range(2):
                wtr.append((wq_n[:, oc, c * P:c * P + P],
                            wqkv[:, c, 0:D].rearrange("p (h g d) -> p g h d", h=GSZ, g=G)[:, 2 * oc:2 * oc + 2], "q"))
            wtr.append((wk_n[:, c * P:c * P + P], wqkv[:, c, D:D + KV], ""))
            wtr.append((wv_n[:, c * P:c * P + P], wqkv[:, c, D + KV:D + 2 * KV], ""))
        for oc in range(2):
            for h in range(GSZ):
                wtr.append((wo_p[:, oc, h, :],
                            woT[:, h, oc * P:oc * P + P], ""))
            for c in range(2):
                wtr.append((w_n[:, oc, c * P:c * P + P], wT[:, c, oc * P:oc * P + P], "i" if c == oc else ""))
            wtr.append((a_n[:, oc * P:oc * P + P], aT[:, oc, :], ""))
            wtr.append((bm_n[:, oc].rearrange("p n r -> p (n r)"), bT[:, oc * P:oc * P + P], ""))
        NWT = len(wtr)

        @block.tensor
        def _(pe):
            mm = nc.tensor.matmul
            pe.wait_ge(S["weights_in"], 16 * 8)
            pe.wait_ge(S["wo_sorted"], 4)
            pe.wait_ge(S["pool_const"], 24)
            for n, (src, _, _) in enumerate(wtr):
                if n >= 4:
                    pe.wait_ge(S["wtr_moved"], n - 3)
                nc.tensor.transpose(bank[n % 4][:, 0:P], src, ident[:, :]).then_inc(S["wtr_done"], 1)
            pe.wait_ge(S["wgath_back"], 16 * 9)
            pe.wait_ge(S["wtr_moved"], NWT)
            nc.tensor.transpose(bank[6][:, 0:TILES], b3_nat[:, :], ident[0:TILES, 0:TILES]).then_inc(S["wtr_done"], 1)
            def tile_pair(it, later):
                for s in range(2):
                    pe.wait_ge(S[f"xt_in{s}"], 16 * (it + 1))
                    pe.wait_ge(S["bd0_ready"], 4 * it + 2 * s + 2)
                    if later:
                        pe.wait_ge(S["x1_ready"], 2 * it)
                    for c in range(2):
                        last = mm(bank[s][:, c * P:c * P + P], xt[s][:, c * P:c * P + P], w0_bd[s], start=True, stop=True)
                    last.then_inc(S["l0_done"], 1)
                for s in range(2):
                    pe.wait_ge(S["x1_ready"], 2 * it + s + 1)
                    if later:
                        pe.wait_ge(S["dve_a"], 12 * it)
                    if later:
                        pe.wait_ge(S["v_copied"], 2 * it)
                    for c in range(2):
                        last = mm(bank[2 + s][:, :], x1t[s][:, c, :], wqkv[:, c, :], start=c == 0, stop=c == 1)
                    last.then_inc(S["qkv_done"], 1)
                for s in range(2):
                    pe.wait_ge(S["rows_ready"], 2 * it + s + 1)
                    if later:
                        pe.wait_ge(S["qt_ready"], 2 * it)
                    for h in range(GSZ):
                        last = nc.tensor.transpose(bank[4 + s][:, h * P:h * P + P], qkv_o[s][:, h * P:h * P + P], ident[:, :])
                    last.then_inc(S["qtr_done"], 1)

            tile_pair(0, False)
            with pe.Fori(1, TILES // 2) as it:
                tile_pair(it, True)
            def phase(ph, later):
                pe.wait_ge(S["merged_in"], 16 * (3 + RS) * (ph + 1))
                if later:
                    pe.wait_ge(S["l3_moved"], 8 * ph)
                n = 0
                for u in range(3):
                    pe.wait_ge(S["k_sorted"], 3 * ph + u + 1)
                    for o4 in range(4):
                        if n >= 2:
                            pe.wait_ge(S["ktr_moved"], 12 * ph + n - 1)
                        for o in range(4):
                            last = nc.tensor.transpose(bank[n % 2][:, o * P:o * P + P], k_perm[:, u, 4 * o4 + o, :], ident[:, :])
                        last.then_inc(S["ktr_done"], 1)
                        n += 1
                n = 0
                for c in range(2):
                    for d4 in range(8):
                        if n >= 2:
                            pe.wait_ge(S["vtr_moved"], 16 * ph + n - 1)
                        for d in range(4):
                            dd = 4 * d4 + d
                            last = nc.tensor.transpose(bank[2 + n % 2][0:KC, d * P:d * P + P],
                                                       v_raw[:, c * KC * HD + dd:(c + 1) * KC * HD:HD], ident[:, :])
                        last.then_inc(S["vtr_done"], 1)
                        n += 1
                pe.wait_ge(S["ktr_moved"], 12 * ph + 12)
                pe.wait_ge(S["vtr_moved"], 16 * ph + 16)

                def finish(i16):
                    r0 = 512 * i16
                    pe.wait_ge(S["o_moved"], 4 * ph + 2 * i16 + 2)
                    for c in range(2):
                        for h in range(GSZ):
                            last = mm(bank[5 + c][:, :], woT[:, h, c * P:c * P + P], oT_ph[:, h, r0:r0 + 512],
                                      start=h == 0, stop=h == GSZ - 1)
                        last.then_inc(S["y_done"], 1)
                    pe.wait_ge(S["y_moved"], 4 * ph + 2 * i16 + 2)
                    for c in range(2):
                        last = mm(bank[5][:, :], aT[:, c, :], xT_ph[:, c, r0:r0 + 512], start=c == 0, stop=c == 1)
                    last.then_inc(S["lo_done"], 1)
                    pe.wait_ge(S["lo_moved"], 2 * ph + i16 + 1)
                    for q in range(4):
                        i = 4 * i16 + q
                        if later or i:
                            pe.wait_ge(S["x3_moved"], 8 * ph + i)
                        rr = slice(r0 + q * P, r0 + q * P + P)
                        for c in range(2):
                            mm(bank[6][:, 0:D], xT_ph[:, c, rr], wT[:, c, :], start=c == 0, stop=False)
                        mm(bank[6][:, 0:D], low[:, q * P:q * P + P], bT[:, :], start=False, stop=True).then_inc(S["x3_done"], 1)
                        pe.wait_ge(S["x3_moved"], 8 * ph + i + 1)
                        pe.wait_ge(S["bd3_ready"], 16 * ph + 2 * i + 2)
                        if later or i:
                            pe.wait_ge(S["l3_moved"], 8 * ph + i)
                        mm(bank[7][:, 0:D], w3_bd[i % 4], x3[i % 2], start=True, stop=True).then_inc(S["l3_done"], 1)

                for step in range(PB + LAG + 1):
                    b = step
                    if b < PB:
                        if b % BPT == 0:
                            pe.wait_ge(S["qbd_ready"], 8 * ph + b // BPT + 1)
                        if b >= 2:
                            pe.wait_ge(S["shifted_done"], 2 * (ph * PB + b - 1))
                        else:
                            if later:
                                pe.wait_ge(S["shifted_done"], 2 * (ph * PB))
                        for j in range(2):
                            last = mm(bank[b % 2][:, 256 * j:256 * j + KEYS],
                                      q_bd[(b // BPT) % 2][:, b % BPT, 2 * j:2 * j + 2, :].rearrange("p g q -> p (g q)"),
                                      kT[:, b, :], start=True, stop=True)
                        last.then_inc(S["s_done"], 1)
                    b = step - LAG
                    if 0 <= b < PB:
                        pe.wait_ge(S["norm_done"], 2 * (ph * PB + b + 1))
                        if b >= 2:
                            pe.wait_ge(S["pt_moved"], ph * PB + b - 1)
                        for c in range(2):
                            for j in range(2):
                                last = nc.tensor.transpose(bank[2 + b % 2][0:KC, (2 * c + j) * P:(2 * c + j + 1) * P],
                                                           normed[b % PR][:, j, c * KC:c * KC + KC], ident[:, :])
                        last.then_inc(S["pt_done"], 1)
                    b = step - LAG - 1
                    if b >= 0:
                        pe.wait_ge(S["pt_moved"], ph * PB + b + 1)
                        if b % 8 == 0:
                            if later or b:
                                pe.wait_ge(S["o_moved"], 4 * ph + b // 8)
                        for c in range(2):
                            for g in range(G):
                                last = mm(bank[4][HD * g:HD * g + HD, (b % 8) * 64:(b % 8) * 64 + 64],
                                          vK[0:KC, c, :, b * G + g], pT[b % 2][0:KC, c * 256 + g * 64:c * 256 + g * 64 + 64],
                                          start=c == 0, stop=c == 1)
                        last.then_inc(S["av_done"], 1)
                        if b % 16 == 15:
                            finish(b // 16)

            phase(0, False)
            with pe.Fori(1, PH) as ph:
                phase(ph, True)

        @block.vector
        def _(dve):
            v = nc.vector
            steps = [0]

            def link(ins):
                ins.then_inc(S["dve_pre"], 1)
                steps[0] += 1
                dve.wait_ge(S["dve_pre"], steps[0])

            dve.wait_ge(S["kv_in"], 16)
            dve.wait_ge(S["pool_const"], 24)
            link(v.tensor_scalar(idx_cols[:, 2:3], kv_col[:, 1:2], T - 1, None, ALU.bitwise_and))
            link(v.tensor_copy(cols[:, 1:2], idx_cols[:, 2:3]))
            for j in range(BPT):
                q = slice(T * j, T * j + T)
                link(v.tensor_scalar(pos_f[q], kv_bc_i[q, 0, j::BPT], cols[q, 1:2], None, ALU.add))
            link(v.tensor_tensor(angle, pos_f[:, :, None].broadcast_to([P, TILES, 16]),
                                 inv_f[:, None, :].broadcast_to([P, TILES, 16]), op=ALU.mult))
            for part, (shift, out_t) in enumerate(((0.0, turn_b), (0.25, turn_c))):
                link(v.tensor_scalar(turn_a, angle, float(1 / (2 * np.pi)), shift, ALU.mult, ALU.add))
                link(v.tensor_scalar(turn_a, turn_a, MAGIC, None, ALU.add))
                link(v.tensor_scalar(turn_a, turn_a, MAGIC, None, ALU.subtract))
                link(v.scalar_tensor_tensor(out_t, turn_a, -TWO_PI_HI, angle, ALU.mult, ALU.add))
                link(v.scalar_tensor_tensor(out_t, turn_a, -TWO_PI_LO, out_t, ALU.mult, ALU.add))
                if part:
                    link(v.tensor_scalar(out_t, out_t, float(np.pi / 2), None, ALU.add))
                v.tensor_scalar(out_t, out_t, -PI, PI, ALU.max, ALU.min).then_inc(S["angles_ready"], 1)

            dve.wait_ge(S["weights_in"], 16 * 8)
            for c in range(2):
                for h in range(GSZ):
                    v.tensor_copy(wo_p[:, c, h, :].rearrange("p (g d) -> p g d", g=G),
                                  wo_n[:, c, :].rearrange("p (g h d) -> p g h d", g=G, h=GSZ)[:, :, h, :]).then_inc(S["wo_sorted"], 1)
            for n, (_, dst, kind) in enumerate(wtr):
                dve.wait_ge(S["wtr_done"], n + 1)
                src = bank[n % 4][:, 0:P]
                if kind == "q":
                    v.tensor_copy(dst, src.rearrange("p (g h d) -> p g h d", g=2, h=2)).then_inc(S["wtr_moved"], 1)
                elif kind == "i":
                    v.tensor_tensor(dst, src, ident[:, :], op=ALU.add).then_inc(S["wtr_moved"], 1)
                else:
                    v.tensor_copy(dst, src).then_inc(S["wtr_moved"], 1)
            dve.wait_ge(S["wtr_done"], NWT + 1)
            link(v.tensor_copy(b3_all[:, :], bank[6][:, 0:TILES]))
            dve.wait_ge(S["const_in"], 16 * (NAD + 3))
            for h0, n in ((0, H), (H, G)):
                link(v.tensor_scalar(gain[:, h0, :], gain[:, h0, :], 1.0, None, ALU.add))
                link(v.tensor_copy(gain[:, h0 + 1:h0 + n, :], gain[:, h0:h0 + 1, :].broadcast_to([P, n - 1, HD])))
            link(v.tensor_scalar(idx_cols[:, 3:4], kv_col[:, 1:2], 4, None, ALU.logical_shift_right))
            link(v.tensor_copy(cols[:, 2:3], idx_cols[:, 3:4]))
            link(v.tensor_scalar(adapt[:, :], n_idx_bc[:, :], cols[:, 2:3], cols[:, 0:1], ALU.is_equal, ALU.mult))

            dve.wait_ge(S["table_in"], 32)
            link(v.tensor_copy(table[:, 0:NBLK], table_i[:, :]))
            kc = lambda n: kv_col[:, n:n + 1]
            link(v.tensor_scalar(kc(2), kc(0), BLK - 1, None, ALU.bitwise_and))
            link(v.tensor_scalar(kc(3), kc(0), 4, None, ALU.logical_shift_right))
            link(v.tensor_scalar(kc(4), kc(0), -(WINDOW - 1.0), 0.0, ALU.add, ALU.max))
            link(v.tensor_scalar(kc(5), kc(4), 4, None, ALU.logical_shift_right))
            link(v.tensor_copy(cols[:, 3:4], kc(2)))
            link(v.tensor_copy(cols[:, 4:5], kc(3)))
            link(v.tensor_copy(cols[:, 5:6], kc(5)))
            link(v.tensor_scalar(hot_r, iota_row, cols[:, 5:6], None, ALU.is_equal))
            link(v.tensor_scalar(hot_w, iota_row, cols[:, 4:5], None, ALU.is_equal))
            for r in range(RSP):
                link(v.tensor_tensor_reduce(out=scrap[:, 0:NBLK], in0=table[:, r:r + NBLK], in1=hot_r, scale=1.0, scalar=0.0,
                                            op0=ALU.mult, op1=ALU.add, accum_out=read_blk[:, r:r + 1]))
            for j in range(WS):
                link(v.tensor_tensor_reduce(out=scrap[:, 0:NBLK], in0=table[:, j:j + NBLK], in1=hot_w, scale=1.0, scalar=0.0,
                                            op0=ALU.mult, op1=ALU.add, accum_out=wblk[:, j:j + 1]))
            link(v.tensor_copy(w_idx[:, :], wblk))
            link(v.tensor_scalar(cols[:, 6:7], cols[:, 3:4], 0.5, None, ALU.is_gt))
            link(v.tensor_copy(wkey[:, 0:2], wblk[:, 0:2]))
            link(v.tensor_scalar(wkey[:, 2:3], wblk[:, 2:3], 1.0, cols[:, 6:7], ALU.add, ALU.mult))
            v.tensor_scalar(wkey[:, 2:3], wkey[:, 2:3], -1.0, None, ALU.add).then_inc(S["dve_tab"], 1)
            link(v.tensor_scalar(kv_bc_i[:, 1, :], kv_bc_i[:, 0, :], -(WINDOW - 1.0), 0.0, ALU.add, ALU.max))
            link(v.tensor_scalar(kv_bc_i[:, 1, :], kv_bc_i[:, 1, :], 4, 4, ALU.logical_shift_right, ALU.logical_shift_left))
            link(v.tensor_tensor(tmp_bc, kv_bc_i[:, 1, :], kv_bc_i[:, 0, :], op=ALU.subtract))
            link(v.tensor_scalar(mask_at[:, :], tmp_bc[0:1, :], float(OFFS), None, ALU.add))
            link(v.tensor_scalar(kv_bc_i[:, 1, :], kv_bc_i[:, 0, :], BLK - 1, None, ALU.bitwise_and))
            link(v.tensor_copy(m_bc, kv_bc_i[:, 1, :]))
            link(v.tensor_tensor(value_bc.rearrange("p (b j) -> p b j", j=WS), value_bc.rearrange("p (b j) -> p b j", j=WS),
                                 m_bc[:, :, None].broadcast_to([P, B, WS]), op=ALU.subtract))
            cov = cover.rearrange("p o (b j) -> p o b j", j=WS)
            io = off_io[:, 0:BLK, None].broadcast_to([P, BLK, B])
            mb = m_bc[:, None, :].broadcast_to([P, BLK, B])
            link(v.tensor_tensor(cov[:, :, :, 0], io, mb, op=ALU.is_ge))
            link(v.memset(cov[:, :, :, 1], 1.0))
            link(v.tensor_tensor(cov[:, :, :, 2], io, mb, op=ALU.is_lt))
            dve.wait_ge(S["keys_back"], 16)
            for j in range(WS):
                link(v.scalar_tensor_tensor(match[:, j, :], wkey_bc, wblk[:, j:j + 1], value_bc, ALU.is_equal, ALU.mult))
                for o in range(BLK):
                    link(v.tensor_tensor_reduce(out=owner_o, in0=match[:, j, :], in1=cover[:, o, :], scale=1.0, scalar=0.0,
                                                op0=ALU.mult, op1=ALU.max, accum_out=own_max[:, j * BLK + o:j * BLK + o + 1]))
            link(v.tensor_scalar(own_any[:, :], own_max, 0.5, None, ALU.is_gt))
            link(v.tensor_scalar(own_none, own_max, 0.5, float(BIG), ALU.is_lt, ALU.mult))
            link(v.tensor_tensor(own_f, own_max, off_io, op=ALU.add))
            link(v.tensor_scalar(own_f, own_f, -64.0, 0.0, ALU.add, ALU.max))
            v.tensor_tensor(own_idx[:, :], own_f, own_none, op=ALU.add).then_inc(S["own_known"], 1)
            v.memset(arena[:, 0:12288], 0.0).then_inc(S["new_zero"], 1)

            def tile_pair(it, later):
                for s in range(2):
                    i6 = 12 * it + 6 * s
                    if later:
                        dve.wait_ge(S["rows_ready"], 2 * it)
                    ps = bank[2 + s]
                    heads = lambda t: t.rearrange("p (h d) -> p h d", d=HD)
                    dve.wait_ge(S["sq_done"], 2 * it + s + 1)
                    v.reduce_sum(ssum[s], heads(sq[s]), axis=AX.X).then_inc(S["ms_done"], 1)
                    dve.wait_ge(S["sqrt_done"], 2 * it + s + 1)
                    v.reciprocal(rstd[s], rtmp[s]).then_inc(S["dve_a"], 1)
                    dve.wait_ge(S["dve_a"], i6 + 1)
                    v.tensor_tensor(heads(nrm[s]), heads(ps[:, 0:QK]), rstd[s][:, :, None].broadcast_to([P, H + G, HD]),
                                    op=ALU.mult).then_inc(S["dve_a"], 1)
                    dve.wait_ge(S["dve_a"], i6 + 2)
                    v.tensor_tensor(heads(gained[s]), heads(nrm[s]), gain[:, :, :], op=ALU.mult).then_inc(S["dve_a"], 1)
                    dve.wait_ge(S["dve_a"], i6 + 3)
                    at = bass.ds(it * 2 + s, 1)
                    v.tensor_tensor(heads(rot_c[s]), heads(gained[s]), cos2[:, at, :].broadcast_to([P, H + G, HD]),
                                    op=ALU.mult).then_inc(S["dve_a"], 1)
                    for half in range(2):
                        o, n = half * 16, 16 - half * 16
                        v.tensor_tensor(heads(rot_s[s])[:, :, o:o + 16], heads(gained[s])[:, :, n:n + 16],
                                        sin2[:, at, o:o + 16].broadcast_to([P, H + G, 16]), op=ALU.mult).then_inc(S["dve_a"], 1)
                    dve.wait_ge(S["dve_a"], i6 + 6)
                    if later:
                        dve.wait_ge(S[f"rows_out{s}"], 16 * it)
                    if later:
                        dve.wait_ge(S["qtr_done"], 2 * it)
                    v.tensor_tensor(qkv_o[s][:, 0:QK], rot_c[s], rot_s[s], op=ALU.add).then_inc(S["rows_ready"], 1)

            tile_pair(0, False)
            with dve.Fori(1, TILES // 2) as it:
                tile_pair(it, True)

            for r in range(RSP):
                link(v.scalar_tensor_tensor(scrap, wkey_bc, read_blk[:, r:r + 1], order_bc, ALU.is_equal, ALU.mult))
                link(v.tensor_reduce(read_w[:, r:r + 1], scrap, axis=AX.X, op=ALU.max))
            link(v.tensor_scalar(r_hit, read_w, 0.5, None, ALU.is_gt))
            link(v.scalar_tensor_tensor(r_a, r_hit, float(BIG), read_blk, ALU.mult, ALU.add))
            link(v.tensor_scalar(r_hit, read_w, 0.5, float(BIG), ALU.is_lt, ALU.mult))
            link(v.scalar_tensor_tensor(r_b, read_w, -1.0, r_hit, ALU.add, ALU.add))
            for n, t in enumerate((r_a, r_b)):
                link(v.tensor_copy(r_int[:, RSP * n:RSP * n + RSP].rearrange("p (q u) -> p q u", u=3),
                                   t.rearrange("p (u q) -> p q u", u=3)))
                for g in range(G):
                    link(v.tensor_scalar(r_int[:, 24 + 48 * n + RSP * g:24 + 48 * n + RSP * g + RSP], t, float(G), float(g),
                                         ALU.mult, ALU.add))
            v.engine_nop().then_inc(S["dve_tab"], 1)

            dve.wait_ge(S["blk_in"], 16 * 6)
            dve.wait_ge(S["rows_in"], 16 * WS * BLK)
            for kv, blk in enumerate((blk_k, blk_v)):
                for j in range(WS):
                    out = blk[:, j, :].rearrange("p (g o d) -> p g o d", g=G, o=BLK)
                    data = row_new[:, j * BLK:(j + 1) * BLK, kv * KV:(kv + 1) * KV].rearrange("p o (g d) -> p g o d", g=G)
                    for g in range(G):
                        link(v.copy_predicated(out[:, g], own_any[:, j * BLK:(j + 1) * BLK, None].broadcast_to([P, BLK, HD]), data[:, g]))
                v.engine_nop().then_inc(S["merged_done"], 1)

            def phase(ph, later):
                def expand(q4):
                    if q4 >= 2:
                        dve.wait_ge(S["s_done"], ph * PB + BPT * (q4 - 1))
                    for g in range(G):
                        last = v.tensor_scalar(
                            q_bd[q4 % 2][:, :, g, :].rearrange("p b (h t) -> p b h t", h=GSZ),
                            qT_ph[:, :, P * q4:P * q4 + P].rearrange("p h (b t) -> p b h t", b=BPT),
                            head_scale[:, g:g + 1], None, ALU.mult)
                    last.then_inc(S["qbd_ready"], 1)
                dve.wait_ge(S["ph_in"], 32 * (ph + 1))
                if later:
                    dve.wait_ge(S["s_done"], ph * PB)
                expand(0)
                dve.wait_ge(S["merged_in"], 16 * (3 + RS) * (ph + 1))
                if later:
                    dve.wait_ge(S["av_done"], ph * PB)
                for u in range(3):
                    v.tensor_copy(k_perm[:, u].rearrange("p o (g d) -> p o g d", g=G),
                                  k_raw[:, u].rearrange("p g o d -> p o g d")).then_inc(S["k_sorted"], 1)
                n = 0
                for u in range(3):
                    for o4 in range(4):
                        q = 4 if u < 2 else 3
                        dve.wait_ge(S["ktr_done"], 12 * ph + n + 1)
                        v.tensor_copy(
                            kT[:, :, u * 64:u * 64 + 16 * q].rearrange("p b (r o) -> p b r o", o=BLK)[:, :, :, 4 * o4:4 * o4 + 4],
                            bank[n % 2][:, :].rearrange("p (o b r) -> p b r o", o=4, r=4)[:, :, 0:q, :]).then_inc(S["ktr_moved"], 1)
                        n += 1
                for step in range(PB + LAG + 2):
                    b = step
                    if b < PB:
                        if b % BPT == 1 and b // BPT + 1 < PB // BPT:
                            expand(b // BPT + 1)
                        dve.wait_ge(S["s_done"], ph * PB + b + 1)
                        dve.wait_ge(S["mask_ready"], ph * PB + b + 1)
                        if b >= 3:
                            dve.wait_ge(S["exp_done"], 2 * (ph * PB + b - 2))
                        else:
                            if later:
                                dve.wait_ge(S["exp_done"], 2 * (ph * PB))
                        hold(dve)
                        for j in range(2):
                            v.tensor_tensor_reduce(out=shifted[b % 3][:, j, :], in0=bank[b % 2][:, 256 * j:256 * j + KEYS],
                                                   in1=masks[b % 8], scale=-1.0, scalar=3.0e38, op0=ALU.add, op1=ALU.min,
                                                   accum_out=neg_max[:, 2 * b + j:2 * b + j + 1]).then_inc(S["shifted_done"], 1)
                    b = step - 1
                    if 0 <= b < PB:
                        dve.wait_ge(S["exp_done"], 2 * (ph * PB + b + 1))
                        v.reciprocal(p_inv[:, 2 * b:2 * b + 2], p_sum[:, 2 * b:2 * b + 2]).then_inc(S["inv_done"], 1)
                    b = step - LAG
                    if 0 <= b < PB and b % 2 == 0:
                        dve.wait_ge(S["pt_done"], ph * PB + b + 1)
                        if later or b > 1:
                            dve.wait_ge(S["av_done"], (ph * PB + b - 1) if b >= 2 else ph * PB)
                        if later or b:
                            dve.wait_ge(S["pt_moved"], ph * PB + b)
                        v.tensor_copy(pT[b % 2][0:KC, :], bank[2 + b % 2][0:KC, :]).then_inc(S["pt_moved"], 1)
                    b = step - LAG - 1
                    if b >= 0 and b % 8 == 7:
                        i8 = b // 8
                        dve.wait_ge(S["av_done"], ph * PB + b + 1)
                        if i8 == 0:
                            if later:
                                dve.wait_ge(S["y_done"], 4 * ph)
                        v.tensor_copy(oT_ph[:, :, 256 * i8:256 * i8 + 256].rearrange("p h (b t) -> p b h t", b=8),
                                      bank[4][:, :].rearrange("p (b h t) -> p b h t", b=8, h=GSZ)).then_inc(S["o_moved"], 1)
                    if b >= 0 and b % 16 == 15:
                        i16 = b // 16
                        r0 = 512 * i16
                        for c in range(2):
                            dve.wait_ge(S["y_done"], 4 * ph + 2 * i16 + c + 1)
                            v.tensor_tensor(xT_ph[:, c, r0:r0 + 512], bank[5 + c][:, :], xT_ph[:, c, r0:r0 + 512],
                                            op=ALU.add).then_inc(S["y_moved"], 1)
                        dve.wait_ge(S["lo_done"], 2 * ph + i16 + 1)
                        if later or i16:
                            dve.wait_ge(S["x3_done"], 8 * ph + 4 * i16)
                        v.tensor_tensor(low[:, :].rearrange("p (b t) -> p b t", t=T),
                                        bank[5][:, :].rearrange("p (b t) -> p b t", t=T),
                                        adapt[:, bass.ds(ph * PB + 16 * i16, 16)][:, :, None].broadcast_to([P, 16, T]),
                                        op=ALU.mult).then_inc(S["lo_moved"], 1)

            phase(0, False)
            with dve.Fori(1, PH) as ph:
                phase(ph, True)

        @block.scalar
        def _(act):
            s_ = nc.scalar
            act.wait_ge(S["angles_ready"], 2)
            s_.activation(sin2[:, :, 0:16], turn_b, ACT.Sin, scale=-1.0).then_inc(S["act_pre"], 1)
            s_.activation(sin2[:, :, 16:32], turn_b, ACT.Sin).then_inc(S["act_pre"], 1)
            for half in range(2):
                s_.activation(cos2[:, :, 16 * half:16 * half + 16], turn_c, ACT.Sin).then_inc(S["act_pre"], 1)
            def tile_pair(it, later):
                for s in range(2):
                    act.wait_ge(S["l0_done"], 2 * it + s + 1)
                    if later:
                        act.wait_ge(S["qkv_done"], 2 * it)
                    if later:
                        act.wait_ge(S[f"x1_out{s}"], 16 * it)
                    s_.activation(x1t[s], bank[s][:, 0:D].rearrange("p (c r) -> p c r", c=2), ACT.Copy).then_inc(S["x1_ready"], 1)
                for s in range(2):
                    act.wait_ge(S["qkv_done"], 2 * it + s + 1)
                    if later:
                        act.wait_ge(S["ms_done"], 2 * it)
                    s_.activation(sq[s], bank[2 + s][:, 0:QK], ACT.Square).then_inc(S["sq_done"], 1)
                    if later:
                        act.wait_ge(S[f"rows_out{s}"], 16 * it)
                    s_.activation(qkv_o[s][:, QK:512], bank[2 + s][:, QK:512], ACT.Copy).then_inc(S["v_copied"], 1)
                    act.wait_ge(S["ms_done"], 2 * it + s + 1)
                    if later:
                        act.wait_ge(S["dve_a"], 12 * it)
                    s_.activation(rtmp[s], ssum[s], ACT.Sqrt, scale=1.0 / HD, bias=eps_t[:, 0:1]).then_inc(S["sqrt_done"], 1)
                for s in range(2):
                    act.wait_ge(S["qtr_done"], 2 * it + s + 1)
                    if later:
                        act.wait_ge(S[f"qt_out{s}"], 16 * it)
                    s_.activation(qt[s], bank[4 + s][:, 0:D].rearrange("p (h r) -> p h r", h=GSZ), ACT.Copy).then_inc(S["qt_ready"], 1)

            tile_pair(0, False)
            with act.Fori(1, TILES // 2) as it:
                tile_pair(it, True)
            def phase(ph, later):
                n = 0
                for c in range(2):
                    for d4 in range(8):
                        act.wait_ge(S["vtr_done"], 16 * ph + n + 1)
                        s_.activation(vK[0:KC, c, 4 * d4:4 * d4 + 4, :].rearrange("p d n -> p (d n)"), bank[2 + n % 2][0:KC, :],
                                      ACT.Copy).then_inc(S["vtr_moved"], 1)
                        n += 1
                for step in range(PB + LAG + 2):
                    b = step
                    if b < PB:
                        if b >= PR:
                            act.wait_ge(S["norm_done"], 2 * (ph * PB + b - PR + 1))
                        for j in range(2):
                            act.wait_ge(S["shifted_done"], 2 * (ph * PB + b) + j + 1)
                            s_.activation(probs[b % PR][:, j, :], shifted[b % 3][:, j, :], ACT.Exp, scale=-1.0,
                                          bias=neg_max[:, 2 * b + j:2 * b + j + 1],
                                          accum_out=p_sum[:, 2 * b + j:2 * b + j + 1]).then_inc(S["exp_done"], 1)
                    b = step - LAG
                    if 0 <= b < PB and b % 2 == 1:
                        act.wait_ge(S["pt_done"], ph * PB + b + 1)
                        if later or b > 1:
                            act.wait_ge(S["av_done"], (ph * PB + b - 1) if b >= 2 else ph * PB)
                        if later or b:
                            act.wait_ge(S["pt_moved"], ph * PB + b)
                        s_.activation(pT[b % 2][0:KC, :], bank[2 + b % 2][0:KC, :], ACT.Copy).then_inc(S["pt_moved"], 1)
                    b = step - LAG - 1
                    if b >= 0 and b % 16 == 15:
                        for q in range(4):
                            i = 4 * (b // 16) + q
                            act.wait_ge(S["x3_done"], 8 * ph + i + 1)
                            if later or i:
                                act.wait_ge(S["l3_done"], 8 * ph + i)
                            s_.activation(x3[i % 2], bank[6][:, 0:D], ACT.Copy).then_inc(S["x3_moved"], 1)
                            act.wait_ge(S["l3_done"], 8 * ph + i + 1)
                            if later or i > 1:
                                act.wait_ge(S[f"out_done{i % 2}"], 16 * 4 * ph + 16 * (i // 2))
                            s_.activation(o_t[i % 2], bank[7][:, 0:D], ACT.Identity,
                                          bias=b3_all[:, bass.ds(ph * 8 + i, 1)]).then_inc(S["l3_moved"], 1)

            phase(0, False)
            with act.Fori(1, PH) as ph:
                phase(ph, True)


_INS = ["x", "itok_B_1_198", "itok_Bx257_0_4111", "itok_B_37_3939", "itok_B_0_6", "itok_B_0_7", "fside_8xS_0",
        "L0_cond_weights", "L1_cond_Wq", "L1_cond_Wk", "L1_cond_Wv", "L1_cond_Wo", "L1_cond_q_norm_scale",
        "L1_cond_k_norm_scale", "L1_cond_k_blocks", "L1_cond_v_blocks", "L2_cond_W", "L2_cond_A", "L2_cond_Bm",
        "L2_cond_scalings", "L3_cond_weights"]


def kernel(**inputs):
    import numpy as _np
    import concourse.bacc as _bacc
    from concourse import mybir as _mybir
    from concourse.bass_utils import run_bass_kernel_spmd as _run

    nc = _bacc.Bacc("TRN2", target_bir_lowering=False, num_devices=1)
    arrays, aps = {}, {}
    for name in _INS:
        arr = _np.ascontiguousarray(inputs[name])
        arrays[f"in_{name}"] = arr
        aps[name] = nc.dram_tensor(f"in_{name}", arr.shape, _mybir.dt.from_np(arr.dtype), kind="ExternalInput").ap()
    aps["out"] = nc.dram_tensor("out", (B, T, D), _mybir.dt.float32, kind="ExternalOutput").ap()
    build(nc, aps)
    r = _run(nc, [arrays], core_ids=[0])
    return r.results[0]["out"]
```

```python
import numpy as np
import concourse.bass as bass
from concourse import mybir
from contextlib import ExitStack

F32 = mybir.dt.float32
I32 = mybir.dt.int32
ALU = mybir.AluOpType
ACT = mybir.ActivationFunctionType
AX = mybir.AxisListType

P = 128
B, T, D = 128, 32, 256
ROWS = B * T
BPT = P // T
TILES = ROWS // P
G, GSZ, HD = 4, 2, 32
H = G * GSZ
QK = (H + G) * HD
KV = G * HD
BLK = 16
NBLK = 257
CACHE = 4112
WINDOW = 128
SCALE = 256.0 ** -0.5
EPS = 1e-6
THETA = 10000.0
ROW_G = BLK * HD
ROW_B = G * ROW_G
WS = 3
NW = B * WS
RS = 11
RSP = 12
KEYS = RS * BLK
KC = KEYS // 2
PH = 4
PB = B // PH
PROWS = PB * T
UROWS = PROWS // 2
OFFS = WINDOW + BLK - 2
BIG = 1 << 20
NEG = -1.0e30
RANK = 16
NAD = P // RANK
TP = NBLK + 15
LAG = 3
STEPS = PB + LAG + 1
UNIT_AT = PB // 2 + LAG + 2
PIECES = {0: ("y", 0), 1: ("y", 1), 3: ("lo", 0)}
for _q in range(4):
    PIECES[4 + 2 * _q] = ("x3", _q)
    PIECES[5 + 2 * _q] = ("l3", _q)
TWO_PI_HI = 6.28125
TWO_PI_LO = float(2 * np.pi - 6.28125)
MAGIC = 12582912.0
PI = float(np.float32(3.1415925))
INV_FREQ = (np.float32(1.0) / np.float32(THETA) ** (np.arange(HD // 2, dtype=np.float32) / np.float32(HD // 2))).astype(np.float32)


def build(nc, a, dbg=None):
    ctx = ExitStack()
    with ctx:
        def sb(name, shape, dt=F32):
            return ctx.enter_context(nc.sbuf_tensor(name, shape, dt))

        def sem(name):
            return ctx.enter_context(nc.semaphore(name))

        def dram(name, shape, dt=F32):
            return nc.dram_tensor(name, shape, dt, kind="Internal").ap()

        x_rows = a["x"].rearrange("b t d -> (b t) d")
        out_rows = a["out"].rearrange("b t d -> (b t) d")
        k_by_block = a["L1_cond_k_blocks"].rearrange("n g o d -> n (g o d)")
        v_by_head = a["L1_cond_v_blocks"].rearrange("n g o d -> (n g) (o d)")
        v_by_block = a["L1_cond_v_blocks"].rearrange("n g o d -> n (g o d)")
        w0_by_b = dram("w0_by_b", [B, T * T])
        w3_by_b = dram("w3_by_b", [B, T * T])
        b3_by_b = dram("b3_by_b", [B, T])
        writer_keys = dram("writer_keys", [NW])
        new_rows = dram("new_rows", [ROWS, 2 * KV])
        x1_T = dram("x1_T", [2, P, ROWS])
        q_T = dram("q_T", [GSZ, P, ROWS])
        merged_k = dram("merged_k", [NW, ROW_B])
        merged_v = dram("merged_v", [NW, ROW_B])
        merged_v_by_head = merged_v.rearrange("n (g e) -> (n g) e", g=G)
        k_slots = dram("k_slots", [2, B * RSP], I32)
        v_slots = dram("v_slots", [2, B * G * RSP], I32)

        ident = sb("ident", [P, P])
        wqkv = sb("wqkv", [P, 2, 512])
        woT = sb("woT", [P, GSZ, D])
        wT = sb("wT", [P, 2, D])
        aT = sb("aT", [P, 2, P])
        bT = sb("bT", [P, D])
        same_b = sb("same_b", [P, BPT])
        head_scale = sb("head_scale", [P, G])
        adapt = sb("adapt", [P, B])
        w0_all = sb("w0_all", [P, TILES, T])
        w3_all = sb("w3_all", [P, TILES, T])
        b3_all = sb("b3_all", [P, TILES])
        b3_nat = sb("b3_nat", [TILES, P])
        tables = sb("tables", [P, 2, TILES, HD])
        cos2, sin2 = tables[:, 0], tables[:, 1]
        k_perm = tables[:, :, :, :].rearrange("p a i d -> p (a i d)").rearrange("p (o e) -> p o e", o=BLK)
        gain = sb("gain", [P, H + G, HD])
        mask_wide = sb("mask_wide", [P, KEYS + OFFS])
        mask_at = sb("mask_at", [1, B], I32)
        eps_t = sb("eps_t", [P, 1])
        slot_idx = sb("slot_idx", [P, PH, 2 * 3 + 2 * RSP], I32)
        slot_now = sb("slot_now", [P, 2 * 3 + 2 * RSP], I32)
        kv_col = sb("kv_col", [P, 8], I32)
        cols = sb("cols", [P, 16])
        own_idx = sb("own_idx", [P, WS * BLK], I32)
        own_any = sb("own_any", [P, WS * BLK], I32)
        w_idx = sb("w_idx", [P, WS], I32)
        idx_cols = sb("idx_cols", [P, 4], I32)

        arena = sb("arena", [P, 25600])
        row_new = arena[:, 0:12288].rearrange("p (s e) -> p s e", s=WS * BLK)
        blk_k = arena[:, 12288:18432].rearrange("p (j e) -> p j e", j=WS)
        blk_v = arena[:, 18432:24576].rearrange("p (j e) -> p j e", j=WS)
        cover = arena[:, 0:6144].rearrange("p (o w) -> p o w", o=BLK)
        match = arena[:, 6144:10752].rearrange("p (r w) -> p r w", r=RSP)
        owner_o = arena[:, 10752:11136]
        match2 = arena[:, 0:4608].rearrange("p (r w) -> p r w", r=RSP)
        k_raw = arena[:, 0:6144].rearrange("p (u g o d) -> p u g o d", u=3, g=G, o=BLK)
        v_raw = arena[:, 6144:11776]
        kT = arena[:, 11776:17408].rearrange("p (b k) -> p b k", b=PB)
        vK = arena[:, 17408:25600].rearrange("p (c d n) -> p c d n", c=2, d=HD)
        stage = arena[:, 12288:17408]
        wq_n = stage[:, 0:512].rearrange("p (c n) -> p c n", c=2)
        wk_n = stage[:, 512:768]
        wv_n = stage[:, 768:1024]
        wo_n = stage[:, 1024:1536].rearrange("p (c n) -> p c n", c=2)
        w_n = stage[:, 1536:2048].rearrange("p (c n) -> p c n", c=2)
        a_n = stage[:, 2048:2304]
        wo_p = stage[:, 2560:3072].rearrange("p (c h n) -> p c h n", c=2, h=GSZ)
        bm_n = stage[:, 2304:2560].rearrange("p (c n r) -> p c n r", c=2, n=NAD)
        small = sb("small", [P, 3264])
        table = small[:, 0:TP]
        hot_r = small[:, 272:272 + NBLK]
        hot_w = small[:, 544:544 + NBLK]
        iota_row = small[:, 816:816 + NBLK]
        wkey_bc = small[:, 1088:1088 + NW]
        value_bc = small[:, 1472:1472 + NW]
        order_bc = small[:, 1856:1856 + NW]
        m_bc = small[:, 2240:2240 + B]
        tmp_bc = small[:, 2368:2368 + B]
        read_blk = small[:, 2496:2496 + RSP]
        read_w = small[:, 2512:2512 + RSP]
        wblk = small[:, 2528:2528 + WS]
        wkey = small[:, 2532:2532 + WS]
        own_max = small[:, 2544:2592]
        own_none = small[:, 2592:2640]
        off_io = small[:, 2640:2688]
        own_f = small[:, 2688:2736]
        r_hit = small[:, 2736:2748]
        r_a = small[:, 2752:2764]
        r_b = small[:, 2768:2780]
        r_ag = small[:, 2784:2832]
        r_bg = small[:, 2832:2880]
        scrap = small[:, 2880:2880 + NW]
        table_i = sb("table_i", [P, NBLK], I32)
        kv_bc_i = sb("kv_bc_i", [P, 2, B], I32)
        r_int = sb("r_int", [P, 2 * RSP + 2 * G * RSP], I32)
        n_idx_bc = sb("n_idx_bc", [P, B], I32)

        ring = sb("ring", [P, 8032])
        def cut(at, n):
            return ring[:, at:at + n]
        PAIR = 2 * P
        xt = [cut(512 * s, 512).rearrange("p (i d) -> p i d", i=2) for s in range(2)]
        w0_bd = [cut(1024 + 256 * s, 256).rearrange("p (i n) -> p i n", i=2) for s in range(2)]
        x1t = [cut(1536 + 512 * s, 512).rearrange("p (c r) -> p c r", c=2) for s in range(2)]
        sq = [cut(2560 + 512 * s, 512) for s in range(2)]
        nrm, gained, rot_c, rot_s = (cut(3584 + 512 * n, 512) for n in range(4))
        kv_o = [cut(5632 + 512 * s, 512).rearrange("p (i n) -> p i n", i=2) for s in range(2)]
        q_o = kv_o
        qt = [cut(6656 + 512 * s, 512).rearrange("p (h r) -> p h r", h=GSZ) for s in range(2)]
        ssum = [cut(7680 + 16 * s, 16) for s in range(2)]
        rstd = [cut(7712 + 16 * s, 16) for s in range(2)]
        rtmp = [cut(7744 + 16 * s, 16) for s in range(2)]
        angle = arena[:, 0:512].rearrange("p (i f) -> p i f", i=TILES)
        turn_a = arena[:, 512:1024].rearrange("p (i f) -> p i f", i=TILES)
        turn_b = arena[:, 1024:1536].rearrange("p (i f) -> p i f", i=TILES)
        turn_c = arena[:, 1536:2048].rearrange("p (i f) -> p i f", i=TILES)
        pos_f = arena[:, 2048:2080]
        inv_f = arena[:, 2080:2096]
        gathered = arena[:, 22528:24576].rearrange("p (a e) -> p a e", a=2)
        gathered_b = arena[:, 24576:24608]
        SR, PR = 2, 4
        shifted = [cut(352 * s, 352).rearrange("p (j k) -> p j k", j=2) for s in range(3)]
        probs = [cut(1056 + 352 * s, 352).rearrange("p (j k) -> p j k", j=2) for s in range(PR)]
        normed = [cut(2464 + 352 * s, 352).rearrange("p (j k) -> p j k", j=2) for s in range(PR)]
        pT = [cut(3872 + 512 * s, 512) for s in range(2)]
        masks = [cut(4896 + KEYS * s, KEYS) for s in range(8)]
        x3 = [cut(6304 + 256 * s, 256) for s in range(2)]
        o_t = [cut(6816 + 256 * s, 256) for s in range(2)]
        w3_bd = [cut(7328 + 128 * s, 128) for s in range(4)]
        neg_max = cut(7840, 64)
        p_sum = cut(7904, 64)
        p_inv = cut(7968, 64)
        q_bd = [sb(f"q_bd{s}", [P, BPT, G, GSZ * T]) for s in range(2)]
        qT_ph = sb("qT_ph", [P, GSZ, PROWS])
        xT_ph = sb("xT_ph", [P, 2, PROWS])
        oT_ph = small[:, 0:GSZ * PROWS].rearrange("p (h r) -> p h r", h=GSZ)
        low = small[:, GSZ * PROWS:GSZ * PROWS + 512]

        bank = [ctx.enter_context(nc.psum_tensor(f"bank{i}", [P, 512], F32)) for i in range(8)]

        names = """weights_in const_in table_in kv_in wgath wgath_out wgath_back pre2 pool_const pool_step held
            wtr_done wtr_moved wo_sorted dve_pre angles_ready act_pre dve_tab keys_out keys_back
            xt_in0 xt_in1 bd0_ready l0_done x1_ready x1_out0 x1_out1 kv_done sq_done ms_done sqrt_done v_copied dve_a
            rows_ready rows_out0 rows_out1 x1_in0 x1_in1 q_done qsq_done qms_done qsqrt_done dve_q q_ready qtr_done
            qt_ready qt_out0 qt_out1 own_known new_zero blk_in rows_in merged_done merged_out slots_out slots_back
            q_in0 q_in1 x1_unit0 x1_unit1 orig_in merged_in slots_now k_sorted ktr_done ktr_moved vtr_done vtr_moved qbd_ready mask_ready
            s_done shifted_done exp_done inv_done norm_done pt_done pt_moved av_done o_moved y_done y_moved
            lo_done lo_moved x3_done x3_moved bd3_ready l3_done l3_moved out_done0 out_done1""".split()
        S = {n: sem(n) for n in names}

        block = ctx.enter_context(nc.Block())

        PAIRS = TILES // 2
        SPLIT = PAIRS - 4

        def rounds(eng, do, last, between=None):
            def static(r):
                do(r, r % 4, lambda lo, hi=99: lo <= r < hi)
            for r in range(4):
                static(r)
            with eng.Fori(1, SPLIT // 4) as turn:
                for s in range(4):
                    do(4 * turn + s, s, lambda lo, hi=99: True)
            if between:
                between()
            for r in range(SPLIT, last):
                static(r)

        def phases(eng, do):
            do(0, False, True)
            with eng.Fori(1, PH - 1) as ph:
                do(ph, True, True)
            do(PH - 1, True, False)

        def hold(eng):
            eng.sem_inc(S["held"], 1)

        @block.sync
        def _(sp):
            for dst, src in ((table_i[:, :], a["itok_Bx257_0_4111"]),
                             (kv_col[:, 0:1], a["itok_B_37_3939"].rearrange("(b o) -> b o", o=1))):
                sp.dma_start(dst, src).then_inc(S["table_in"], 16)
            lens = a["itok_B_37_3939"].rearrange("(o b) -> o b", o=1)
            sp.dma_start(kv_bc_i[:, 0, :], lens.broadcast_to([P, B])).then_inc(S["kv_in"], 16)
            for dst, src in ((wq_n, a["L1_cond_Wq"].rearrange("(c p) d -> p c d", p=P)),
                             (wk_n, a["L1_cond_Wk"]), (wv_n, a["L1_cond_Wv"]),
                             (wo_n, a["L1_cond_Wo"].rearrange("(c p) d -> p c d", p=P)),
                             (w_n, a["L2_cond_W"].rearrange("(c p) d -> p c d", p=P)),
                             (a_n, a["L2_cond_A"].rearrange("n r d -> (n r) d")),
                             (bm_n[:, 0], a["L2_cond_Bm"].rearrange("n (c p) r -> c p n r", p=P)[0]),
                             (bm_n[:, 1], a["L2_cond_Bm"].rearrange("n (c p) r -> c p n r", p=P)[1])):
                sp.dma_start(dst, src).then_inc(S["weights_in"], 16)
            ones = lambda n: a[n].rearrange("(o d) -> o d", o=1)
            for n in range(NAD):
                sp.dma_start(cols[RANK * n:RANK * n + RANK, 0:1], ones("L2_cond_scalings")[:, n:n + 1].broadcast_to([RANK, 1])
                             ).then_inc(S["const_in"], 16)
            sp.dma_start(gain[:, 0, :], ones("L1_cond_q_norm_scale").broadcast_to([P, HD])).then_inc(S["const_in"], 16)
            sp.dma_start(gain[:, H, :], ones("L1_cond_k_norm_scale").broadcast_to([P, HD])).then_inc(S["const_in"], 16)
            sp.dma_start(n_idx_bc[:, :], ones("itok_B_0_6").broadcast_to([P, B])).then_inc(S["const_in"], 16)
            sp.wait_ge(S["wgath"], 48)
            sp.dma_start(w0_by_b, gathered[:, 0, :]).then_inc(S["wgath_out"], 16)
            sp.dma_start(w3_by_b, gathered[:, 1, :]).then_inc(S["wgath_out"], 16)
            sp.dma_start(b3_by_b, gathered_b).then_inc(S["wgath_out"], 16)
            sp.wait_ge(S["wgath_out"], 48)
            for dst, src in ((w0_all, w0_by_b), (w3_all, w3_by_b)):
                for j in range(BPT):
                    sp.dma_start(dst[T * j:T * j + T, :, :],
                                 src.rearrange("(i j) (t d) -> j t i d", j=BPT, d=T)[j]).then_inc(S["wgath_back"], 16)
            sp.dma_start(b3_nat[:, :], b3_by_b.rearrange("(i j) d -> i (j d)", j=BPT)).then_inc(S["wgath_back"], 16)
            sp.wait_ge(S["dve_tab"], 1)
            sp.dma_start(writer_keys.rearrange("(b j) -> b j", j=WS), wkey).then_inc(S["keys_out"], 16)
            sp.wait_ge(S["keys_out"], 16)
            sp.dma_start(wkey_bc, writer_keys.rearrange("(o w) -> o w", o=1).broadcast_to([P, NW])).then_inc(S["keys_back"], 16)
            def pair_at(n):
                return bass.ds(n * PAIR if isinstance(n, int) else sp.snap(n * PAIR), PAIR)

            def a1(r, s4, on):
                s = s4 % 2
                if on(0, PAIRS):
                    here = pair_at(r)
                    if on(2):
                        sp.wait_ge(S["l0_done"], r - 1)
                    hold(sp)
                    sp.dma_start(xt[s], x_rows[here, :].rearrange("(i p) d -> p i d", p=P)
                                 ).then_inc(S[f"xt_in{s}"], 16)
                if on(1, PAIRS + 1):
                    here = pair_at(r - 1)
                    sp.wait_ge(S["x1_ready"], r)
                    hold(sp)
                    sp.dma_start(x1_T.rearrange("c p r -> p c r")[:, :, here], x1t[1 - s]
                                 ).then_inc(S[f"x1_out{1 - s}"], 16)
                if on(3, PAIRS + 3):
                    here = pair_at(r - 3)
                    sp.wait_ge(S["rows_ready"], r - 2)
                    sp.wait_ge(S["v_copied"], r - 2)
                    hold(sp)
                    sp.dma_start(new_rows[here, :].rearrange("(i p) d -> p i d", p=P), kv_o[1 - s]
                                 ).then_inc(S[f"rows_out{1 - s}"], 16)
            rounds(sp, a1, PAIRS + 3)
            for s in range(2):
                sp.wait_ge(S[f"x1_out{s}"], 16 * (PAIRS // 2))
            def a2(r, s4, on):
                s = s4 % 2
                if on(0, PAIRS):
                    here = pair_at(r)
                    if on(2):
                        sp.wait_ge(S["q_done"], r - 1)
                    else:
                        sp.wait_ge(S["kv_done"], PAIRS)
                    hold(sp)
                    sp.dma_start(x1t[s], x1_T.rearrange("c p r -> p c r")[:, :, here]
                                 ).then_inc(S[f"x1_in{s}"], 16)
                if on(3, PAIRS + 3):
                    here = pair_at(r - 3)
                    sp.wait_ge(S["qt_ready"], r - 2)
                    hold(sp)
                    sp.dma_start(q_T.rearrange("h p r -> p h r")[:, :, here], qt[1 - s]
                                 ).then_inc(S[f"qt_out{1 - s}"], 16)
            rounds(sp, a2, PAIRS + 3)
            for s in range(2):
                sp.wait_ge(S[f"qt_out{s}"], 16 * (PAIRS // 2))

            def store(ph, i):
                sp.wait_ge(S["l3_moved"], 8 * ph + i + 1)
                sp.dma_start(out_rows[bass.ds(ph * PROWS + i * P, P), :], o_t[i % 2]).then_inc(S[f"out_done{i % 2}"], 16)

            def load_q(ph, half):
                sp.dma_start(qT_ph[:, :, half * UROWS:(half + 1) * UROWS],
                             q_T.rearrange("h p r -> p h r")[:, :, bass.ds(ph * PROWS + half * UROWS, UROWS)]).then_inc(S[f"q_in{half}"], 16)

            def load_x1(ph, half):
                sp.dma_start(xT_ph[:, :, half * UROWS:(half + 1) * UROWS],
                             x1_T.rearrange("c p r -> p c r")[:, :, bass.ds(ph * PROWS + half * UROWS, UROWS)]
                             ).then_inc(S[f"x1_unit{half}"], 16)

            def phase(ph, later, more):
                if later:
                    sp.wait_ge(S["qbd_ready"], 8 * ph - 4)
                load_q(ph, 0)
                if later:
                    sp.wait_ge(S["qbd_ready"], 8 * ph)
                load_q(ph, 1)
                if later:
                    sp.wait_ge(S["x3_done"], 8 * ph - 4)
                load_x1(ph, 0)
                if later:
                    for i in range(4, 8):
                        store(ph - 1, i)
                    sp.wait_ge(S["x3_done"], 8 * ph)
                load_x1(ph, 1)
                for i in range(4):
                    store(ph, i)
            phases(sp, phase)
            for i in range(4, 8):
                store(PH - 1, i)
            for s in range(2):
                sp.wait_ge(S[f"out_done{s}"], 16 * PH * 4)

        @block.gpsimd
        def _(pool):
            g = nc.gpsimd
            steps = [0]

            def link(ins):
                ins.then_inc(S["pool_step"], 1)
                steps[0] += 1
                pool.wait_ge(S["pool_step"], steps[0])

            for n, name in enumerate(("itok_B_1_198", "itok_B_0_7")):
                pool.dma_start(idx_cols[:, n:n + 1], a[name].rearrange("(b o) -> b o", o=1)).then_inc(S["pre2"], 16)
            pool.wait_ge(S["pre2"], 32)
            g.indirect_dma_start(gathered[:, 0, :], None, a["L0_cond_weights"].rearrange("s c d -> s (c d)"),
                                 bass.IndirectOffsetOnAxis(ap=idx_cols[:, 0:1], axis=0),
                                 bounds_check=199, oob_is_err=False).then_inc(S["wgath"], 16)
            g.indirect_dma_start(gathered[:, 1, :], None, a["L3_cond_weights"].rearrange("s c d -> s (c d)"),
                                 bass.IndirectOffsetOnAxis(ap=idx_cols[:, 1:2], axis=0),
                                 bounds_check=7, oob_is_err=False).then_inc(S["wgath"], 16)
            g.indirect_dma_start(gathered_b, None, a["fside_8xS_0"],
                                 bass.IndirectOffsetOnAxis(ap=idx_cols[:, 1:2], axis=0),
                                 bounds_check=7, oob_is_err=False).then_inc(S["wgath"], 16)
            link(g.memset(ident[:, :], 0.0))
            link(g.affine_select(out=ident[:, :], in_=ident[:, :], compare_op=ALU.not_equal, fill=1.0, base=0,
                                 pattern=[[-1, P]], channel_multiplier=1))
            g.iota(iota_row, pattern=[[1, NBLK]], base=0, channel_multiplier=0,
                   allow_small_or_imprecise_dtypes=True).then_inc(S["pool_const"], 1)
            g.iota(off_io, pattern=[[0, WS], [1, BLK]], base=0, channel_multiplier=0,
                   allow_small_or_imprecise_dtypes=True).then_inc(S["pool_const"], 1)
            g.iota(order_bc, pattern=[[1, NW]], base=1, channel_multiplier=0,
                   allow_small_or_imprecise_dtypes=True).then_inc(S["pool_const"], 1)
            g.iota(value_bc.rearrange("p (b j) -> p b j", j=WS), pattern=[[T, B], [BLK, WS]], base=64, channel_multiplier=0,
                   allow_small_or_imprecise_dtypes=True).then_inc(S["pool_const"], 1)
            g.iota(kv_col[:, 1:2], pattern=[[0, 1]], base=0, channel_multiplier=1).then_inc(S["pool_const"], 1)
            g.memset(eps_t[:, :], EPS).then_inc(S["pool_const"], 1)
            for f in range(HD // 2):
                g.memset(inv_f[:, f:f + 1], float(INV_FREQ[f])).then_inc(S["pool_const"], 1)
            for m, v in ((same_b, 1.0), (head_scale, SCALE)):
                link(g.memset(m[:, :], v))
                link(g.affine_select(out=m[:, :], in_=m[:, :], compare_op=ALU.is_ge, fill=0.0, base=0,
                                     pattern=[[-T, BPT]], channel_multiplier=1))
                link(g.affine_select(out=m[:, :], in_=m[:, :], compare_op=ALU.is_ge, fill=0.0, base=T - 1,
                                     pattern=[[T, BPT]], channel_multiplier=-1))
            pool.wait_ge(S["wgath"], 48)
            for q in range(BPT):
                m = mask_wide[T * q:T * q + T, :]
                link(g.memset(m, 0.0))
                link(g.affine_select(out=m, in_=m, compare_op=ALU.is_ge, fill=NEG, base=OFFS,
                                     pattern=[[-1, KEYS + OFFS]], channel_multiplier=1))
                link(g.affine_select(out=m, in_=m, compare_op=ALU.is_ge, fill=NEG, base=WINDOW - 1 - OFFS,
                                     pattern=[[1, KEYS + OFFS]], channel_multiplier=-1))
            g.memset(small[:, NBLK:TP], 0.0).then_inc(S["pool_const"], 1)
            pool.wait_ge(S["pool_step"], steps[0])
            g.memset(cols[:, 15:16], 0.0).then_inc(S["pool_const"], 1)
            pool.wait_ge(S["wgath_back"], 16 * 9)
            def a1(r, s4, on):
                s = s4 % 2
                if on(0, PAIRS):
                    if on(2):
                        pool.wait_ge(S["l0_done"], r - 1)
                    for i in range(2):
                        g.tensor_tensor(w0_bd[s][:, i, :].rearrange("p (j d) -> p j d", j=BPT),
                                        w0_all[:, bass.ds(r * 2 + i, 1), :].broadcast_to([P, BPT, T]),
                                        same_b[:, :, None].broadcast_to([P, BPT, T]), op=ALU.mult).then_inc(S["bd0_ready"], 1)
                    pool.wait_ge(S["bd0_ready"], 3 * r + 2)
                    g.tensor_tensor(w0_bd[s], w0_bd[s], ident[:, None, :].broadcast_to([P, 2, P]), op=ALU.add
                                    ).then_inc(S["bd0_ready"], 1)
            rounds(pool, a1, PAIRS)
            pool.wait_ge(S["own_known"], 1)
            for j in range(WS):
                for dst, src in ((blk_k, k_by_block), (blk_v, v_by_block)):
                    g.indirect_dma_start(dst[:, j, :], None, src, bass.IndirectOffsetOnAxis(ap=w_idx[:, j:j + 1], axis=0),
                                         bounds_check=CACHE - 1, oob_is_err=False).then_inc(S["blk_in"], 16)
            g.memset(arena[:, 0:12288], 0.0).then_inc(S["new_zero"], 1)
            pool.wait_ge(S["new_zero"], 1)
            for s in range(2):
                pool.wait_ge(S[f"rows_out{s}"], 16 * (PAIRS // 2))
            for n in range(WS * BLK):
                g.indirect_dma_start(row_new[:, n, :], None, new_rows, bass.IndirectOffsetOnAxis(ap=own_idx[:, n:n + 1], axis=0),
                                     bounds_check=ROWS - 1, oob_is_err=False).then_inc(S["rows_in"], 16)
            pool.wait_ge(S["dve_tab"], 2)
            for n in range(2):
                pool.dma_start(k_slots[n].rearrange("(b e) -> b e", e=RSP), r_int[:, RSP * n:RSP * n + RSP]).then_inc(S["slots_out"], 16)
                pool.dma_start(v_slots[n].rearrange("(b e) -> b e", e=G * RSP),
                             r_int[:, 24 + 48 * n:24 + 48 * n + 48]).then_inc(S["slots_out"], 16)
            pool.wait_ge(S["slots_out"], 64)
            for n in range(2):
                pool.dma_start(slot_idx[:, :, 3 * n:3 * n + 3],
                             k_slots[n].rearrange("(h p u) -> p h u", p=P, u=3)).then_inc(S["slots_back"], 16)
                pool.dma_start(slot_idx[:, :, 6 + RSP * n:6 + RSP * n + RSP],
                             v_slots[n].rearrange("(h p r) -> p h r", p=P, r=RSP)).then_inc(S["slots_back"], 16)
            for n, (dst, blk) in enumerate(((merged_k, blk_k), (merged_v, blk_v))):
                pool.wait_ge(S["merged_done"], n + 1)
                pool.dma_start(dst.rearrange("(b j) e -> b j e", j=WS), blk).then_inc(S["merged_out"], 16)
            pool.wait_ge(S["slots_back"], 64)

            def gather(n, i):
                done = ("orig_in", "merged_in")[n]
                if i < 3:
                    g.indirect_dma_start(k_raw[:, i].rearrange("p g o d -> p (g o d)"), None, (k_by_block, merged_k)[n],
                                         bass.IndirectOffsetOnAxis(ap=slot_now[:, 3 * n + i:3 * n + i + 1], axis=0),
                                         bounds_check=(CACHE, NW)[n] - 1, oob_is_err=False).then_inc(S[done], 16)
                else:
                    r = i - 3
                    c = 6 + RSP * n + r
                    g.indirect_dma_start(v_raw[:, ROW_G * r:ROW_G * (r + 1)], None, (v_by_head, merged_v_by_head)[n],
                                         bass.IndirectOffsetOnAxis(ap=slot_now[:, c:c + 1], axis=0),
                                         bounds_check=(CACHE, NW)[n] * G - 1, oob_is_err=False).then_inc(S[done], 16)

            NG = 3 + RS
            g.tensor_copy(slot_now[:, :], slot_idx[:, 0, :]).then_inc(S["slots_now"], 1)
            pool.wait_ge(S["slots_now"], 1)
            for i in range(NG):
                gather(0, i)
            pool.wait_ge(S["orig_in"], 16 * NG)
            pool.wait_ge(S["merged_out"], 32)
            for i in range(NG):
                gather(1, i)
            pool.wait_ge(S["qtr_done"], PAIRS)

            def spread_w3(ph, i):
                g.tensor_tensor(w3_bd[i % 4].rearrange("p (j d) -> p j d", j=BPT),
                                w3_all[:, bass.ds(ph * 8 + i, 1), :].broadcast_to([P, BPT, T]),
                                same_b[:, :, None].broadcast_to([P, BPT, T]), op=ALU.mult).then_inc(S["bd3_ready"], 1)
                pool.wait_ge(S["bd3_ready"], 16 * ph + 2 * i + 1)
                g.tensor_tensor(w3_bd[i % 4], w3_bd[i % 4], ident[:, :], op=ALU.add).then_inc(S["bd3_ready"], 1)

            def phase(ph, later, more):
                for b in range(PB + 1):
                    if b < PB:
                        if b >= 8:
                            pool.wait_ge(S["shifted_done"], 2 * (ph * PB + b - 7))
                        elif later:
                            pool.wait_ge(S["shifted_done"], 2 * (ph * PB))
                        at = pool.value_load(mask_at[0:1, bass.ds(ph * PB + b, 1)], min_val=0, max_val=OFFS)
                        g.tensor_tensor(masks[b % 8], mask_wide[:, bass.ds(at, KEYS)],
                                        cols[:, 15:16].broadcast_to([P, KEYS]), op=ALU.add).then_inc(S["mask_ready"], 1)
                    if more and b >= 1:
                        if b == 1:
                            pool.wait_ge(S["k_sorted"], 3 * ph + 3)
                            pool.wait_ge(S["vtr_done"], 16 * ph + 16)
                            hold(pool)
                            g.tensor_copy(slot_now[:, :], slot_idx[:, bass.ds(ph + 1, 1), :].rearrange("p h e -> p (h e)")
                                          ).then_inc(S["slots_now"], 1)
                            pool.wait_ge(S["slots_now"], ph + 2)
                            hold(pool)
                        if 2 <= b < 2 + NG:
                            gather(0, b - 2)
                        if b == 2 + NG:
                            pool.wait_ge(S["orig_in"], 16 * NG * (ph + 2))
                            hold(pool)
                        if 2 + NG <= b < 2 + 2 * NG:
                            gather(1, b - 2 - NG)
                    if b in (14, 16, 18, 20):
                        i = (b - 14) // 2
                        if later:
                            pool.wait_ge(S["l3_done"], 8 * ph - 3 + i)
                        spread_w3(ph, i)
                for i in range(4, 8):
                    pool.wait_ge(S["l3_done"], 8 * ph + i - 3)
                    spread_w3(ph, i)
            phases(pool, phase)

        wtr = []
        for c in range(2):
            for oc in range(2):
                wtr.append((wq_n[:, oc, c * P:c * P + P],
                            wqkv[:, c, 0:D].rearrange("p (h g d) -> p g h d", h=GSZ, g=G)[:, 2 * oc:2 * oc + 2], "q"))
            wtr.append((wk_n[:, c * P:c * P + P], wqkv[:, c, D:D + KV], ""))
            wtr.append((wv_n[:, c * P:c * P + P], wqkv[:, c, D + KV:D + 2 * KV], ""))
        for oc in range(2):
            for h in range(GSZ):
                wtr.append((wo_p[:, oc, h, :],
                            woT[:, h, oc * P:oc * P + P], ""))
            for c in range(2):
                wtr.append((w_n[:, oc, c * P:c * P + P], wT[:, c, oc * P:oc * P + P], "i" if c == oc else ""))
            wtr.append((a_n[:, oc * P:oc * P + P], aT[:, oc, :], ""))
            wtr.append((bm_n[:, oc].rearrange("p n r -> p (n r)"), bT[:, oc * P:oc * P + P], ""))
        NWT = len(wtr)

        @block.tensor
        def _(pe):
            mm = nc.tensor.matmul
            pe.wait_ge(S["weights_in"], 16 * 8)
            pe.wait_ge(S["wo_sorted"], 4)
            pe.wait_ge(S["pool_const"], 24)
            for n, (src, _, _) in enumerate(wtr):
                if n >= 4:
                    pe.wait_ge(S["wtr_moved"], n - 3)
                nc.tensor.transpose(bank[n % 4][:, 0:P], src, ident[:, :]).then_inc(S["wtr_done"], 1)
            pe.wait_ge(S["wgath_back"], 16 * 9)
            pe.wait_ge(S["wtr_moved"], NWT)
            nc.tensor.transpose(bank[6][:, 0:TILES], b3_nat[:, :], ident[0:TILES, 0:TILES]).then_inc(S["wtr_done"], 1)
            def a1(r, s4, on):
                s = s4 % 2
                if on(0, PAIRS):
                    if on(2):
                        pe.wait_ge(S["x1_ready"], r - 1)
                    pe.wait_ge(S["bd0_ready"], 3 * r + 3)
                    pe.wait_ge(S[f"xt_in{s}"], 16 + 8 * (r - s))
                    for i in range(2):
                        for c in range(2):
                            last = mm(bank[s][:, c * PAIR + i * P:c * PAIR + i * P + P], xt[s][:, i, c * P:c * P + P],
                                      w0_bd[s][:, i, :], start=True, stop=True)
                    last.then_inc(S["l0_done"], 1)
                if on(1, PAIRS + 1):
                    pe.wait_ge(S["x1_ready"], r)
                    if on(4):
                        pe.wait_ge(S["dve_a"], 6 * (r - 4) + 1)
                        pe.wait_ge(S["v_copied"], r - 3)
                    for i in range(2):
                        for c in range(2):
                            last = mm(bank[2 + (s4 - 1) % 4][:, i * 256:i * 256 + 256], x1t[1 - s][:, c, i * P:i * P + P],
                                      wqkv[:, c, D:2 * D], start=c == 0, stop=c == 1)
                    last.then_inc(S["kv_done"], 1)
            rounds(pe, a1, PAIRS + 1)
            def a2(r, s4, on):
                s = s4 % 2
                if on(0, PAIRS):
                    pe.wait_ge(S[f"x1_in{s}"], 16 + 8 * (r - s))
                    if on(4):
                        pe.wait_ge(S["dve_q"], 6 * (r - 4) + 2)
                    else:
                        pe.wait_ge(S["dve_a"], 6 * (PAIRS - 4 + r) + 2)
                        pe.wait_ge(S["v_copied"], PAIRS - 3 + r)
                    for i in range(2):
                        for c in range(2):
                            last = mm(bank[2 + s4][:, i * 256:i * 256 + 256], x1t[s][:, c, i * P:i * P + P],
                                      wqkv[:, c, 0:D], start=c == 0, stop=c == 1)
                    last.then_inc(S["q_done"], 1)
                if on(2, PAIRS + 2):
                    pe.wait_ge(S["q_ready"], r - 1)
                    if on(4):
                        pe.wait_ge(S["qt_ready"], r - 3)
                    for h in range(GSZ):
                        for i in range(2):
                            last = nc.tensor.transpose(bank[6 + s][:, h * PAIR + i * P:h * PAIR + i * P + P],
                                                       q_o[s][:, i, h * P:h * P + P], ident[:, :])
                    last.then_inc(S["qtr_done"], 1)
            rounds(pe, a2, PAIRS + 2)

            def finish(w, piece, first):
                unit, half = w
                r0 = UROWS * half
                what, q = piece
                if what == "y":
                    if q == 0:
                        pe.wait_ge(S["o_moved"], 2 * unit + 2)
                        if not first:
                            pe.wait_ge(S["lo_moved"], unit)
                            pe.wait_ge(S["x3_moved"], 4 * unit)
                    for h in range(GSZ):
                        last = mm(bank[5 + q][:, :], woT[:, h, q * P:q * P + P], oT_ph[:, h, r0:r0 + UROWS],
                                  start=h == 0, stop=h == GSZ - 1)
                    last.then_inc(S["y_done"], 1)
                elif what == "lo":
                    pe.wait_ge(S["y_moved"], 2 * unit + 2)
                    for c in range(2):
                        last = mm(bank[5][:, :], aT[:, c, :], xT_ph[:, c, r0:r0 + UROWS], start=c == 0, stop=c == 1)
                    last.then_inc(S["lo_done"], 1)
                elif what == "x3":
                    pe.wait_ge(S["lo_moved"], unit + 1)
                    if q or not first:
                        pe.wait_ge(S["x3_moved"], 4 * unit + q)
                    rr = slice(r0 + q * P, r0 + q * P + P)
                    for c in range(2):
                        mm(bank[6][:, 0:D], xT_ph[:, c, rr], wT[:, c, :], start=c == 0, stop=False)
                    mm(bank[6][:, 0:D], low[:, q * P:q * P + P], bT[:, :], start=False, stop=True).then_inc(S["x3_done"], 1)
                else:
                    pe.wait_ge(S["x3_moved"], 4 * unit + q + 1)
                    pe.wait_ge(S["bd3_ready"], 8 * unit + 2 * q + 2)
                    if q or not first:
                        pe.wait_ge(S["l3_moved"], 4 * unit + q)
                    mm(bank[7][:, 0:D], w3_bd[q], x3[q % 2], start=True, stop=True).then_inc(S["l3_done"], 1)

            def phase(ph, later, more):
                pe.wait_ge(S["merged_in"], 16 * (3 + RS) * (ph + 1))
                vt = [0]

                def v_transposes(count):
                    for n in range(vt[0], vt[0] + count):
                        c, d4 = n // 8, n % 8
                        if n >= 2:
                            pe.wait_ge(S["vtr_moved"], 16 * ph + n - 1)
                        for d in range(4):
                            dd = 4 * d4 + d
                            last = nc.tensor.transpose(bank[2 + n % 2][0:KC, d * P:d * P + P],
                                                       v_raw[:, c * KC * HD + dd:(c + 1) * KC * HD:HD], ident[:, :])
                        last.then_inc(S["vtr_done"], 1)
                    vt[0] += count

                n = 0
                v_transposes(3)
                for u in range(3):
                    pe.wait_ge(S["k_sorted"], 3 * ph + u + 1)
                    for o4 in range(4):
                        if n >= 2:
                            pe.wait_ge(S["ktr_moved"], 12 * ph + n - 1)
                        for o in range(4):
                            last = nc.tensor.transpose(bank[n % 2][:, o * P:o * P + P], k_perm[:, 4 * o4 + o, :], ident[:, :])
                        last.then_inc(S["ktr_done"], 1)
                        n += 1
                        if n % 4 == 2:
                            v_transposes(2)
                    v_transposes((2, 3, 2)[u])
                pe.wait_ge(S["ktr_moved"], 12 * ph + 12)
                pe.wait_ge(S["vtr_moved"], 16 * ph + 16)

                for step in range(STEPS):
                    b = step
                    if b < PB:
                        if b % BPT == 0:
                            pe.wait_ge(S["qbd_ready"], 8 * ph + b // BPT + 1)
                        if b >= 2:
                            pe.wait_ge(S["shifted_done"], 2 * (ph * PB + b - 1))
                        elif later:
                            pe.wait_ge(S["shifted_done"], 2 * (ph * PB))
                        for j in range(2):
                            last = mm(bank[b % 2][:, 256 * j:256 * j + KEYS],
                                      q_bd[(b // BPT) % 2][:, b % BPT, 2 * j:2 * j + 2, :].rearrange("p g q -> p (g q)"),
                                      kT[:, b, :], start=True, stop=True)
                        last.then_inc(S["s_done"], 1)
                    b = step - LAG
                    if 0 <= b < PB:
                        pe.wait_ge(S["norm_done"], 2 * (ph * PB + b + 1))
                        if b >= 2:
                            pe.wait_ge(S["pt_moved"], ph * PB + b - 1)
                        for c in range(2):
                            for j in range(2):
                                last = nc.tensor.transpose(bank[2 + b % 2][0:KC, (2 * c + j) * P:(2 * c + j + 1) * P],
                                                           normed[b % PR][:, j, c * KC:c * KC + KC], ident[:, :])
                        last.then_inc(S["pt_done"], 1)
                    b = step - LAG - 1
                    if b >= 0:
                        pe.wait_ge(S["pt_moved"], ph * PB + b + 1)
                        if b % 8 == 0 and (later or b):
                            pe.wait_ge(S["o_moved"], 4 * ph + b // 8)
                        for c in range(2):
                            for g in range(G):
                                last = mm(bank[4][HD * g:HD * g + HD, (b % 8) * 64:(b % 8) * 64 + 64],
                                          vK[0:KC, c, :, b * G + g], pT[b % 2][0:KC, c * 256 + g * 64:c * 256 + g * 64 + 64],
                                          start=c == 0, stop=c == 1)
                        last.then_inc(S["av_done"], 1)
                    if later and step in PIECES:
                        finish((2 * ph - 1, 1), PIECES[step], False)
                    if step - UNIT_AT in PIECES:
                        finish((2 * ph, 0), PIECES[step - UNIT_AT], not later)
            phases(pe, phase)
            for step in sorted(PIECES):
                finish((2 * PH - 1, 1), PIECES[step], False)

        @block.vector
        def _(dve):
            v = nc.vector
            steps = [0]

            def link(ins):
                ins.then_inc(S["dve_pre"], 1)
                steps[0] += 1
                dve.wait_ge(S["dve_pre"], steps[0])

            dve.wait_ge(S["kv_in"], 16)
            dve.wait_ge(S["pool_const"], 24)
            link(v.tensor_scalar(idx_cols[:, 2:3], kv_col[:, 1:2], T - 1, None, ALU.bitwise_and))
            link(v.tensor_copy(cols[:, 1:2], idx_cols[:, 2:3]))
            for j in range(BPT):
                q = slice(T * j, T * j + T)
                link(v.tensor_scalar(pos_f[q], kv_bc_i[q, 0, j::BPT], cols[q, 1:2], None, ALU.add))
            link(v.tensor_tensor(angle, pos_f[:, :, None].broadcast_to([P, TILES, 16]),
                                 inv_f[:, None, :].broadcast_to([P, TILES, 16]), op=ALU.mult))
            for part, (shift, out_t) in enumerate(((0.0, turn_b), (0.25, turn_c))):
                link(v.tensor_scalar(turn_a, angle, float(1 / (2 * np.pi)), shift, ALU.mult, ALU.add))
                link(v.tensor_scalar(turn_a, turn_a, MAGIC, None, ALU.add))
                link(v.tensor_scalar(turn_a, turn_a, MAGIC, None, ALU.subtract))
                link(v.scalar_tensor_tensor(out_t, turn_a, -TWO_PI_HI, angle, ALU.mult, ALU.add))
                link(v.scalar_tensor_tensor(out_t, turn_a, -TWO_PI_LO, out_t, ALU.mult, ALU.add))
                if part:
                    link(v.tensor_scalar(out_t, out_t, float(np.pi / 2), None, ALU.add))
                v.tensor_scalar(out_t, out_t, -PI, PI, ALU.max, ALU.min).then_inc(S["angles_ready"], 1)

            dve.wait_ge(S["weights_in"], 16 * 8)
            for c in range(2):
                for h in range(GSZ):
                    v.tensor_copy(wo_p[:, c, h, :].rearrange("p (g d) -> p g d", g=G),
                                  wo_n[:, c, :].rearrange("p (g h d) -> p g h d", g=G, h=GSZ)[:, :, h, :]).then_inc(S["wo_sorted"], 1)
            for n, (_, dst, kind) in enumerate(wtr):
                dve.wait_ge(S["wtr_done"], n + 1)
                src = bank[n % 4][:, 0:P]
                if kind == "q":
                    v.tensor_copy(dst, src.rearrange("p (g h d) -> p g h d", g=2, h=2)).then_inc(S["wtr_moved"], 1)
                elif kind == "i":
                    v.tensor_tensor(dst, src, ident[:, :], op=ALU.add).then_inc(S["wtr_moved"], 1)
                else:
                    v.tensor_copy(dst, src).then_inc(S["wtr_moved"], 1)
            dve.wait_ge(S["wtr_done"], NWT + 1)
            link(v.tensor_copy(b3_all[:, :], bank[6][:, 0:TILES]))
            dve.wait_ge(S["const_in"], 16 * (NAD + 3))
            for h0, n in ((0, H), (H, G)):
                link(v.tensor_scalar(gain[:, h0, :], gain[:, h0, :], 1.0, None, ALU.add))
                link(v.tensor_copy(gain[:, h0 + 1:h0 + n, :], gain[:, h0:h0 + 1, :].broadcast_to([P, n - 1, HD])))
            link(v.tensor_scalar(idx_cols[:, 3:4], kv_col[:, 1:2], 4, None, ALU.logical_shift_right))
            link(v.tensor_copy(cols[:, 2:3], idx_cols[:, 3:4]))
            link(v.tensor_scalar(adapt[:, :], n_idx_bc[:, :], cols[:, 2:3], cols[:, 0:1], ALU.is_equal, ALU.mult))

            dve.wait_ge(S["table_in"], 32)
            link(v.tensor_copy(table[:, 0:NBLK], table_i[:, :]))
            kc = lambda n: kv_col[:, n:n + 1]
            link(v.tensor_scalar(kc(2), kc(0), BLK - 1, None, ALU.bitwise_and))
            link(v.tensor_scalar(kc(3), kc(0), 4, None, ALU.logical_shift_right))
            link(v.tensor_scalar(kc(4), kc(0), -(WINDOW - 1.0), 0.0, ALU.add, ALU.max))
            link(v.tensor_scalar(kc(5), kc(4), 4, None, ALU.logical_shift_right))
            link(v.tensor_copy(cols[:, 3:4], kc(2)))
            link(v.tensor_copy(cols[:, 4:5], kc(3)))
            link(v.tensor_copy(cols[:, 5:6], kc(5)))
            link(v.tensor_scalar(hot_r, iota_row, cols[:, 5:6], None, ALU.is_equal))
            link(v.tensor_scalar(hot_w, iota_row, cols[:, 4:5], None, ALU.is_equal))
            for r in range(RSP):
                link(v.tensor_tensor_reduce(out=scrap[:, 0:NBLK], in0=table[:, r:r + NBLK], in1=hot_r, scale=1.0, scalar=0.0,
                                            op0=ALU.mult, op1=ALU.add, accum_out=read_blk[:, r:r + 1]))
            for j in range(WS):
                link(v.tensor_tensor_reduce(out=scrap[:, 0:NBLK], in0=table[:, j:j + NBLK], in1=hot_w, scale=1.0, scalar=0.0,
                                            op0=ALU.mult, op1=ALU.add, accum_out=wblk[:, j:j + 1]))
            link(v.tensor_copy(w_idx[:, :], wblk))
            link(v.tensor_scalar(cols[:, 6:7], cols[:, 3:4], 0.5, None, ALU.is_gt))
            link(v.tensor_copy(wkey[:, 0:2], wblk[:, 0:2]))
            link(v.tensor_scalar(wkey[:, 2:3], wblk[:, 2:3], 1.0, cols[:, 6:7], ALU.add, ALU.mult))
            v.tensor_scalar(wkey[:, 2:3], wkey[:, 2:3], -1.0, None, ALU.add).then_inc(S["dve_tab"], 1)
            link(v.tensor_scalar(kv_bc_i[:, 1, :], kv_bc_i[:, 0, :], -(WINDOW - 1.0), 0.0, ALU.add, ALU.max))
            link(v.tensor_scalar(kv_bc_i[:, 1, :], kv_bc_i[:, 1, :], 4, 4, ALU.logical_shift_right, ALU.logical_shift_left))
            link(v.tensor_tensor(tmp_bc, kv_bc_i[:, 1, :], kv_bc_i[:, 0, :], op=ALU.subtract))
            link(v.tensor_scalar(mask_at[:, :], tmp_bc[0:1, :], float(OFFS), None, ALU.add))
            link(v.tensor_scalar(kv_bc_i[:, 1, :], kv_bc_i[:, 0, :], BLK - 1, None, ALU.bitwise_and))
            link(v.tensor_copy(m_bc, kv_bc_i[:, 1, :]))
            link(v.tensor_tensor(value_bc.rearrange("p (b j) -> p b j", j=WS), value_bc.rearrange("p (b j) -> p b j", j=WS),
                                 m_bc[:, :, None].broadcast_to([P, B, WS]), op=ALU.subtract))
            cov = cover.rearrange("p o (b j) -> p o b j", j=WS)
            io = off_io[:, 0:BLK, None].broadcast_to([P, BLK, B])
            mb = m_bc[:, None, :].broadcast_to([P, BLK, B])
            dve.wait_ge(S["act_pre"], 4)
            link(v.tensor_tensor(cov[:, :, :, 0], io, mb, op=ALU.is_ge))
            link(v.memset(cov[:, :, :, 1], 1.0))
            link(v.tensor_tensor(cov[:, :, :, 2], io, mb, op=ALU.is_lt))
            dve.wait_ge(S["keys_back"], 16)
            for j in range(WS):
                link(v.scalar_tensor_tensor(match[:, j, :], wkey_bc, wblk[:, j:j + 1], value_bc, ALU.is_equal, ALU.mult))
                for o in range(BLK):
                    link(v.tensor_tensor_reduce(out=owner_o, in0=match[:, j, :], in1=cover[:, o, :], scale=1.0, scalar=0.0,
                                                op0=ALU.mult, op1=ALU.max, accum_out=own_max[:, j * BLK + o:j * BLK + o + 1]))
            link(v.tensor_scalar(own_any[:, :], own_max, 0.5, None, ALU.is_gt))
            link(v.tensor_scalar(own_none, own_max, 0.5, float(BIG), ALU.is_lt, ALU.mult))
            link(v.tensor_tensor(own_f, own_max, off_io, op=ALU.add))
            link(v.tensor_scalar(own_f, own_f, -64.0, 0.0, ALU.add, ALU.max))
            v.tensor_tensor(own_idx[:, :], own_f, own_none, op=ALU.add).then_inc(S["own_known"], 1)

            def normed_heads(ps, heads, rs, gain_t, at, chain, base):
                n = 2 * heads * HD
                v4 = lambda t: t[:, 0:n].rearrange("p (i h d) -> p i h d", i=2, d=HD)
                v.tensor_tensor(v4(nrm), ps, rs.rearrange("p (i h) -> p i h", i=2)[:, :, :, None].broadcast_to([P, 2, heads, HD]),
                                op=ALU.mult).then_inc(S[chain], 1)
                dve.wait_ge(S[chain], base + 2)
                v.tensor_tensor(v4(gained), v4(nrm), gain_t[:, None].broadcast_to([P, 2, heads, HD]), op=ALU.mult
                                ).then_inc(S[chain], 1)
                dve.wait_ge(S[chain], base + 3)
                v.tensor_tensor(v4(rot_c), v4(gained), cos2[:, at, :][:, :, None, :].broadcast_to([P, 2, heads, HD]),
                                op=ALU.mult).then_inc(S[chain], 1)
                for half in range(2):
                    o, m = half * 16, 16 - half * 16
                    v.tensor_tensor(v4(rot_s)[:, :, :, o:o + 16], v4(gained)[:, :, :, m:m + 16],
                                    sin2[:, at, o:o + 16][:, :, None, :].broadcast_to([P, 2, heads, 16]), op=ALU.mult
                                    ).then_inc(S[chain], 1)

            dve.wait_ge(S["act_pre"], 4)
            def a1(r, s4, on):
                s = s4 % 2
                if on(1, PAIRS + 1):
                    dve.wait_ge(S["sq_done"], r)
                    v.reduce_sum(ssum[1 - s][:, 0:2 * G], sq[1 - s][:, 0:2 * KV].rearrange("p (h d) -> p h d", d=HD), axis=AX.X
                                 ).then_inc(S["ms_done"], 1)
                if on(2, PAIRS + 2):
                    base = 6 * (r - 2)
                    dve.wait_ge(S["sqrt_done"], r - 1)
                    if on(3):
                        dve.wait_ge(S["rows_ready"], r - 2)
                    v.reciprocal(rstd[s][:, 0:2 * G], rtmp[s][:, 0:2 * G]).then_inc(S["dve_a"], 1)
                    dve.wait_ge(S["dve_a"], base + 1)
                    normed_heads(bank[2 + (s4 - 2) % 4][:, :].rearrange("p (i h d) -> p i h d", i=2, d=HD)[:, :, 0:G, :], G, rstd[s][:, 0:2 * G],
                                 gain[:, H:H + G, :], bass.ds((r - 2) * 2, 2), "dve_a", base)
                    dve.wait_ge(S["dve_a"], base + 6)
                    if on(4):
                        dve.wait_ge(S[f"rows_out{s}"], 8 * (r - 2 - s))
                    v.tensor_tensor(kv_o[s][:, :, 0:KV], rot_c[:, 0:2 * KV].rearrange("p (i n) -> p i n", i=2),
                                    rot_s[:, 0:2 * KV].rearrange("p (i n) -> p i n", i=2), op=ALU.add).then_inc(S["rows_ready"], 1)
            rounds(dve, a1, PAIRS + 2)

            for r in range(RSP):
                link(v.scalar_tensor_tensor(scrap, wkey_bc, read_blk[:, r:r + 1], order_bc, ALU.is_equal, ALU.mult))
                link(v.tensor_reduce(read_w[:, r:r + 1], scrap, axis=AX.X, op=ALU.max))
            link(v.tensor_scalar(r_hit, read_w, 0.5, None, ALU.is_gt))
            link(v.scalar_tensor_tensor(r_a, r_hit, float(BIG), read_blk, ALU.mult, ALU.add))
            link(v.tensor_scalar(r_hit, read_w, 0.5, float(BIG), ALU.is_lt, ALU.mult))
            link(v.scalar_tensor_tensor(r_b, read_w, -1.0, r_hit, ALU.add, ALU.add))
            for n, t in enumerate((r_a, r_b)):
                link(v.tensor_copy(r_int[:, RSP * n:RSP * n + RSP].rearrange("p (q u) -> p q u", u=3),
                                   t.rearrange("p (u q) -> p q u", u=3)))
                for g in range(G):
                    link(v.tensor_scalar(r_int[:, 24 + 48 * n + RSP * g:24 + 48 * n + RSP * g + RSP], t, float(G), float(g),
                                         ALU.mult, ALU.add))
            v.engine_nop().then_inc(S["dve_tab"], 1)

            def a2(r, s4, on):
                s = s4 % 2
                if on(1, PAIRS + 1):
                    dve.wait_ge(S["qsq_done"], r)
                    v.reduce_sum(ssum[1 - s][:, 0:2 * H], sq[1 - s].rearrange("p (h d) -> p h d", d=HD), axis=AX.X
                                 ).then_inc(S["qms_done"], 1)
                if on(2, PAIRS + 2):
                    base = 6 * (r - 2)
                    dve.wait_ge(S["qsqrt_done"], r - 1)
                    if on(3):
                        dve.wait_ge(S["q_ready"], r - 2)
                    else:
                        dve.wait_ge(S["rows_ready"], PAIRS)
                    v.reciprocal(rstd[s], rtmp[s]).then_inc(S["dve_q"], 1)
                    dve.wait_ge(S["dve_q"], base + 1)
                    normed_heads(bank[2 + (s4 - 2) % 4][:, :].rearrange("p (i h d) -> p i h d", i=2, d=HD), H, rstd[s],
                                 gain[:, 0:H, :], bass.ds((r - 2) * 2, 2), "dve_q", base)
                    dve.wait_ge(S["dve_q"], base + 6)
                    if on(4):
                        dve.wait_ge(S["qtr_done"], r - 3)
                    elif on(2, 3):
                        for n in range(2):
                            dve.wait_ge(S[f"rows_out{n}"], 16 * (PAIRS // 2))
                    v.tensor_tensor(q_o[s].rearrange("p i n -> p (i n)"), rot_c, rot_s, op=ALU.add).then_inc(S["q_ready"], 1)

            def merge():
                dve.wait_ge(S["blk_in"], 16 * 6)
                dve.wait_ge(S["rows_in"], 16 * WS * BLK)
                for kv, blk in enumerate((blk_k, blk_v)):
                    for j in range(WS):
                        out = blk[:, j, :].rearrange("p (g o d) -> p g o d", g=G, o=BLK)
                        data = row_new[:, j * BLK:(j + 1) * BLK, kv * KV:(kv + 1) * KV].rearrange("p o (g d) -> p g o d", g=G)
                        for g in range(G):
                            link(v.copy_predicated(out[:, g], own_any[:, j * BLK:(j + 1) * BLK, None].broadcast_to([P, BLK, HD]), data[:, g]))
                    v.engine_nop().then_inc(S["merged_done"], 1)
            rounds(dve, a2, PAIRS + 2, merge)

            def finish(w, piece, first):
                unit, half, batch0, turn = w
                r0 = UROWS * half
                what, q = piece
                if what == "y":
                    dve.wait_ge(S[f"x1_unit{half}"], 16 * turn)
                    dve.wait_ge(S["y_done"], 2 * unit + q + 1)
                    v.tensor_tensor(xT_ph[:, q, r0:r0 + UROWS], bank[5 + q][:, :], xT_ph[:, q, r0:r0 + UROWS],
                                    op=ALU.add).then_inc(S["y_moved"], 1)
                elif what == "lo":
                    dve.wait_ge(S["lo_done"], unit + 1)
                    if not first:
                        dve.wait_ge(S["x3_done"], 4 * unit)
                    v.tensor_tensor(low[:, :].rearrange("p (b t) -> p b t", t=T),
                                    bank[5][:, :].rearrange("p (b t) -> p b t", t=T),
                                    adapt[:, bass.ds(batch0, 16)][:, :, None].broadcast_to([P, 16, T]),
                                    op=ALU.mult).then_inc(S["lo_moved"], 1)

            def phase(ph, later, more):
                def expand(q4):
                    if q4 % 4 == 0:
                        dve.wait_ge(S[f"q_in{q4 // 4}"], 16 * (ph + 1))
                    if q4 >= 2:
                        dve.wait_ge(S["s_done"], ph * PB + BPT * (q4 - 1))
                    for g in range(G):
                        last = v.tensor_scalar(
                            q_bd[q4 % 2][:, :, g, :].rearrange("p b (h t) -> p b h t", h=GSZ),
                            qT_ph[:, :, P * q4:P * q4 + P].rearrange("p h (b t) -> p b h t", b=BPT),
                            head_scale[:, g:g + 1], None, ALU.mult)
                    last.then_inc(S["qbd_ready"], 1)

                dve.wait_ge(S["merged_in"], 16 * (3 + RS) * (ph + 1))
                if later:
                    dve.wait_ge(S["s_done"], ph * PB)
                n = 0
                for u in range(3):
                    if u or later:
                        dve.wait_ge(S["ktr_done"], 12 * ph + 4 * u)
                    v.tensor_copy(k_perm.rearrange("p o (g d) -> p o g d", g=G),
                                  k_raw[:, u].rearrange("p g o d -> p o g d")).then_inc(S["k_sorted"], 1)
                    for o4 in range(4):
                        q = 4 if u < 2 else 3
                        dve.wait_ge(S["ktr_done"], 12 * ph + n + 1)
                        v.tensor_copy(
                            kT[:, :, u * 64:u * 64 + 16 * q].rearrange("p b (r o) -> p b r o", o=BLK)[:, :, :, 4 * o4:4 * o4 + 4],
                            bank[n % 2][:, :].rearrange("p (o b r) -> p b r o", o=4, r=4)[:, :, 0:q, :]).then_inc(S["ktr_moved"], 1)
                        n += 1
                expand(0)
                for step in range(STEPS + 1):
                    b = step
                    if b < PB:
                        if b % BPT == 1 and b // BPT + 1 < PB // BPT:
                            expand(b // BPT + 1)
                        dve.wait_ge(S["s_done"], ph * PB + b + 1)
                        dve.wait_ge(S["mask_ready"], ph * PB + b + 1)
                        if b >= 3:
                            dve.wait_ge(S["exp_done"], 2 * (ph * PB + b - 2))
                        elif later:
                            dve.wait_ge(S["exp_done"], 2 * (ph * PB))
                        hold(dve)
                        for j in range(2):
                            v.tensor_tensor_reduce(out=shifted[b % 3][:, j, :], in0=bank[b % 2][:, 256 * j:256 * j + KEYS],
                                                   in1=masks[b % 8], scale=-1.0, scalar=3.0e38, op0=ALU.add, op1=ALU.min,
                                                   accum_out=neg_max[:, 2 * b + j:2 * b + j + 1]).then_inc(S["shifted_done"], 1)
                    b = step - 1
                    if 0 <= b < PB:
                        dve.wait_ge(S["exp_done"], 2 * (ph * PB + b + 1))
                        v.reciprocal(p_inv[:, 2 * b:2 * b + 2], p_sum[:, 2 * b:2 * b + 2]).then_inc(S["inv_done"], 1)
                        dve.wait_ge(S["inv_done"], ph * PB + b + 1)
                        if b >= PR:
                            dve.wait_ge(S["pt_done"], ph * PB + b - PR + 1)
                        elif later:
                            dve.wait_ge(S["pt_done"], ph * PB)
                        for j in range(2):
                            v.tensor_scalar(normed[b % PR][:, j, :], probs[b % PR][:, j, :], p_inv[:, 2 * b + j:2 * b + j + 1], 1.0,
                                            ALU.mult, ALU.mult).then_inc(S["norm_done"], 1)
                    b = step - LAG
                    if 0 <= b < PB and b % 2 == 0:
                        dve.wait_ge(S["pt_done"], ph * PB + b + 1)
                        if b >= 2:
                            dve.wait_ge(S["av_done"], ph * PB + b - 1)
                        elif later:
                            dve.wait_ge(S["av_done"], ph * PB)
                        if later or b:
                            dve.wait_ge(S["pt_moved"], ph * PB + b)
                        v.tensor_copy(pT[b % 2][0:KC, :], bank[2 + b % 2][0:KC, :]).then_inc(S["pt_moved"], 1)
                    b = step - LAG - 1
                    if b >= 0 and b % 8 == 7:
                        i8 = b // 8
                        dve.wait_ge(S["av_done"], ph * PB + b + 1)
                        if later:
                            dve.wait_ge(S["y_done"], 4 * ph - 2 + 2 * (i8 // 2))
                        v.tensor_copy(oT_ph[:, :, 256 * i8:256 * i8 + 256].rearrange("p h (b t) -> p b h t", b=8),
                                      bank[4][:, :].rearrange("p (b h t) -> p b h t", b=8, h=GSZ)).then_inc(S["o_moved"], 1)
                    if later and step - 1 in PIECES:
                        finish((2 * ph - 1, 1, ph * PB - 16, ph), PIECES[step - 1], False)
                    if step - 1 - UNIT_AT in PIECES:
                        finish((2 * ph, 0, ph * PB, ph + 1), PIECES[step - 1 - UNIT_AT], not later)
            phases(dve, phase)
            for step in sorted(PIECES):
                finish((2 * PH - 1, 1, B - 16, PH), PIECES[step], False)

        @block.scalar
        def _(act):
            s_ = nc.scalar
            act.wait_ge(S["angles_ready"], 2)
            s_.activation(sin2[:, :, 0:16], turn_b, ACT.Sin, scale=-1.0).then_inc(S["act_pre"], 1)
            s_.activation(sin2[:, :, 16:32], turn_b, ACT.Sin).then_inc(S["act_pre"], 1)
            for half in range(2):
                s_.activation(cos2[:, :, 16 * half:16 * half + 16], turn_c, ACT.Sin).then_inc(S["act_pre"], 1)
            def a1(r, s4, on):
                s = s4 % 2
                if on(2, PAIRS + 2):
                    ps = bank[2 + (s4 - 2) % 4][:, :].rearrange("p (i n) -> p i n", i=2)
                    if on(4):
                        act.wait_ge(S[f"rows_out{s}"], 8 * (r - 2 - s))
                    s_.activation(kv_o[s][:, :, KV:2 * KV], ps[:, :, KV:2 * KV], ACT.Copy).then_inc(S["v_copied"], 1)
                    act.wait_ge(S["ms_done"], r - 1)
                    if on(4):
                        act.wait_ge(S["dve_a"], 6 * (r - 4) + 1)
                    s_.activation(rtmp[s][:, 0:2 * G], ssum[s][:, 0:2 * G], ACT.Sqrt, scale=1.0 / HD, bias=eps_t[:, 0:1]
                                  ).then_inc(S["sqrt_done"], 1)
                if on(0, PAIRS):
                    act.wait_ge(S["l0_done"], r + 1)
                    if on(2):
                        act.wait_ge(S["kv_done"], r - 1)
                        act.wait_ge(S[f"x1_out{s}"], 8 * (r - s))
                    s_.activation(x1t[s].rearrange("p c r -> p (c r)"), bank[s][:, :], ACT.Copy).then_inc(S["x1_ready"], 1)
                if on(1, PAIRS + 1):
                    act.wait_ge(S["kv_done"], r)
                    if on(3):
                        act.wait_ge(S["ms_done"], r - 2)
                    ps = bank[2 + (s4 - 1) % 4][:, :].rearrange("p (i n) -> p i n", i=2)
                    s_.activation(sq[1 - s][:, 0:2 * KV].rearrange("p (i n) -> p i n", i=2), ps[:, :, 0:KV], ACT.Square
                                  ).then_inc(S["sq_done"], 1)
            rounds(act, a1, PAIRS + 2)
            def a2(r, s4, on):
                s = s4 % 2
                if on(2, PAIRS + 2):
                    act.wait_ge(S["qms_done"], r - 1)
                    if on(4):
                        act.wait_ge(S["dve_q"], 6 * (r - 4) + 1)
                    else:
                        act.wait_ge(S["dve_a"], 6 * PAIRS)
                    s_.activation(rtmp[s], ssum[s], ACT.Sqrt, scale=1.0 / HD, bias=eps_t[:, 0:1]).then_inc(S["qsqrt_done"], 1)
                if on(0, PAIRS):
                    act.wait_ge(S["q_done"], r + 1)
                    if on(2):
                        act.wait_ge(S["qms_done"], r - 1)
                    else:
                        act.wait_ge(S["ms_done"], PAIRS)
                    s_.activation(sq[s], bank[2 + s4][:, :], ACT.Square).then_inc(S["qsq_done"], 1)
                if on(2, PAIRS + 2):
                    act.wait_ge(S["qtr_done"], r - 1)
                    if on(4):
                        act.wait_ge(S[f"qt_out{s}"], 8 * (r - 2 - s))
                    s_.activation(qt[s].rearrange("p h r -> p (h r)"), bank[6 + s][:, :], ACT.Copy).then_inc(S["qt_ready"], 1)
            rounds(act, a2, PAIRS + 2)

            def finish(w, piece, first):
                unit, q0 = w
                what, q = piece
                if what == "x3":
                    act.wait_ge(S["x3_done"], 4 * unit + q + 1)
                    if q > 1 or not first:
                        act.wait_ge(S["l3_done"], 4 * unit + q - 1)
                    s_.activation(x3[q % 2], bank[6][:, 0:D], ACT.Copy).then_inc(S["x3_moved"], 1)
                elif what == "l3":
                    act.wait_ge(S["l3_done"], 4 * unit + q + 1)
                    if q > 1 or not first:
                        act.wait_ge(S[f"out_done{q % 2}"], 32 * unit + 16 * (q // 2))
                    s_.activation(o_t[q % 2], bank[7][:, 0:D], ACT.Identity, bias=b3_all[:, bass.ds(q0 + q, 1)]
                                  ).then_inc(S["l3_moved"], 1)

            def phase(ph, later, more):
                for n in range(16):
                    c, d4 = n // 8, n % 8
                    act.wait_ge(S["vtr_done"], 16 * ph + n + 1)
                    if later and n == 0:
                        act.wait_ge(S["av_done"], ph * PB)
                    s_.activation(vK[0:KC, c, 4 * d4:4 * d4 + 4, :].rearrange("p d n -> p (d n)"), bank[2 + n % 2][0:KC, :],
                                  ACT.Copy).then_inc(S["vtr_moved"], 1)
                for step in range(STEPS + 1):
                    b = step
                    if b < PB:
                        if b >= PR:
                            act.wait_ge(S["norm_done"], 2 * (ph * PB + b - PR + 1))
                        for j in range(2):
                            act.wait_ge(S["shifted_done"], 2 * (ph * PB + b) + j + 1)
                            s_.activation(probs[b % PR][:, j, :], shifted[b % 3][:, j, :], ACT.Exp, scale=-1.0,
                                          bias=neg_max[:, 2 * b + j:2 * b + j + 1],
                                          accum_out=p_sum[:, 2 * b + j:2 * b + j + 1]).then_inc(S["exp_done"], 1)
                    b = step - LAG
                    if 0 <= b < PB and b % 2 == 1:
                        act.wait_ge(S["pt_done"], ph * PB + b + 1)
                        if b >= 2:
                            act.wait_ge(S["av_done"], ph * PB + b - 1)
                        elif later:
                            act.wait_ge(S["av_done"], ph * PB)
                        act.wait_ge(S["pt_moved"], ph * PB + b)
                        s_.activation(pT[b % 2][0:KC, :], bank[2 + b % 2][0:KC, :], ACT.Copy).then_inc(S["pt_moved"], 1)
                    if later and step - 1 in PIECES:
                        finish((2 * ph - 1, 8 * ph - 4), PIECES[step - 1], False)
                    if step - 1 - UNIT_AT in PIECES:
                        finish((2 * ph, 8 * ph), PIECES[step - 1 - UNIT_AT], not later)
            phases(act, phase)
            for step in sorted(PIECES):
                finish((2 * PH - 1, TILES - 4), PIECES[step], False)


_INS = ["x", "itok_B_1_198", "itok_Bx257_0_4111", "itok_B_37_3939", "itok_B_0_6", "itok_B_0_7", "fside_8xS_0",
        "L0_cond_weights", "L1_cond_Wq", "L1_cond_Wk", "L1_cond_Wv", "L1_cond_Wo", "L1_cond_q_norm_scale",
        "L1_cond_k_norm_scale", "L1_cond_k_blocks", "L1_cond_v_blocks", "L2_cond_W", "L2_cond_A", "L2_cond_Bm",
        "L2_cond_scalings", "L3_cond_weights"]


def kernel(**inputs):
    import numpy as _np
    import concourse.bacc as _bacc
    from concourse import mybir as _mybir
    from concourse.bass_utils import run_bass_kernel_spmd as _run

    nc = _bacc.Bacc("TRN2", target_bir_lowering=False, num_devices=1)
    arrays, aps = {}, {}
    for name in _INS:
        arr = _np.ascontiguousarray(inputs[name])
        arrays[f"in_{name}"] = arr
        aps[name] = nc.dram_tensor(f"in_{name}", arr.shape, _mybir.dt.from_np(arr.dtype), kind="ExternalInput").ap()
    aps["out"] = nc.dram_tensor("out", (B, T, D), _mybir.dt.float32, kind="ExternalOutput").ap()
    build(nc, aps)
    r = _run(nc, [arrays], core_ids=[0])
    return r.results[0]["out"]
```

```python
import numpy as np
import concourse.bass as bass
from concourse import mybir
from contextlib import ExitStack

F32 = mybir.dt.float32
I32 = mybir.dt.int32
ALU = mybir.AluOpType
ACT = mybir.ActivationFunctionType
AX = mybir.AxisListType

P = 128
B, T, D = 128, 32, 256
ROWS = B * T
BPT = P // T
TILES = ROWS // P
G, GSZ, HD = 4, 2, 32
H = G * GSZ
QK = (H + G) * HD
KV = G * HD
BLK = 16
NBLK = 257
CACHE = 4112
WINDOW = 128
SCALE = 256.0 ** -0.5
EPS = 1e-6
THETA = 10000.0
ROW_G = BLK * HD
ROW_B = G * ROW_G
WS = 3
NW = B * WS
RS = 11
RSP = 12
KEYS = RS * BLK
KC = KEYS // 2
PH = 4
PB = B // PH
PROWS = PB * T
UROWS = PROWS // 2
OFFS = WINDOW + BLK - 2
BIG = 1 << 20
NEG = -1.0e30
RANK = 16
NAD = P // RANK
TP = NBLK + 15
LAG = 3
STEPS = PB + LAG + 1
VTR = (8, 8)
UNIT_AT = PB // 2 + LAG + 2
PIECES = {0: ("y", 0), 1: ("y", 1), 3: ("lo", 0)}
for _q in range(4):
    PIECES[4 + 2 * _q] = ("x3", _q)
    PIECES[5 + 2 * _q] = ("l3", _q)
TWO_PI_HI = 6.28125
TWO_PI_LO = float(2 * np.pi - 6.28125)
MAGIC = 12582912.0
PI = float(np.float32(3.1415925))
INV_FREQ = (np.float32(1.0) / np.float32(THETA) ** (np.arange(HD // 2, dtype=np.float32) / np.float32(HD // 2))).astype(np.float32)


def build(nc, a):
    ctx = ExitStack()
    with ctx:
        def sb(name, shape, dt=F32):
            return ctx.enter_context(nc.sbuf_tensor(name, shape, dt))

        def sem(name):
            return ctx.enter_context(nc.semaphore(name))

        def dram(name, shape, dt=F32):
            return nc.dram_tensor(name, shape, dt, kind="Internal").ap()

        x_rows = a["x"].rearrange("b t d -> (b t) d")
        out_rows = a["out"].rearrange("b t d -> (b t) d")
        k_by_block = a["L1_cond_k_blocks"].rearrange("n g o d -> n (g o d)")
        v_by_head = a["L1_cond_v_blocks"].rearrange("n g o d -> (n g) (o d)")
        v_by_block = a["L1_cond_v_blocks"].rearrange("n g o d -> n (g o d)")
        w0_by_b = dram("w0_by_b", [B, T * T])
        w3_by_b = dram("w3_by_b", [B, T * T])
        b3_by_b = dram("b3_by_b", [B, T])
        writer_keys = dram("writer_keys", [NW])
        new_rows = dram("new_rows", [ROWS, 2 * KV])
        x1_T = dram("x1_T", [2, P, ROWS])
        q_T = dram("q_T", [GSZ, P, ROWS])
        merged_k = dram("merged_k", [NW, ROW_B])
        merged_v = dram("merged_v", [NW, ROW_B])
        merged_v_by_head = merged_v.rearrange("n (g e) -> (n g) e", g=G)
        k_slots = dram("k_slots", [2, B * RSP], I32)
        v_slots = dram("v_slots", [2, B * G * RSP], I32)

        ident = sb("ident", [P, P])
        wqkv = sb("wqkv", [P, 2, 512])
        woT = sb("woT", [P, GSZ, D])
        wT = sb("wT", [P, 2, D])
        aT = sb("aT", [P, 2, P])
        bT = sb("bT", [P, D])
        same_b = sb("same_b", [P, BPT])
        head_scale = sb("head_scale", [P, G])
        adapt = sb("adapt", [P, B])
        w0_all = sb("w0_all", [P, TILES, T])
        w3_all = sb("w3_all", [P, TILES, T])
        b3_all = sb("b3_all", [P, TILES])
        b3_nat = sb("b3_nat", [TILES, P])
        tables = sb("tables", [P, 2, TILES, HD])
        q_area = sb("q_area", [P, 2048])
        q_tables = q_area[:, :].rearrange("p (a i d) -> p a i d", a=2, i=TILES)
        k_perm = [[t.rearrange("p a b -> p (a b)").rearrange("p (o e) -> p o e", o=BLK // 2) for t in two]
                  for two in ((tables[:, 0], tables[:, 1]), (w0_all[:, :, :], wqkv[:, :, 0:512]))]
        gain = sb("gain", [P, 2, HD])
        mask_wide = sb("mask_wide", [P, KEYS + OFFS])
        mask_at = sb("mask_at", [1, B], I32)
        eps_t = sb("eps_t", [P, 1])
        slot_idx = sb("slot_idx", [P, PH, 2 * 3 + 2 * RSP], I32)
        slot_now = sb("slot_now", [P, 2 * 3 + 2 * RSP], I32)
        kv_col = sb("kv_col", [P, 8], I32)
        cols = sb("cols", [P, 16])
        own_idx = sb("own_idx", [P, WS * BLK], I32)
        own_any = sb("own_any", [P, WS * BLK], I32)
        w_idx = sb("w_idx", [P, WS], I32)
        idx_cols = sb("idx_cols", [P, 4], I32)

        arena = sb("arena", [P, 25600])
        row_new = arena[:, 0:12288].rearrange("p (s e) -> p s e", s=WS * BLK)
        blk_k = arena[:, 12288:18432].rearrange("p (j e) -> p j e", j=WS)
        blk_v = arena[:, 18432:24576].rearrange("p (j e) -> p j e", j=WS)
        match = arena[:, 2112:2112 + WS * NW].rearrange("p (j w) -> p j w", j=WS)
        cover = arena[:, 3264:3264 + NW].rearrange("p (b j) -> p b j", j=WS)
        owner_o = arena[:, 3648:3648 + WS * NW].rearrange("p (j w) -> p j w", j=WS)
        k_raw = arena[:, 0:6144].rearrange("p (u g o d) -> p u g o d", u=3, g=G, o=BLK)
        v_raw = arena[:, 6144:11776]
        kT = arena[:, 11776:17408].rearrange("p (b k) -> p b k", b=PB)
        vK = arena[:, 17408:25600].rearrange("p (c d n) -> p c d n", c=2, d=HD)
        stage = arena[:, 4864:7936]
        wq_n = stage[:, 0:512].rearrange("p (c n) -> p c n", c=2)
        wk_n = stage[:, 512:768]
        wv_n = stage[:, 768:1024]
        wo_n = stage[:, 1024:1536].rearrange("p (c n) -> p c n", c=2)
        w_n = stage[:, 1536:2048].rearrange("p (c n) -> p c n", c=2)
        a_n = stage[:, 2048:2304]
        wo_p = stage[:, 2560:3072].rearrange("p (c h n) -> p c h n", c=2, h=GSZ)
        bm_n = stage[:, 2304:2560].rearrange("p (c n r) -> p c n r", c=2, n=NAD)
        small = sb("small", [P, 3264])
        table = small[:, 0:TP]
        hot_r = small[:, 272:272 + NBLK]
        hot_w = small[:, 544:544 + NBLK]
        iota_row = small[:, 816:816 + NBLK]
        wkey_bc = small[:, 1088:1088 + NW]
        value_bc = small[:, 1472:1472 + NW]
        order_bc = small[:, 1856:1856 + NW]
        m_bc = small[:, 2240:2240 + B]
        tmp_bc = small[:, 2368:2368 + B]
        read_blk = small[:, 2496:2496 + RSP]
        read_w = small[:, 2512:2512 + RSP]
        wblk = small[:, 2528:2528 + WS]
        wkey = small[:, 2532:2532 + WS]
        own_max = small[:, 2544:2592]
        own_now = small[:, 2592:2592 + WS]
        off_io = small[:, 2640:2688]
        own_f = small[:, 2688:2736]
        r_hit = small[:, 2736:2748]
        r_a = small[:, 2752:2764]
        r_b = small[:, 2768:2780]
        scrap = small[:, 2880:2880 + NW]
        table_i = sb("table_i", [P, NBLK], I32)
        kv_bc_i = sb("kv_bc_i", [P, 2, B], I32)
        r_int = sb("r_int", [P, 2 * RSP + 2 * G * RSP], I32)
        n_idx_bc = sb("n_idx_bc", [P, B], I32)

        ring = sb("ring", [P, 8032])
        def cut(at, n):
            return ring[:, at:at + n]
        PAIR = 2 * P
        xt = [arena[:, 10240 + 512 * s:10752 + 512 * s].rearrange("p (i d) -> p i d", i=2) for s in range(4)]
        w0_bd = [cut(1024 + 256 * s, 256).rearrange("p (i n) -> p i n", i=2) for s in range(2)]
        x1t = [cut(1536 + 512 * s, 512).rearrange("p (c r) -> p c r", c=2) for s in range(2)]
        x1q = [cut(at, 512).rearrange("p (c r) -> p c r", c=2) for at in (0, 512, 1536, 2048)]
        sq = [cut(2560 + 512 * s, 512) for s in range(2)]
        nrm, rot_c, rot_s = (cut(at, 512) for at in (3584, 4608, 5120))
        kv_o = [cut(5632 + 512 * s, 512).rearrange("p (i n) -> p i n", i=2) for s in range(2)]
        q_o = kv_o
        qt = [cut(at, 512).rearrange("p (h r) -> p h r", h=GSZ) for at in (6656, 7168, 1024, 4096)]
        ssum = [cut(7680 + 16 * s, 16) for s in range(2)]
        rstd = [cut(7712 + 16 * s, 16) for s in range(2)]
        rtmp = [cut(7744 + 16 * s, 16) for s in range(2)]
        angle = arena[:, 0:512].rearrange("p (i f) -> p i f", i=TILES)
        turn_a = arena[:, 512:1024].rearrange("p (i f) -> p i f", i=TILES)
        turn_b = arena[:, 1024:1536].rearrange("p (i f) -> p i f", i=TILES)
        turn_c = arena[:, 1536:2048].rearrange("p (i f) -> p i f", i=TILES)
        pos_f = arena[:, 2048:2080]
        inv_f = arena[:, 2080:2096]
        gathered = arena[:, 7936:9984].rearrange("p (a e) -> p a e", a=2)
        gathered_b = arena[:, 9984:10016]
        PR = 4
        shifted = [cut(352 * s, 352).rearrange("p (j k) -> p j k", j=2) for s in range(3)]
        probs = [cut(1056 + 352 * s, 352).rearrange("p (j k) -> p j k", j=2) for s in range(PR)]
        normed = [cut(2464 + 352 * s, 352).rearrange("p (j k) -> p j k", j=2) for s in range(PR)]
        pT = [cut(3872 + 512 * s, 512) for s in range(2)]
        masks = [cut(4896 + KEYS * s, KEYS) for s in range(8)]
        x3 = [cut(6304 + 256 * s, 256) for s in range(2)]
        o_t = [cut(6816 + 256 * s, 256) for s in range(2)]
        w3_bd = [cut(7328 + 128 * s, 128) for s in range(4)]
        neg_max = cut(7840, 64)
        p_sum = cut(7904, 64)
        p_inv = cut(7968, 64)
        q_bd = [q_area[:, 1024 * s:1024 * s + 1024].rearrange("p (b g n) -> p b g n", b=BPT, g=G) for s in range(2)]
        qT_ph = sb("qT_ph", [P, GSZ, PROWS])
        xT_ph = sb("xT_ph", [P, 2, PROWS])
        oT_ph = small[:, 0:GSZ * PROWS].rearrange("p (h r) -> p h r", h=GSZ)
        low = small[:, GSZ * PROWS:GSZ * PROWS + 512]

        bank = [ctx.enter_context(nc.psum_tensor(f"bank{i}", [P, 512], F32)) for i in range(8)]

        names = """weights_in const_in table_in kv_in wgath wgath_out wgath_back pre2 tab_const pool_const ident_ready
            pool_step held wtr_done wtr_moved wo_sorted dve_pre angles_ready act_pre dve_tab keys_out keys_back xt_in0
            xt_in1 xt_in2 xt_in3 bd0_ready l0_done x1_ready x1_out0 x1_out1 kv_done sq_done ms_done sqrt_done v_copied
            dve_a rows_ready own_step reader_step rows_out0 rows_out1 x1_in0 x1_in1 x1_in2 x1_in3 q_done qsq_done
            qms_done qsqrt_done dve_q q_ready qtr_done qt_ready qt_out0 qt_out1 qt_out2 qt_out3 own_known blk_in
            rows_in0 rows_in1 rows_in2 merged_done merged_out slots_out slots_back q_in0 q_in1 x1_unit0 x1_unit1
            orig_in merged_in slots_now k_sorted0 k_sorted1 ktr_done ktr_moved0 ktr_moved1 vtr_done vtr_moved0
            vtr_moved1 qbd_ready mask_ready s_done shifted_done exp_done inv_done norm_done pt_done pt_moved av_done
            o_moved y_done y_moved lo_done lo_moved x3_done x3_moved bd3_ready l3_done l3_moved out_done0 out_done1""".split()
        S = {n: sem(n) for n in names}

        block = ctx.enter_context(nc.Block())

        PAIRS = TILES // 2
        SLOTS_AT, MERGE0, MERGE1 = 4, 5, 7
        FIRST1, FIRST2 = 4, 8

        def rounds(eng, do, first, last, between=None):
            def static(r):
                do(r, r % 4, lambda lo, hi=99: lo <= r < hi)
            for r in range(first):
                static(r)
            if between:
                between()
            with eng.Fori(first // 4, PAIRS // 4) as turn:
                for s in range(4):
                    do(4 * turn + s, s, lambda lo, hi=99: True)
            for r in range(PAIRS, last):
                static(r)

        def phases(eng, do):
            do(0, False, True)
            with eng.Fori(1, PH - 1) as ph:
                do(ph, True, True)
            do(PH - 1, True, False)

        def hold(eng):
            eng.sem_inc(S["held"], 1)

        wtr = []
        for c in range(2):
            for oc in range(2):
                wtr.append((wq_n[:, oc, c * P:c * P + P],
                            wqkv[:, c, 0:D].rearrange("p (h g d) -> p g h d", h=GSZ, g=G)[:, 2 * oc:2 * oc + 2], "q"))
            wtr.append((wk_n[:, c * P:c * P + P], wqkv[:, c, D:D + KV], ""))
            wtr.append((wv_n[:, c * P:c * P + P], wqkv[:, c, D + KV:D + 2 * KV], ""))
        for oc in range(2):
            for h in range(GSZ):
                wtr.append((wo_p[:, oc, h, :],
                            woT[:, h, oc * P:oc * P + P], ""))
            for c in range(2):
                wtr.append((w_n[:, oc, c * P:c * P + P], wT[:, c, oc * P:oc * P + P], "i" if c == oc else ""))
            wtr.append((a_n[:, oc * P:oc * P + P], aT[:, oc, :], ""))
            wtr.append((bm_n[:, oc].rearrange("p n r -> p (n r)"), bT[:, oc * P:oc * P + P], ""))
        NWT = len(wtr)

        @block.sync
        def _(sp):
            for dst, src in ((table_i[:, :], a["itok_Bx257_0_4111"]),
                             (kv_col[:, 0:1], a["itok_B_37_3939"].rearrange("(b o) -> b o", o=1))):
                sp.dma_start(dst, src).then_inc(S["table_in"], 16)
            lens = a["itok_B_37_3939"].rearrange("(o b) -> o b", o=1)
            sp.dma_start(kv_bc_i[:, 0, :], lens.broadcast_to([P, B])).then_inc(S["kv_in"], 16)
            for dst, src in ((wq_n, a["L1_cond_Wq"].rearrange("(c p) d -> p c d", p=P)),
                             (wk_n, a["L1_cond_Wk"]), (wv_n, a["L1_cond_Wv"]),
                             (wo_n, a["L1_cond_Wo"].rearrange("(c p) d -> p c d", p=P)),
                             (w_n, a["L2_cond_W"].rearrange("(c p) d -> p c d", p=P)),
                             (a_n, a["L2_cond_A"].rearrange("n r d -> (n r) d")),
                             (bm_n[:, 0], a["L2_cond_Bm"].rearrange("n (c p) r -> c p n r", p=P)[0]),
                             (bm_n[:, 1], a["L2_cond_Bm"].rearrange("n (c p) r -> c p n r", p=P)[1])):
                sp.dma_start(dst, src).then_inc(S["weights_in"], 16)
            ones = lambda n: a[n].rearrange("(o d) -> o d", o=1)
            for n in range(NAD):
                sp.dma_start(cols[RANK * n:RANK * n + RANK, 0:1], ones("L2_cond_scalings")[:, n:n + 1].broadcast_to([RANK, 1])
                             ).then_inc(S["const_in"], 16)
            sp.dma_start(gain[:, 0, :], ones("L1_cond_q_norm_scale").broadcast_to([P, HD])).then_inc(S["const_in"], 16)
            sp.dma_start(gain[:, 1, :], ones("L1_cond_k_norm_scale").broadcast_to([P, HD])).then_inc(S["const_in"], 16)
            sp.dma_start(n_idx_bc[:, :], ones("itok_B_0_6").broadcast_to([P, B])).then_inc(S["const_in"], 16)
            sp.wait_ge(S["wgath"], 48)
            sp.dma_start(w0_by_b, gathered[:, 0, :]).then_inc(S["wgath_out"], 16)
            sp.dma_start(w3_by_b, gathered[:, 1, :]).then_inc(S["wgath_out"], 16)
            sp.dma_start(b3_by_b, gathered_b).then_inc(S["wgath_out"], 16)
            sp.wait_ge(S["wgath_out"], 48)
            for dst, src in ((w0_all, w0_by_b), (w3_all, w3_by_b)):
                for j in range(BPT):
                    sp.dma_start(dst[T * j:T * j + T, :, :],
                                 src.rearrange("(i j) (t d) -> j t i d", j=BPT, d=T)[j]).then_inc(S["wgath_back"], 16)
            sp.dma_start(b3_nat[:, :], b3_by_b.rearrange("(i j) d -> i (j d)", j=BPT)).then_inc(S["wgath_back"], 16)
            sp.wait_ge(S["dve_tab"], 1)
            sp.dma_start(writer_keys.rearrange("(b j) -> b j", j=WS), wkey).then_inc(S["keys_out"], 16)
            sp.wait_ge(S["keys_out"], 16)
            sp.dma_start(wkey_bc, writer_keys.rearrange("(o w) -> o w", o=1).broadcast_to([P, NW])).then_inc(S["keys_back"], 16)
            def pair_at(n):
                return bass.ds(n * PAIR if isinstance(n, int) else sp.snap(n * PAIR), PAIR)

            def a1(r, s4, on):
                s = s4 % 2
                if on(0, PAIRS):
                    here = pair_at(r)
                    if on(4):
                        sp.wait_ge(S["l0_done"], r - 3)
                    hold(sp)
                    sp.dma_start(xt[s4], x_rows[here, :].rearrange("(i p) d -> p i d", p=P)
                                 ).then_inc(S[f"xt_in{s4}"], 16)
                if on(3, PAIRS + 3):
                    here = pair_at(r - 3)
                    sp.wait_ge(S["x1_ready"], r - 2)
                    hold(sp)
                    sp.dma_start(x1_T.rearrange("c p r -> p c r")[:, :, here], x1t[1 - s]
                                 ).then_inc(S[f"x1_out{1 - s}"], 16)
                if on(5, PAIRS + 5):
                    here = pair_at(r - 5)
                    sp.wait_ge(S["rows_ready"], r - 4)
                    sp.wait_ge(S["v_copied"], r - 4)
                    hold(sp)
                    sp.dma_start(new_rows[here, :].rearrange("(i p) d -> p i d", p=P), kv_o[1 - s]
                                 ).then_inc(S[f"rows_out{1 - s}"], 16)
            rounds(sp, a1, 8, PAIRS + 5)
            for s in range(2):
                sp.wait_ge(S[f"x1_out{s}"], 16 * (PAIRS // 2))
            def a2(r, s4, on):
                s = s4 % 2
                if on(0, PAIRS):
                    here = pair_at(r)
                    if on(4):
                        sp.wait_ge(S["q_done"], r - 3)
                    elif on(2):
                        sp.wait_ge(S["kv_done"], PAIRS)
                    hold(sp)
                    sp.dma_start(x1q[s4], x1_T.rearrange("c p r -> p c r")[:, :, here]
                                 ).then_inc(S[f"x1_in{s4}"], 16)
                if on(5, PAIRS + 5):
                    here = pair_at(r - 5)
                    sp.wait_ge(S["qt_ready"], r - 4)
                    hold(sp)
                    sp.dma_start(q_T.rearrange("h p r -> p h r")[:, :, here], qt[(s4 - 5) % 4]
                                 ).then_inc(S[f"qt_out{(s4 - 5) % 4}"], 16)
            rounds(sp, a2, 8, PAIRS + 5)
            for s in range(4):
                sp.wait_ge(S[f"qt_out{s}"], 16 * (PAIRS // 4))

            def store(ph, i):
                sp.wait_ge(S["l3_moved"], 8 * ph + i + 1)
                sp.dma_start(out_rows[bass.ds(ph * PROWS + i * P, P), :], o_t[i % 2]).then_inc(S[f"out_done{i % 2}"], 16)

            def load_q(ph, half):
                sp.dma_start(qT_ph[:, :, half * UROWS:(half + 1) * UROWS],
                             q_T.rearrange("h p r -> p h r")[:, :, bass.ds(ph * PROWS + half * UROWS, UROWS)]).then_inc(S[f"q_in{half}"], 16)

            def load_x1(ph, half):
                sp.dma_start(xT_ph[:, :, half * UROWS:(half + 1) * UROWS],
                             x1_T.rearrange("c p r -> p c r")[:, :, bass.ds(ph * PROWS + half * UROWS, UROWS)]
                             ).then_inc(S[f"x1_unit{half}"], 16)

            def phase(ph, later, more):
                if later:
                    sp.wait_ge(S["x3_done"], 8 * ph - 4)
                load_x1(ph, 0)
                if later:
                    for i in range(4, 8):
                        store(ph - 1, i)
                    sp.wait_ge(S["x3_done"], 8 * ph)
                load_x1(ph, 1)
                if more:
                    sp.wait_ge(S["qbd_ready"], 8 * ph + 4)
                    load_q(ph + 1, 0)
                for i in range(3):
                    store(ph, i)
                if more:
                    sp.wait_ge(S["qbd_ready"], 8 * ph + 8)
                    load_q(ph + 1, 1)
                store(ph, 3)
            load_q(0, 0)
            load_q(0, 1)
            phases(sp, phase)
            for i in range(4, 8):
                store(PH - 1, i)
            for s in range(2):
                sp.wait_ge(S[f"out_done{s}"], 16 * PH * 4)

        @block.gpsimd
        def _(pool):
            g = nc.gpsimd
            steps = [0]

            def link(ins):
                ins.then_inc(S["pool_step"], 1)
                steps[0] += 1
                pool.wait_ge(S["pool_step"], steps[0])

            for n, name in enumerate(("itok_B_1_198", "itok_B_0_7")):
                pool.dma_start(idx_cols[:, n:n + 1], a[name].rearrange("(b o) -> b o", o=1)).then_inc(S["pre2"], 16)
            g.iota(iota_row, pattern=[[1, NBLK]], base=0, channel_multiplier=0,
                   allow_small_or_imprecise_dtypes=True).then_inc(S["tab_const"], 1)
            g.memset(small[:, NBLK:TP], 0.0).then_inc(S["tab_const"], 1)
            link(g.memset(ident[:, :], 0.0))
            link(g.affine_select(out=ident[:, :], in_=ident[:, :], compare_op=ALU.not_equal, fill=1.0, base=0,
                                 pattern=[[-1, P]], channel_multiplier=1))
            g.engine_nop().then_inc(S["ident_ready"], 1)
            pool.wait_ge(S["pre2"], 32)
            g.indirect_dma_start(gathered[:, 0, :], None, a["L0_cond_weights"].rearrange("s c d -> s (c d)"),
                                 bass.IndirectOffsetOnAxis(ap=idx_cols[:, 0:1], axis=0),
                                 bounds_check=199, oob_is_err=False).then_inc(S["wgath"], 16)
            g.indirect_dma_start(gathered[:, 1, :], None, a["L3_cond_weights"].rearrange("s c d -> s (c d)"),
                                 bass.IndirectOffsetOnAxis(ap=idx_cols[:, 1:2], axis=0),
                                 bounds_check=7, oob_is_err=False).then_inc(S["wgath"], 16)
            g.indirect_dma_start(gathered_b, None, a["fside_8xS_0"],
                                 bass.IndirectOffsetOnAxis(ap=idx_cols[:, 1:2], axis=0),
                                 bounds_check=7, oob_is_err=False).then_inc(S["wgath"], 16)
            g.iota(off_io, pattern=[[0, WS], [1, BLK]], base=0, channel_multiplier=0,
                   allow_small_or_imprecise_dtypes=True).then_inc(S["pool_const"], 1)
            g.iota(order_bc, pattern=[[1, NW]], base=1, channel_multiplier=0,
                   allow_small_or_imprecise_dtypes=True).then_inc(S["pool_const"], 1)
            g.iota(value_bc.rearrange("p (b j) -> p b j", j=WS), pattern=[[T, B], [BLK, WS]], base=64, channel_multiplier=0,
                   allow_small_or_imprecise_dtypes=True).then_inc(S["pool_const"], 1)
            g.iota(kv_col[:, 1:2], pattern=[[0, 1]], base=0, channel_multiplier=1).then_inc(S["pool_const"], 1)
            g.memset(eps_t[:, :], EPS).then_inc(S["pool_const"], 1)
            for f in range(HD // 2):
                g.memset(inv_f[:, f:f + 1], float(INV_FREQ[f])).then_inc(S["pool_const"], 1)
            for m, v in ((same_b, 1.0), (head_scale, SCALE)):
                link(g.memset(m[:, :], v))
                link(g.affine_select(out=m[:, :], in_=m[:, :], compare_op=ALU.is_ge, fill=0.0, base=0,
                                     pattern=[[-T, BPT]], channel_multiplier=1))
                link(g.affine_select(out=m[:, :], in_=m[:, :], compare_op=ALU.is_ge, fill=0.0, base=T - 1,
                                     pattern=[[T, BPT]], channel_multiplier=-1))
            pool.wait_ge(S["pool_step"], steps[0])
            g.memset(cols[:, 15:16], 0.0).then_inc(S["pool_const"], 1)
            pool.wait_ge(S["wgath_back"], 16 * 9)
            pool.wait_ge(S["dve_tab"], 1)
            for j in range(WS):
                for dst, src in ((blk_k, k_by_block), (blk_v, v_by_block)):
                    g.indirect_dma_start(dst[:, j, :], None, src, bass.IndirectOffsetOnAxis(ap=w_idx[:, j:j + 1], axis=0),
                                         bounds_check=CACHE - 1, oob_is_err=False).then_inc(S["blk_in"], 16)
            def a1(r, s4, on):
                s = s4 % 2
                if on(0, PAIRS):
                    if on(2):
                        pool.wait_ge(S["l0_done"], r - 1)
                    for i in range(2):
                        g.tensor_tensor(w0_bd[s][:, i, :].rearrange("p (j d) -> p j d", j=BPT),
                                        w0_all[:, bass.ds(r * 2 + i, 1), :].broadcast_to([P, BPT, T]),
                                        same_b[:, :, None].broadcast_to([P, BPT, T]), op=ALU.mult).then_inc(S["bd0_ready"], 1)
                    pool.wait_ge(S["bd0_ready"], 3 * r + 2)
                    g.tensor_tensor(w0_bd[s], w0_bd[s], ident[:, None, :].broadcast_to([P, 2, P]), op=ALU.add
                                    ).then_inc(S["bd0_ready"], 1)
            rounds(pool, a1, FIRST1, PAIRS)
            pool.wait_ge(S["blk_in"], 16 * 6)
            for q in range(BPT):
                m = mask_wide[T * q:T * q + T, :]
                link(g.memset(m, 0.0))
                link(g.affine_select(out=m, in_=m, compare_op=ALU.is_ge, fill=NEG, base=OFFS,
                                     pattern=[[-1, KEYS + OFFS]], channel_multiplier=1))
                link(g.affine_select(out=m, in_=m, compare_op=ALU.is_ge, fill=NEG, base=WINDOW - 1 - OFFS,
                                     pattern=[[1, KEYS + OFFS]], channel_multiplier=-1))
            pool.wait_ge(S["own_known"], 1)
            for s in range(2):
                pool.wait_ge(S[f"rows_out{s}"], 16 * (PAIRS // 2))
            for j in range(WS):
                for n in range(j * BLK, (j + 1) * BLK):
                    g.indirect_dma_start(row_new[:, n, :], None, new_rows, bass.IndirectOffsetOnAxis(ap=own_idx[:, n:n + 1], axis=0),
                                         bounds_check=ROWS - 1, oob_is_err=False).then_inc(S[f"rows_in{j}"], 16)
            pool.wait_ge(S["slots_back"], 64)

            def gather(n, i):
                done = ("orig_in", "merged_in")[n]
                if i < 3:
                    g.indirect_dma_start(k_raw[:, i].rearrange("p g o d -> p (g o d)"), None, (k_by_block, merged_k)[n],
                                         bass.IndirectOffsetOnAxis(ap=slot_now[:, 3 * n + i:3 * n + i + 1], axis=0),
                                         bounds_check=(CACHE, NW)[n] - 1, oob_is_err=False).then_inc(S[done], 16)
                else:
                    r = i - 3
                    c = 6 + RSP * n + r
                    g.indirect_dma_start(v_raw[:, ROW_G * r:ROW_G * (r + 1)], None, (v_by_head, merged_v_by_head)[n],
                                         bass.IndirectOffsetOnAxis(ap=slot_now[:, c:c + 1], axis=0),
                                         bounds_check=(CACHE, NW)[n] * G - 1, oob_is_err=False).then_inc(S[done], 16)

            NG = 3 + RS
            g.tensor_copy(slot_now[:, :], slot_idx[:, 0, :]).then_inc(S["slots_now"], 1)
            pool.wait_ge(S["slots_now"], 1)
            for i in range(NG):
                need = {0: 1, 2: 2, 7: 3}
                if i in need:
                    pool.wait_ge(S["merged_done"], need[i])
                gather(0, i)
            pool.wait_ge(S["orig_in"], 16 * NG)
            pool.wait_ge(S["merged_out"], 32 * WS)
            for i in range(NG):
                gather(1, i)
            pool.wait_ge(S["qtr_done"], PAIRS)

            def spread_w3(ph, i):
                g.tensor_tensor(w3_bd[i % 4].rearrange("p (j d) -> p j d", j=BPT),
                                w3_all[:, bass.ds(ph * 8 + i, 1), :].broadcast_to([P, BPT, T]),
                                same_b[:, :, None].broadcast_to([P, BPT, T]), op=ALU.mult).then_inc(S["bd3_ready"], 1)
                pool.wait_ge(S["bd3_ready"], 16 * ph + 2 * i + 1)
                g.tensor_tensor(w3_bd[i % 4], w3_bd[i % 4], ident[:, :], op=ALU.add).then_inc(S["bd3_ready"], 1)

            def phase(ph, later, more):
                for b in range(PB + 1):
                    if b < PB:
                        if b >= 8:
                            pool.wait_ge(S["shifted_done"], 2 * (ph * PB + b - 7))
                        elif later:
                            pool.wait_ge(S["shifted_done"], 2 * (ph * PB))
                        at = pool.value_load(mask_at[0:1, bass.ds(ph * PB + b, 1)], min_val=0, max_val=OFFS)
                        g.tensor_tensor(masks[b % 8], mask_wide[:, bass.ds(at, KEYS)],
                                        cols[:, 15:16].broadcast_to([P, KEYS]), op=ALU.add).then_inc(S["mask_ready"], 1)
                    if more and b >= 1:
                        if b == 1:
                            for half in range(2):
                                pool.wait_ge(S[f"k_sorted{half}"], 3 * ph + 3)
                            hold(pool)
                            g.tensor_copy(slot_now[:, :], slot_idx[:, bass.ds(ph + 1, 1), :].rearrange("p h e -> p (h e)")
                                          ).then_inc(S["slots_now"], 1)
                            pool.wait_ge(S["slots_now"], ph + 2)
                            hold(pool)
                        if b == 5:
                            pool.wait_ge(S["vtr_done"], 16 * ph + 16)
                            hold(pool)
                        if 2 <= b < 2 + NG:
                            gather(0, b - 2)
                        if b == 2 + NG:
                            pool.wait_ge(S["orig_in"], 16 * NG * (ph + 2))
                            hold(pool)
                        if 2 + NG <= b < 2 + 2 * NG:
                            gather(1, b - 2 - NG)
                    if b in (14, 16, 18, 20):
                        i = (b - 14) // 2
                        if later:
                            pool.wait_ge(S["l3_done"], 8 * ph - 3 + i)
                        spread_w3(ph, i)
                for i in range(4, 8):
                    pool.wait_ge(S["l3_done"], 8 * ph + i - 3)
                    spread_w3(ph, i)
            phases(pool, phase)

        @block.tensor
        def _(pe):
            mm = nc.tensor.matmul
            pe.wait_ge(S["weights_in"], 16 * 8)
            pe.wait_ge(S["wo_sorted"], 4)
            pe.wait_ge(S["ident_ready"], 1)
            for n, (src, _, _) in enumerate(wtr):
                if n >= 4:
                    pe.wait_ge(S["wtr_moved"], n - 3)
                nc.tensor.transpose(bank[n % 4][:, 0:P], src, ident[:, :]).then_inc(S["wtr_done"], 1)
            pe.wait_ge(S["wgath_back"], 16 * 9)
            pe.wait_ge(S["wtr_moved"], NWT)
            nc.tensor.transpose(bank[6][:, 0:TILES], b3_nat[:, :], ident[0:TILES, 0:TILES]).then_inc(S["wtr_done"], 1)
            def a1(r, s4, on):
                s = s4 % 2
                if on(0, PAIRS):
                    if on(2):
                        pe.wait_ge(S["x1_ready"], r - 1)
                    pe.wait_ge(S["bd0_ready"], 3 * r + 3)
                    pe.wait_ge(S[f"xt_in{s4}"], 16 + 4 * (r - s4))
                    for i in range(2):
                        for c in range(2):
                            last = mm(bank[s][:, c * PAIR + i * P:c * PAIR + i * P + P], xt[s4][:, i, c * P:c * P + P],
                                      w0_bd[s][:, i, :], start=True, stop=True)
                    last.then_inc(S["l0_done"], 1)
                if on(1, PAIRS + 1):
                    pe.wait_ge(S["x1_ready"], r)
                    if on(4):
                        pe.wait_ge(S["dve_a"], 5 * (r - 4) + 1)
                        pe.wait_ge(S["v_copied"], r - 3)
                    for i in range(2):
                        for c in range(2):
                            last = mm(bank[2 + (s4 - 1) % 4][:, i * 256:i * 256 + 256], x1t[1 - s][:, c, i * P:i * P + P],
                                      wqkv[:, c, D:2 * D], start=c == 0, stop=c == 1)
                    last.then_inc(S["kv_done"], 1)
            rounds(pe, a1, FIRST1, PAIRS + 1)
            def a2(r, s4, on):
                s = s4 % 2
                if on(0, PAIRS):
                    pe.wait_ge(S[f"x1_in{s4}"], 16 + 4 * (r - s4))
                    if on(4):
                        pe.wait_ge(S["dve_q"], 5 * (r - 4) + 2)
                    else:
                        pe.wait_ge(S["dve_a"], 5 * (PAIRS - 4 + r) + 2)
                        pe.wait_ge(S["v_copied"], PAIRS - 3 + r)
                    for i in range(2):
                        for c in range(2):
                            last = mm(bank[2 + s4][:, i * 256:i * 256 + 256], x1q[s4][:, c, i * P:i * P + P],
                                      wqkv[:, c, 0:D], start=c == 0, stop=c == 1)
                    last.then_inc(S["q_done"], 1)
                if on(2, PAIRS + 2):
                    pe.wait_ge(S["q_ready"], r - 1)
                    if on(4):
                        pe.wait_ge(S["qt_ready"], r - 3)
                    for h in range(GSZ):
                        for i in range(2):
                            last = nc.tensor.transpose(bank[6 + s][:, h * PAIR + i * P:h * PAIR + i * P + P],
                                                       q_o[s][:, i, h * P:h * P + P], ident[:, :])
                    last.then_inc(S["qtr_done"], 1)
            rounds(pe, a2, FIRST2, PAIRS + 2)

            def finish(w, piece, first):
                unit, half = w
                r0 = UROWS * half
                what, q = piece
                if what == "y":
                    if q == 0:
                        pe.wait_ge(S["o_moved"], 2 * unit + 2)
                        if not first:
                            pe.wait_ge(S["lo_moved"], unit)
                            pe.wait_ge(S["x3_moved"], 4 * unit)
                    for h in range(GSZ):
                        last = mm(bank[5 + q][:, :], woT[:, h, q * P:q * P + P], oT_ph[:, h, r0:r0 + UROWS],
                                  start=h == 0, stop=h == GSZ - 1)
                    last.then_inc(S["y_done"], 1)
                elif what == "lo":
                    pe.wait_ge(S["y_moved"], 2 * unit + 2)
                    for c in range(2):
                        last = mm(bank[5][:, :], aT[:, c, :], xT_ph[:, c, r0:r0 + UROWS], start=c == 0, stop=c == 1)
                    last.then_inc(S["lo_done"], 1)
                elif what == "x3":
                    pe.wait_ge(S["lo_moved"], unit + 1)
                    if q or not first:
                        pe.wait_ge(S["x3_moved"], 4 * unit + q)
                    rr = slice(r0 + q * P, r0 + q * P + P)
                    for c in range(2):
                        mm(bank[6][:, 0:D], xT_ph[:, c, rr], wT[:, c, :], start=c == 0, stop=False)
                    mm(bank[6][:, 0:D], low[:, q * P:q * P + P], bT[:, :], start=False, stop=True).then_inc(S["x3_done"], 1)
                else:
                    pe.wait_ge(S["x3_moved"], 4 * unit + q + 1)
                    pe.wait_ge(S["bd3_ready"], 8 * unit + 2 * q + 2)
                    if q or not first:
                        pe.wait_ge(S["l3_moved"], 4 * unit + q)
                    mm(bank[7][:, 0:D], w3_bd[q], x3[q % 2], start=True, stop=True).then_inc(S["l3_done"], 1)

            def transpose_keys(ph, u, later):
                if u == 0 and later:
                    pe.wait_ge(S["shifted_done"], 2 * (ph * PB))
                for half in range(2):
                    pe.wait_ge(S[f"k_sorted{half}"], 3 * ph + u + 1)
                for n in range(4 * u, 4 * u + 4):
                    if n >= 2:
                        pe.wait_ge(S[f"ktr_moved{n % 2}"], 6 * ph + n // 2)
                    for o in range(4):
                        last = nc.tensor.transpose(bank[n % 2][:, o * P:o * P + P], k_perm[u % 2][(n % 4) // 2][:, 4 * (n % 2) + o, :], ident[:, :])
                    last.then_inc(S["ktr_done"], 1)

            def phase(ph, later, more):
                pe.wait_ge(S["merged_in"], 16 * (3 + RS) * (ph + 1))
                for half in range(2):
                    pe.wait_ge(S[f"ktr_moved{half}"], 6 * ph + 6)

                for step in range(STEPS):
                    b = step
                    if b < PB:
                        if b % BPT == 0:
                            pe.wait_ge(S["qbd_ready"], 8 * ph + b // BPT + 1)
                        if b >= 2:
                            pe.wait_ge(S["shifted_done"], 2 * (ph * PB + b - 1))
                        elif later:
                            pe.wait_ge(S["shifted_done"], 2 * (ph * PB))
                        for j in range(2):
                            last = mm(bank[b % 2][:, 256 * j:256 * j + KEYS],
                                      q_bd[(b // BPT) % 2][:, b % BPT, 2 * j:2 * j + 2, :].rearrange("p g q -> p (g q)"),
                                      kT[:, b, :], start=True, stop=True)
                        last.then_inc(S["s_done"], 1)
                    if step < len(VTR):
                        for n in range(sum(VTR[:step]), sum(VTR[:step + 1])):
                            c, d4 = n // 8, n % 8
                            if n >= 3:
                                pe.wait_ge(S[f"vtr_moved{(n - 3) % 2}"], 8 * ph + (n - 3) // 2 + 1)
                            elif later:
                                pe.wait_ge(S["pt_moved"], ph * PB)
                                pe.wait_ge(S["o_moved"], 4 * ph)
                            for d in range(4):
                                dd = 4 * d4 + d
                                last = nc.tensor.transpose(bank[2 + n % 3][0:KC, d * P:d * P + P],
                                                           v_raw[:, c * KC * HD + dd:(c + 1) * KC * HD:HD], ident[:, :])
                            last.then_inc(S["vtr_done"], 1)
                    b = step - LAG
                    if 0 <= b < PB:
                        pe.wait_ge(S["norm_done"], 2 * (ph * PB + b + 1))
                        if b >= 2:
                            pe.wait_ge(S["pt_moved"], ph * PB + b - 1)
                        elif b == 0:
                            pe.wait_ge(S["vtr_moved0"], 8 * ph + 8)
                            pe.wait_ge(S["vtr_moved1"], 8 * ph + 8)
                        for c in range(2):
                            for j in range(2):
                                last = nc.tensor.transpose(bank[2 + b % 2][0:KC, (2 * c + j) * P:(2 * c + j + 1) * P],
                                                           normed[b % PR][:, j, c * KC:c * KC + KC], ident[:, :])
                        last.then_inc(S["pt_done"], 1)
                    b = step - LAG - 1
                    if b >= 0:
                        pe.wait_ge(S["pt_moved"], ph * PB + b + 1)
                        if b % 8 == 0 and (later or b):
                            pe.wait_ge(S["o_moved"], 4 * ph + b // 8)
                        for c in range(2):
                            for g in range(G):
                                last = mm(bank[4][HD * g:HD * g + HD, (b % 8) * 64:(b % 8) * 64 + 64],
                                          vK[0:KC, c, :, b * G + g], pT[b % 2][0:KC, c * 256 + g * 64:c * 256 + g * 64 + 64],
                                          start=c == 0, stop=c == 1)
                        last.then_inc(S["av_done"], 1)
                    if later and step in PIECES:
                        finish((2 * ph - 1, 1), PIECES[step], False)
                    if step - UNIT_AT in PIECES:
                        finish((2 * ph, 0), PIECES[step - UNIT_AT], not later)
                    if more and 0 <= step - PB < 3:
                        transpose_keys(ph + 1, step - PB, True)
            for u in range(3):
                transpose_keys(0, u, False)
            phases(pe, phase)
            for step in sorted(PIECES):
                finish((2 * PH - 1, 1), PIECES[step], False)

        @block.vector
        def _(dve):
            v = nc.vector
            steps = [0]

            def link(ins):
                ins.then_inc(S["dve_pre"], 1)
                steps[0] += 1
                dve.wait_ge(S["dve_pre"], steps[0])

            dve.wait_ge(S["table_in"], 32)
            dve.wait_ge(S["tab_const"], 2)
            link(v.tensor_copy(table[:, 0:NBLK], table_i[:, :]))
            kc = lambda n: kv_col[:, n:n + 1]
            link(v.tensor_scalar(kc(2), kc(0), BLK - 1, None, ALU.bitwise_and))
            link(v.tensor_scalar(kc(3), kc(0), 4, None, ALU.logical_shift_right))
            link(v.tensor_scalar(kc(4), kc(0), -(WINDOW - 1.0), 0.0, ALU.add, ALU.max))
            link(v.tensor_scalar(kc(5), kc(4), 4, None, ALU.logical_shift_right))
            link(v.tensor_copy(cols[:, 3:4], kc(2)))
            link(v.tensor_copy(cols[:, 4:5], kc(3)))
            link(v.tensor_copy(cols[:, 5:6], kc(5)))
            link(v.tensor_scalar(hot_r, iota_row, cols[:, 5:6], None, ALU.is_equal))
            link(v.tensor_scalar(hot_w, iota_row, cols[:, 4:5], None, ALU.is_equal))
            for j in range(WS):
                link(v.tensor_tensor_reduce(out=scrap[:, 0:NBLK], in0=table[:, j:j + NBLK], in1=hot_w, scale=1.0, scalar=0.0,
                                            op0=ALU.mult, op1=ALU.add, accum_out=wblk[:, j:j + 1]))
            link(v.tensor_copy(w_idx[:, :], wblk))
            link(v.tensor_scalar(cols[:, 6:7], cols[:, 3:4], 0.5, None, ALU.is_gt))
            link(v.tensor_copy(wkey[:, 0:2], wblk[:, 0:2]))
            link(v.tensor_scalar(wkey[:, 2:3], wblk[:, 2:3], 1.0, cols[:, 6:7], ALU.add, ALU.mult))
            v.tensor_scalar(wkey[:, 2:3], wkey[:, 2:3], -1.0, None, ALU.add).then_inc(S["dve_tab"], 1)
            dve.wait_ge(S["kv_in"], 16)
            dve.wait_ge(S["pool_const"], 22)
            link(v.tensor_scalar(idx_cols[:, 2:3], kv_col[:, 1:2], T - 1, None, ALU.bitwise_and))
            link(v.tensor_copy(cols[:, 1:2], idx_cols[:, 2:3]))
            for j in range(BPT):
                q = slice(T * j, T * j + T)
                link(v.tensor_scalar(pos_f[q], kv_bc_i[q, 0, j::BPT], cols[q, 1:2], None, ALU.add))
            link(v.tensor_tensor(angle, pos_f[:, :, None].broadcast_to([P, TILES, 16]),
                                 inv_f[:, None, :].broadcast_to([P, TILES, 16]), op=ALU.mult))
            for part, (shift, out_t) in enumerate(((0.0, turn_b), (0.25, turn_c))):
                link(v.tensor_scalar(turn_a, angle, float(1 / (2 * np.pi)), shift, ALU.mult, ALU.add))
                link(v.tensor_scalar(turn_a, turn_a, MAGIC, None, ALU.add))
                link(v.tensor_scalar(turn_a, turn_a, MAGIC, None, ALU.subtract))
                link(v.scalar_tensor_tensor(out_t, turn_a, -TWO_PI_HI, angle, ALU.mult, ALU.add))
                link(v.scalar_tensor_tensor(out_t, turn_a, -TWO_PI_LO, out_t, ALU.mult, ALU.add))
                if part:
                    link(v.tensor_scalar(out_t, out_t, float(np.pi / 2), None, ALU.add))
                v.tensor_scalar(out_t, out_t, -PI, PI, ALU.max, ALU.min).then_inc(S["angles_ready"], 1)

            dve.wait_ge(S["weights_in"], 16 * 8)
            for c in range(2):
                for h in range(GSZ):
                    v.tensor_copy(wo_p[:, c, h, :].rearrange("p (g d) -> p g d", g=G),
                                  wo_n[:, c, :].rearrange("p (g h d) -> p g h d", g=G, h=GSZ)[:, :, h, :]).then_inc(S["wo_sorted"], 1)
            for n, (_, dst, kind) in enumerate(wtr):
                dve.wait_ge(S["wtr_done"], n + 1)
                src = bank[n % 4][:, 0:P]
                if kind == "q":
                    v.tensor_copy(dst, src.rearrange("p (g h d) -> p g h d", g=2, h=2)).then_inc(S["wtr_moved"], 1)
                elif kind == "i":
                    v.tensor_tensor(dst, src, ident[:, :], op=ALU.add).then_inc(S["wtr_moved"], 1)
                else:
                    v.tensor_copy(dst, src).then_inc(S["wtr_moved"], 1)
            dve.wait_ge(S["const_in"], 16 * (NAD + 3))
            link(v.tensor_scalar(gain[:, :, :], gain[:, :, :], 1.0, None, ALU.add))
            dve.wait_ge(S["act_pre"], 4)
            for n, out_t in enumerate((q_tables, tables)):
                gain_b = lambda o: gain[:, n, None, o:o + 16].broadcast_to([P, TILES, 16])
                for half in range(2):
                    o, m = 16 * half, 16 - 16 * half
                    for part, at in ((0, o), (1, m)):
                        link(v.tensor_tensor(out_t[:, part, :, o:o + 16], tables[:, part, :, o:o + 16], gain_b(at), op=ALU.mult))
            link(v.tensor_scalar(idx_cols[:, 3:4], kv_col[:, 1:2], 4, None, ALU.logical_shift_right))
            link(v.tensor_copy(cols[:, 2:3], idx_cols[:, 3:4]))
            link(v.tensor_scalar(adapt[:, :], n_idx_bc[:, :], cols[:, 2:3], cols[:, 0:1], ALU.is_equal, ALU.mult))

            link(v.tensor_scalar(kv_bc_i[:, 1, :], kv_bc_i[:, 0, :], -(WINDOW - 1.0), 0.0, ALU.add, ALU.max))
            link(v.tensor_scalar(kv_bc_i[:, 1, :], kv_bc_i[:, 1, :], 4, 4, ALU.logical_shift_right, ALU.logical_shift_left))
            link(v.tensor_tensor(tmp_bc, kv_bc_i[:, 1, :], kv_bc_i[:, 0, :], op=ALU.subtract))
            link(v.tensor_scalar(mask_at[:, :], tmp_bc[0:1, :], float(OFFS), None, ALU.add))
            link(v.tensor_scalar(kv_bc_i[:, 1, :], kv_bc_i[:, 0, :], BLK - 1, None, ALU.bitwise_and))
            link(v.tensor_copy(m_bc, kv_bc_i[:, 1, :]))
            link(v.tensor_tensor(value_bc.rearrange("p (b j) -> p b j", j=WS), value_bc.rearrange("p (b j) -> p b j", j=WS),
                                 m_bc[:, :, None].broadcast_to([P, B, WS]), op=ALU.subtract))
            dve.wait_ge(S["wtr_done"], NWT + 1)
            link(v.tensor_copy(b3_all[:, :], bank[6][:, 0:TILES]))
            dve.wait_ge(S["act_pre"], 4)
            dve.wait_ge(S["keys_back"], 16)
            for j in range(WS):
                link(v.scalar_tensor_tensor(match[:, j, :], wkey_bc, wblk[:, j:j + 1], value_bc, ALU.is_equal, ALU.mult))
            link(v.memset(cover[:, :, 1], 1.0))

            def owners_cover(o, first):
                if not first:
                    dve.wait_ge(S["own_step"], 6 * o)
                v.tensor_scalar(cover[:, :, 0], m_bc, off_io[:, bass.ds(o, 1)], None, ALU.is_le).then_inc(S["own_step"], 1)
                v.tensor_scalar(cover[:, :, 2], m_bc, off_io[:, bass.ds(o, 1)], None, ALU.is_gt).then_inc(S["own_step"], 1)

            def owners_max(o, j):
                if j == 0:
                    dve.wait_ge(S["own_step"], 6 * o + 2)
                    hold(dve)
                v.tensor_tensor_reduce(out=owner_o[:, j, :], in0=match[:, j, :], in1=cover.rearrange("p b j -> p (b j)"),
                                       scale=1.0, scalar=0.0, op0=ALU.mult, op1=ALU.max, accum_out=own_now[:, j:j + 1]
                                       ).then_inc(S["own_step"], 1)

            def owners_keep(o):
                dve.wait_ge(S["own_step"], 6 * o + 5)
                hold(dve)
                v.tensor_copy(own_max.rearrange("p (j o) -> p j o", j=WS)[:, :, bass.ds(o, 1)], own_now[:, :, None]
                              ).then_inc(S["own_step"], 1)

            def by_head(t, heads):
                return t[:, 0:2 * heads * HD].rearrange("p (i h d) -> p i h d", i=2, d=HD)

            def scale_heads(ps, heads, rs, chain):
                v.tensor_tensor(by_head(nrm, heads), ps,
                                rs.rearrange("p (i h) -> p i h", i=2)[:, :, :, None].broadcast_to([P, 2, heads, HD]),
                                op=ALU.mult).then_inc(S[chain], 1)

            def rotate_heads(heads, table, at, chain):
                v.tensor_tensor(by_head(rot_c, heads), by_head(nrm, heads),
                                table[:, 0, at, :][:, :, None, :].broadcast_to([P, 2, heads, HD]), op=ALU.mult).then_inc(S[chain], 1)
                for half in range(2):
                    o, m = half * 16, 16 - half * 16
                    v.tensor_tensor(by_head(rot_s, heads)[:, :, :, o:o + 16], by_head(nrm, heads)[:, :, :, m:m + 16],
                                    table[:, 1, at, o:o + 16][:, :, None, :].broadcast_to([P, 2, heads, 16]), op=ALU.mult
                                    ).then_inc(S[chain], 1)

            def a1(r, s4, on):
                s = s4 % 2
                own = on(0, BLK)
                if own:
                    owners_cover(r, not on(1))
                if on(1, PAIRS + 1):
                    dve.wait_ge(S["sq_done"], r)
                    v.reduce_sum(ssum[1 - s][:, 0:2 * G], sq[1 - s][:, 0:2 * KV].rearrange("p (h d) -> p h d", d=HD), axis=AX.X
                                 ).then_inc(S["ms_done"], 1)
                if on(2, PAIRS + 2):
                    base = 5 * (r - 2)
                    dve.wait_ge(S["sqrt_done"], r - 1)
                    if on(3):
                        dve.wait_ge(S["rows_ready"], r - 2)
                    v.reciprocal(rstd[s][:, 0:2 * G], rtmp[s][:, 0:2 * G]).then_inc(S["dve_a"], 1)
                if own:
                    owners_max(r, 0)
                if on(2, PAIRS + 2):
                    dve.wait_ge(S["dve_a"], base + 1)
                    hold(dve)
                    ps = bank[2 + (s4 - 2) % 4][:, :].rearrange("p (i h d) -> p i h d", i=2, d=HD)
                    scale_heads(ps[:, :, 0:G, :], G, rstd[s][:, 0:2 * G], "dve_a")
                if own:
                    owners_max(r, 1)
                if on(2, PAIRS + 2):
                    dve.wait_ge(S["dve_a"], base + 2)
                    rotate_heads(G, tables, bass.ds((r - 2) * 2, 2), "dve_a")
                if own:
                    owners_max(r, 2)
                if on(2, PAIRS + 2):
                    dve.wait_ge(S["dve_a"], base + 5)
                    if on(4):
                        dve.wait_ge(S[f"rows_out{s}"], 8 * (r - 2 - s))
                    v.tensor_tensor(kv_o[s][:, :, 0:KV], rot_c[:, 0:2 * KV].rearrange("p (i n) -> p i n", i=2),
                                    rot_s[:, 0:2 * KV].rearrange("p (i n) -> p i n", i=2), op=ALU.add).then_inc(S["rows_ready"], 1)
                if own:
                    owners_keep(r)

            rounds(dve, a1, FIRST1, PAIRS + 2)
            dve.wait_ge(S["own_step"], 6 * BLK)
            link(v.tensor_scalar(own_any[:, :], own_max, 0.5, None, ALU.is_gt))
            link(v.tensor_tensor(own_f, own_max, off_io, op=ALU.add))
            v.tensor_scalar(own_idx[:, :], own_f, -64.0, 0.0, ALU.add, ALU.max).then_inc(S["own_known"], 1)
            for r in range(RSP):
                link(v.tensor_tensor_reduce(out=scrap[:, 0:NBLK], in0=table[:, r:r + NBLK], in1=hot_r, scale=1.0, scalar=0.0,
                                            op0=ALU.mult, op1=ALU.add, accum_out=read_blk[:, r:r + 1]))

            def match_step(r, part):
                if isinstance(r, int) and 6 * r + part < 2 * RSP:
                    n, reduce = divmod(6 * r + part, 2)
                    if n or reduce:
                        dve.wait_ge(S["reader_step"], 2 * n + reduce)
                    if reduce:
                        v.tensor_reduce(read_w[:, n:n + 1], scrap, axis=AX.X, op=ALU.max).then_inc(S["reader_step"], 1)
                    else:
                        v.scalar_tensor_tensor(scrap, wkey_bc, read_blk[:, n:n + 1], order_bc, ALU.is_equal, ALU.mult
                                               ).then_inc(S["reader_step"], 1)

            def a2(r, s4, on):
                s = s4 % 2
                if isinstance(r, int) and r == SLOTS_AT:
                    merged_slots()
                if isinstance(r, int) and r == MERGE0:
                    merge(0)
                if isinstance(r, int) and r == MERGE1:
                    merge(1)
                if on(1, PAIRS + 1):
                    dve.wait_ge(S["qsq_done"], r)
                    v.reduce_sum(ssum[1 - s][:, 0:2 * H], sq[1 - s].rearrange("p (h d) -> p h d", d=HD), axis=AX.X
                                 ).then_inc(S["qms_done"], 1)
                if on(2, PAIRS + 2):
                    base = 5 * (r - 2)
                    dve.wait_ge(S["qsqrt_done"], r - 1)
                    if on(3):
                        dve.wait_ge(S["q_ready"], r - 2)
                    else:
                        dve.wait_ge(S["rows_ready"], PAIRS)
                    v.reciprocal(rstd[s], rtmp[s]).then_inc(S["dve_q"], 1)
                match_step(r, 0)
                if on(2, PAIRS + 2):
                    dve.wait_ge(S["dve_q"], base + 1)
                    ps = bank[2 + (s4 - 2) % 4][:, :].rearrange("p (i h d) -> p i h d", i=2, d=HD)
                    scale_heads(ps, H, rstd[s], "dve_q")
                match_step(r, 1)
                if on(2, PAIRS + 2):
                    dve.wait_ge(S["dve_q"], base + 2)
                    rotate_heads(H, q_tables, bass.ds((r - 2) * 2, 2), "dve_q")
                for part in range(2, 6):
                    match_step(r, part)
                if on(2, PAIRS + 2):
                    dve.wait_ge(S["dve_q"], base + 5)
                    if on(4):
                        dve.wait_ge(S["qtr_done"], r - 3)
                    elif on(2, 3):
                        for n in range(2):
                            dve.wait_ge(S[f"rows_out{n}"], 16 * (PAIRS // 2))
                    v.tensor_tensor(q_o[s].rearrange("p i n -> p (i n)"), rot_c, rot_s, op=ALU.add).then_inc(S["q_ready"], 1)

            def merged_slots():
                dve.wait_ge(S["reader_step"], 2 * RSP)
                link(v.tensor_scalar(r_hit, read_w, 0.5, None, ALU.is_gt))
                link(v.scalar_tensor_tensor(r_a, r_hit, float(BIG), read_blk, ALU.mult, ALU.add))
                link(v.tensor_scalar(r_hit, read_w, 0.5, float(BIG), ALU.is_lt, ALU.mult))
                link(v.scalar_tensor_tensor(r_b, read_w, -1.0, r_hit, ALU.add, ALU.add))
                for n, t in enumerate((r_a, r_b)):
                    link(v.tensor_copy(r_int[:, RSP * n:RSP * n + RSP].rearrange("p (q u) -> p q u", u=3),
                                       t.rearrange("p (u q) -> p q u", u=3)))
                    for g in range(G):
                        link(v.tensor_scalar(r_int[:, 24 + 48 * n + RSP * g:24 + 48 * n + RSP * g + RSP], t, float(G), float(g),
                                             ALU.mult, ALU.add))
                v.engine_nop().then_inc(S["dve_tab"], 1)

            def merge(j):
                if j == 0:
                    dve.wait_ge(S["blk_in"], 16 * 6)
                dve.wait_ge(S[f"rows_in{j}"], 16 * BLK)
                for kv, blk in enumerate((blk_k, blk_v)):
                    out = blk[:, j, :].rearrange("p (g o d) -> p g o d", g=G, o=BLK)
                    data = row_new[:, j * BLK:(j + 1) * BLK, kv * KV:(kv + 1) * KV].rearrange("p o (g d) -> p g o d", g=G)
                    for g in range(G):
                        link(v.copy_predicated(out[:, g], own_any[:, j * BLK:(j + 1) * BLK, None].broadcast_to([P, BLK, HD]), data[:, g]))
                v.engine_nop().then_inc(S["merged_done"], 1)
            rounds(dve, a2, FIRST2, PAIRS + 2, lambda: merge(2))

            def finish(w, piece, first):
                unit, half, batch0, turn = w
                r0 = UROWS * half
                what, q = piece
                if what == "y":
                    dve.wait_ge(S[f"x1_unit{half}"], 16 * turn)
                    dve.wait_ge(S["y_done"], 2 * unit + q + 1)
                    v.tensor_tensor(xT_ph[:, q, r0:r0 + UROWS], bank[5 + q][:, :], xT_ph[:, q, r0:r0 + UROWS],
                                    op=ALU.add).then_inc(S["y_moved"], 1)
                elif what == "lo":
                    dve.wait_ge(S["lo_done"], unit + 1)
                    if not first:
                        dve.wait_ge(S["x3_done"], 4 * unit)
                    v.tensor_tensor(low[:, :].rearrange("p (b t) -> p b t", t=T),
                                    bank[5][:, :].rearrange("p (b t) -> p b t", t=T),
                                    adapt[:, bass.ds(batch0, 16)][:, :, None].broadcast_to([P, 16, T]),
                                    op=ALU.mult).then_inc(S["lo_moved"], 1)

            def sort_keys(ph, u, later):
                if u == 0:
                    dve.wait_ge(S["merged_in"], 16 * (3 + RS) * (ph + 1))
                if u < 2 and later:
                    dve.wait_ge(S["ktr_done"], 12 * ph)
                if u == 2:
                    dve.wait_ge(S["ktr_done"], 12 * ph + 4)
                v.tensor_copy(k_perm[u % 2][0].rearrange("p o (g d) -> p o g d", g=G),
                     k_raw[:, u, :, 0:8, :].rearrange("p g o d -> p o g d")).then_inc(S["k_sorted1"], 1)

            def move_keys(ph, u, later):
                if u == 0 and later:
                    dve.wait_ge(S["s_done"], ph * PB)
                q = 4 if u < 2 else 3
                for o4 in (1, 3):
                    n = 4 * u + o4
                    dve.wait_ge(S["ktr_done"], 12 * ph + n + 1)
                    v.tensor_copy(
                        kT[:, :, u * 64:u * 64 + 16 * q].rearrange("p b (r o) -> p b r o", o=BLK)[:, :, :, 4 * o4:4 * o4 + 4],
                        bank[n % 2][:, :].rearrange("p (o b r) -> p b r o", o=4, r=4)[:, :, 0:q, :]).then_inc(S["ktr_moved1"], 1)

            def expand(ph, q4):
                if q4 % 4 == 0:
                    dve.wait_ge(S[f"q_in{q4 // 4}"], 16 * (ph + 1))
                if q4 >= 2:
                    dve.wait_ge(S["s_done"], ph * PB + BPT * (q4 - 1))
                for g in range(G):
                    last = v.tensor_scalar(
                        q_bd[q4 % 2][:, :, g, :].rearrange("p b (h t) -> p b h t", h=GSZ),
                        qT_ph[:, :, P * q4:P * q4 + P].rearrange("p h (b t) -> p b h t", b=BPT),
                        head_scale[:, g:g + 1], None, ALU.mult)
                last.then_inc(S["qbd_ready"], 1)

            def phase(ph, later, more):
                for step in range(STEPS + 1):
                    b = step
                    if b < PB:
                        if b % BPT == 1 and b // BPT + 1 < PB // BPT:
                            expand(ph, b // BPT + 1)
                        dve.wait_ge(S["s_done"], ph * PB + b + 1)
                        dve.wait_ge(S["mask_ready"], ph * PB + b + 1)
                        if b >= 3:
                            dve.wait_ge(S["exp_done"], 2 * (ph * PB + b - 2))
                        elif later:
                            dve.wait_ge(S["exp_done"], 2 * (ph * PB))
                        hold(dve)
                        for j in range(2):
                            v.tensor_tensor_reduce(out=shifted[b % 3][:, j, :], in0=bank[b % 2][:, 256 * j:256 * j + KEYS],
                                                   in1=masks[b % 8], scale=-1.0, scalar=3.0e38, op0=ALU.add, op1=ALU.min,
                                                   accum_out=neg_max[:, 2 * b + j:2 * b + j + 1]).then_inc(S["shifted_done"], 1)
                    if step < len(VTR):
                        for n in range(sum(VTR[:step]), sum(VTR[:step + 1])):
                            if n % 2:
                                c, d4 = n // 8, n % 8
                                dve.wait_ge(S["vtr_done"], 16 * ph + n + 1)
                                if later and n == 1:
                                    dve.wait_ge(S["av_done"], ph * PB)
                                v.tensor_copy(vK[0:KC, c, 4 * d4:4 * d4 + 4, :].rearrange("p d n -> p (d n)"), bank[2 + n % 3][0:KC, :]
                                              ).then_inc(S["vtr_moved1"], 1)
                    b = step - 1
                    if 0 <= b < PB:
                        dve.wait_ge(S["exp_done"], 2 * (ph * PB + b + 1))
                        v.reciprocal(p_inv[:, 2 * b:2 * b + 2], p_sum[:, 2 * b:2 * b + 2]).then_inc(S["inv_done"], 1)
                        dve.wait_ge(S["inv_done"], ph * PB + b + 1)
                        if b >= PR:
                            dve.wait_ge(S["pt_done"], ph * PB + b - PR + 1)
                        elif later:
                            dve.wait_ge(S["pt_done"], ph * PB)
                        for j in range(2):
                            v.tensor_scalar(normed[b % PR][:, j, :], probs[b % PR][:, j, :], p_inv[:, 2 * b + j:2 * b + j + 1], 1.0,
                                            ALU.mult, ALU.mult).then_inc(S["norm_done"], 1)
                    b = step - LAG - 1
                    if b >= 0 and b % 8 == 7:
                        i8 = b // 8
                        dve.wait_ge(S["av_done"], ph * PB + b + 1)
                        if later:
                            dve.wait_ge(S["y_done"], 4 * ph - 2 + 2 * (i8 // 2))
                        v.tensor_copy(oT_ph[:, :, 256 * i8:256 * i8 + 256].rearrange("p h (b t) -> p b h t", b=8),
                                      bank[4][:, :].rearrange("p (b h t) -> p b h t", b=8, h=GSZ)).then_inc(S["o_moved"], 1)
                    if later and step - 1 in PIECES:
                        finish((2 * ph - 1, 1, ph * PB - 16, ph), PIECES[step - 1], False)
                    if step - 1 - UNIT_AT in PIECES:
                        finish((2 * ph, 0, ph * PB, ph + 1), PIECES[step - 1 - UNIT_AT], not later)
                    if more and 0 <= step - PB + 1 < 3:
                        sort_keys(ph + 1, step - PB + 1, True)
                    if more and step == PB:
                        expand(ph + 1, 0)
                    if more and 0 <= step - PB < 3:
                        move_keys(ph + 1, step - PB, True)
            sort_keys(0, 0, False)
            sort_keys(0, 1, False)
            move_keys(0, 0, False)
            sort_keys(0, 2, False)
            move_keys(0, 1, False)
            move_keys(0, 2, False)
            expand(0, 0)
            phases(dve, phase)
            for step in sorted(PIECES):
                finish((2 * PH - 1, 1, B - 16, PH), PIECES[step], False)

        @block.scalar
        def _(act):
            s_ = nc.scalar
            act.wait_ge(S["angles_ready"], 2)
            s_.activation(tables[:, 1, :, 0:16], turn_b, ACT.Sin, scale=-1.0).then_inc(S["act_pre"], 1)
            s_.activation(tables[:, 1, :, 16:32], turn_b, ACT.Sin).then_inc(S["act_pre"], 1)
            for half in range(2):
                s_.activation(tables[:, 0, :, 16 * half:16 * half + 16], turn_c, ACT.Sin).then_inc(S["act_pre"], 1)
            def a1(r, s4, on):
                s = s4 % 2
                if on(2, PAIRS + 2):
                    ps = bank[2 + (s4 - 2) % 4][:, :].rearrange("p (i n) -> p i n", i=2)
                    if on(4):
                        act.wait_ge(S[f"rows_out{s}"], 8 * (r - 2 - s))
                    s_.activation(kv_o[s][:, :, KV:2 * KV], ps[:, :, KV:2 * KV], ACT.Copy).then_inc(S["v_copied"], 1)
                    act.wait_ge(S["ms_done"], r - 1)
                    if on(4):
                        act.wait_ge(S["dve_a"], 5 * (r - 4) + 1)
                    s_.activation(rtmp[s][:, 0:2 * G], ssum[s][:, 0:2 * G], ACT.Sqrt, scale=1.0 / HD, bias=eps_t[:, 0:1]
                                  ).then_inc(S["sqrt_done"], 1)
                if on(0, PAIRS):
                    act.wait_ge(S["l0_done"], r + 1)
                    if on(2):
                        act.wait_ge(S["kv_done"], r - 1)
                        act.wait_ge(S[f"x1_out{s}"], 8 * (r - s))
                    s_.activation(x1t[s].rearrange("p c r -> p (c r)"), bank[s][:, :], ACT.Copy).then_inc(S["x1_ready"], 1)
                if on(1, PAIRS + 1):
                    act.wait_ge(S["kv_done"], r)
                    if on(3):
                        act.wait_ge(S["ms_done"], r - 2)
                    ps = bank[2 + (s4 - 1) % 4][:, :].rearrange("p (i n) -> p i n", i=2)
                    s_.activation(sq[1 - s][:, 0:2 * KV].rearrange("p (i n) -> p i n", i=2), ps[:, :, 0:KV], ACT.Square
                                  ).then_inc(S["sq_done"], 1)
            rounds(act, a1, FIRST1, PAIRS + 2)
            def store_merged(j):
                act.wait_ge(S["merged_done"], j + 1)
                for dst, blk in ((merged_k, blk_k), (merged_v, blk_v)):
                    act.dma_start(dst.rearrange("(b j) e -> j b e", j=WS)[j], blk[:, j, :]).then_inc(S["merged_out"], 16)

            def slots_out():
                act.wait_ge(S["dve_tab"], 2)
                for n in range(2):
                    act.dma_start(k_slots[n].rearrange("(b e) -> b e", e=RSP), r_int[:, RSP * n:RSP * n + RSP]).then_inc(S["slots_out"], 16)
                    act.dma_start(v_slots[n].rearrange("(b e) -> b e", e=G * RSP),
                                 r_int[:, 24 + 48 * n:24 + 48 * n + 48]).then_inc(S["slots_out"], 16)

            def slots_back():
                act.wait_ge(S["slots_out"], 64)
                for n in range(2):
                    act.dma_start(slot_idx[:, :, 3 * n:3 * n + 3],
                                 k_slots[n].rearrange("(h p u) -> p h u", p=P, u=3)).then_inc(S["slots_back"], 16)
                    act.dma_start(slot_idx[:, :, 6 + RSP * n:6 + RSP * n + RSP],
                                 v_slots[n].rearrange("(h p r) -> p h r", p=P, r=RSP)).then_inc(S["slots_back"], 16)

            def a2(r, s4, on):
                s = s4 % 2
                if isinstance(r, int) and r == MERGE0 + 1:
                    store_merged(0)
                if isinstance(r, int) and r == SLOTS_AT + 1:
                    slots_out()
                if isinstance(r, int) and r == SLOTS_AT + 2:
                    slots_back()
                if isinstance(r, int) and r == MERGE1:
                    store_merged(1)
                if on(2, PAIRS + 2):
                    act.wait_ge(S["qms_done"], r - 1)
                    if on(4):
                        act.wait_ge(S["dve_q"], 5 * (r - 4) + 1)
                    else:
                        act.wait_ge(S["dve_a"], 5 * PAIRS)
                    s_.activation(rtmp[s], ssum[s], ACT.Sqrt, scale=1.0 / HD, bias=eps_t[:, 0:1]).then_inc(S["qsqrt_done"], 1)
                if on(0, PAIRS):
                    act.wait_ge(S["q_done"], r + 1)
                    if on(2):
                        act.wait_ge(S["qms_done"], r - 1)
                    else:
                        act.wait_ge(S["ms_done"], PAIRS)
                    s_.activation(sq[s], bank[2 + s4][:, :], ACT.Square).then_inc(S["qsq_done"], 1)
                if on(2, PAIRS + 2):
                    act.wait_ge(S["qtr_done"], r - 1)
                    here = (s4 - 2) % 4
                    if on(6):
                        act.wait_ge(S[f"qt_out{here}"], 4 * (r - 2 - here))
                    s_.activation(qt[here].rearrange("p h r -> p (h r)"), bank[6 + s][:, :], ACT.Copy).then_inc(S["qt_ready"], 1)
            rounds(act, a2, FIRST2, PAIRS + 2, lambda: store_merged(2))

            def finish(w, piece, first):
                unit, q0 = w
                what, q = piece
                if what == "x3":
                    act.wait_ge(S["x3_done"], 4 * unit + q + 1)
                    if q > 1 or not first:
                        act.wait_ge(S["l3_done"], 4 * unit + q - 1)
                    s_.activation(x3[q % 2], bank[6][:, 0:D], ACT.Copy).then_inc(S["x3_moved"], 1)
                elif what == "l3":
                    act.wait_ge(S["l3_done"], 4 * unit + q + 1)
                    if q > 1 or not first:
                        act.wait_ge(S[f"out_done{q % 2}"], 32 * unit + 16 * (q // 2))
                    s_.activation(o_t[q % 2], bank[7][:, 0:D], ACT.Identity, bias=b3_all[:, bass.ds(q0 + q, 1)]
                                  ).then_inc(S["l3_moved"], 1)

            def sort_keys(ph, u, later):
                if u == 0:
                    act.wait_ge(S["merged_in"], 16 * (3 + RS) * (ph + 1))
                if u < 2 and later:
                    act.wait_ge(S["ktr_done"], 12 * ph)
                if u == 2:
                    act.wait_ge(S["ktr_done"], 12 * ph + 4)
                s_.activation(k_perm[u % 2][1].rearrange("p o (g d) -> p o g d", g=G),
                     k_raw[:, u, :, 8:16, :].rearrange("p g o d -> p o g d"), ACT.Copy).then_inc(S["k_sorted0"], 1)

            def move_keys(ph, u, later):
                if u == 0 and later:
                    act.wait_ge(S["s_done"], ph * PB)
                q = 4 if u < 2 else 3
                for o4 in (0, 2):
                    n = 4 * u + o4
                    act.wait_ge(S["ktr_done"], 12 * ph + n + 1)
                    s_.activation(
                        kT[:, :, u * 64:u * 64 + 16 * q].rearrange("p b (r o) -> p b r o", o=BLK)[:, :, :, 4 * o4:4 * o4 + 4],
                        bank[n % 2][:, :].rearrange("p (o b r) -> p b r o", o=4, r=4)[:, :, 0:q, :], ACT.Copy).then_inc(S["ktr_moved0"], 1)

            def phase(ph, later, more):
                for step in range(STEPS + 1):
                    if later and step - 1 in PIECES:
                        finish((2 * ph - 1, 8 * ph - 4), PIECES[step - 1], False)
                    if step - 1 - UNIT_AT in PIECES:
                        finish((2 * ph, 8 * ph), PIECES[step - 1 - UNIT_AT], not later)
                    if step < len(VTR):
                        for n in range(sum(VTR[:step]), sum(VTR[:step + 1])):
                            if n % 2 == 0:
                                c, d4 = n // 8, n % 8
                                act.wait_ge(S["vtr_done"], 16 * ph + n + 1)
                                if later and n == 0:
                                    act.wait_ge(S["av_done"], ph * PB)
                                s_.activation(vK[0:KC, c, 4 * d4:4 * d4 + 4, :].rearrange("p d n -> p (d n)"), bank[2 + n % 3][0:KC, :],
                                              ACT.Copy).then_inc(S["vtr_moved0"], 1)
                    b = step
                    if b < PB:
                        if b >= PR:
                            act.wait_ge(S["norm_done"], 2 * (ph * PB + b - PR + 1))
                        for j in range(2):
                            act.wait_ge(S["shifted_done"], 2 * (ph * PB + b) + j + 1)
                            s_.activation(probs[b % PR][:, j, :], shifted[b % 3][:, j, :], ACT.Exp, scale=-1.0,
                                          bias=neg_max[:, 2 * b + j:2 * b + j + 1],
                                          accum_out=p_sum[:, 2 * b + j:2 * b + j + 1]).then_inc(S["exp_done"], 1)
                    b = step - LAG
                    if 0 <= b < PB:
                        act.wait_ge(S["pt_done"], ph * PB + b + 1)
                        if b >= 2:
                            act.wait_ge(S["av_done"], ph * PB + b - 1)
                        elif later:
                            act.wait_ge(S["av_done"], ph * PB)
                        s_.activation(pT[b % 2][0:KC, :], bank[2 + b % 2][0:KC, :], ACT.Copy).then_inc(S["pt_moved"], 1)
                    if more and 0 <= step - PB + 1 < 3:
                        sort_keys(ph + 1, step - PB + 1, True)
                    if more and 0 <= step - PB < 3:
                        move_keys(ph + 1, step - PB, True)
            sort_keys(0, 0, False)
            sort_keys(0, 1, False)
            move_keys(0, 0, False)
            sort_keys(0, 2, False)
            move_keys(0, 1, False)
            move_keys(0, 2, False)
            phases(act, phase)
            for step in sorted(PIECES):
                finish((2 * PH - 1, TILES - 4), PIECES[step], False)


_INS = ["x", "itok_B_1_198", "itok_Bx257_0_4111", "itok_B_37_3939", "itok_B_0_6", "itok_B_0_7", "fside_8xS_0",
        "L0_cond_weights", "L1_cond_Wq", "L1_cond_Wk", "L1_cond_Wv", "L1_cond_Wo", "L1_cond_q_norm_scale",
        "L1_cond_k_norm_scale", "L1_cond_k_blocks", "L1_cond_v_blocks", "L2_cond_W", "L2_cond_A", "L2_cond_Bm",
        "L2_cond_scalings", "L3_cond_weights"]


def kernel(**inputs):
    import numpy as _np
    import concourse.bacc as _bacc
    from concourse import mybir as _mybir
    from concourse.bass_utils import run_bass_kernel_spmd as _run

    nc = _bacc.Bacc("TRN2", target_bir_lowering=False, num_devices=1)
    arrays, aps = {}, {}
    for name in _INS:
        arr = _np.ascontiguousarray(inputs[name])
        arrays[f"in_{name}"] = arr
        aps[name] = nc.dram_tensor(f"in_{name}", arr.shape, _mybir.dt.from_np(arr.dtype), kind="ExternalInput").ap()
    aps["out"] = nc.dram_tensor("out", (B, T, D), _mybir.dt.float32, kind="ExternalOutput").ap()
    build(nc, aps)
    r = _run(nc, [arrays], core_ids=[0])
    return r.results[0]["out"]
```
